# Optimizing a Trainium2 kernel written in Bass

```python
import numpy as np
import jax
import jax.numpy as jnp

def _softmax(x, axis=-1):
    return jax.nn.softmax(x, axis=axis)

def _gelu(x):
    return jax.nn.gelu(x, approximate=True)

def _silu(x):
    return jax.nn.silu(x)

def _sigmoid(x):
    return jax.nn.sigmoid(x)

def _layernorm(x, axis=-1, eps=1e-05):
    m = jnp.mean(x, axis=axis, keepdims=True)
    v = jnp.var(x, axis=axis, keepdims=True)
    return (x - m) / jnp.sqrt(v + eps)

def _scatter_add(tgt, idx, src, axis=0):
    return tgt.at[idx].add(src)

def _segment_sum(src, seg, n):
    return jax.ops.segment_sum(src, seg, n)
kernel_name = 'mk_seq_preln_d2_jaxref_r8_4d83df'

def setup_inputs(seed: int=0):
    np.random.seed(seed)
    _w = jnp.asarray

    def _L0_attn_setup():
        import jax, jax.numpy as jnp
        import numpy as np
        B, S, D = (4, 512, 128)

        def log_g(x):
            return jnp.where(x >= 0, jnp.log(jnp.maximum(x, 0.0) + 0.5), -jax.nn.softplus(-x))

        def heinsen_scan_log(log_coeffs, log_values):
            a_star = jnp.cumsum(log_coeffs, axis=1)
            log_h0_plus_b_star = jax.lax.cumlogsumexp(log_values - a_star, axis=1)
            return jnp.exp(a_star + log_h0_plus_b_star)
        key = jax.random.key(seed)
        kx, kw = jax.random.split(key)
        x = jax.random.normal(kx, (B, S, D), dtype=jnp.float32)
        W = jax.random.normal(kw, (D, 2 * D), dtype=jnp.float32) * (1.0 / np.sqrt(D))
        return {'x': x, 'W': W}
    _L0_attn_in = _L0_attn_setup()

    def _L0_ffn_setup():
        import jax, jax.numpy as jnp
        import numpy as np
        B, S, D, F, E = (4, 256, 128, 512, 8)
        LN_EPS = 1e-05
        key = jax.random.key(seed)
        ks = jax.random.split(key, 6)
        sc = 0.02
        return {'x': jax.random.normal(ks[0], (B, S, D), dtype=jnp.float32), 'Wr': jax.random.normal(ks[1], (D, E), dtype=jnp.float32) * sc, 'br': jnp.zeros((E,), jnp.float32), 'ln_g': jnp.ones((D,), jnp.float32), 'ln_b': jnp.zeros((D,), jnp.float32), 'W1': jax.random.normal(ks[2], (E, D, F), dtype=jnp.float32) * sc, 'b1': jnp.zeros((E, F), jnp.float32), 'W2': jax.random.normal(ks[3], (E, F, D), dtype=jnp.float32) * sc, 'b2': jnp.zeros((E, D), jnp.float32)}
    _L0_ffn_in = _L0_ffn_setup()

    def _L1_attn_setup():
        import jax, jax.numpy as jnp
        import numpy as np
        D_MODEL = 128
        HEADS = 16
        SCALE = float(np.sqrt(D_MODEL / HEADS))
        key = jax.random.key(seed)
        ks = jax.random.split(key, 5)
        B, S, D = (4, 256, D_MODEL)
        q = jax.random.normal(ks[0], (B, S, D), dtype=jnp.float32)
        init = 0.02
        wq = jax.random.normal(ks[1], (D, D), dtype=jnp.float32) * init
        wk = jax.random.normal(ks[2], (D, D), dtype=jnp.float32) * init
        wv = jax.random.normal(ks[3], (D, D), dtype=jnp.float32) * init
        wo = jax.random.normal(ks[4], (D, D), dtype=jnp.float32) * init
        return {'q': q, 'wq': wq, 'wk': wk, 'wv': wv, 'wo': wo}
    _L1_attn_in = _L1_attn_setup()

    def _L1_ffn_setup():
        import jax, jax.numpy as jnp
        import numpy as np
        E = 16
        K = 4
        B, S, H, I = (4, 128, 128, 256)
        key = jax.random.key(seed)
        k0, k1, k2, k3 = jax.random.split(key, 4)
        scale = 0.02
        return {'hidden_states': jax.random.normal(k0, (B, S, H), jnp.float32), 'router_w': jax.random.normal(k1, (H, E), jnp.float32) * scale, 'router_b': jnp.zeros((E,), jnp.float32), 'w1': jax.random.normal(k2, (E, H, I), jnp.float32) * scale, 'b1': jnp.zeros((E, I), jnp.float32), 'w2': jax.random.normal(k3, (E, I, H), jnp.float32) * scale, 'b2': jnp.zeros((E, H), jnp.float32)}
    _L1_ffn_in = _L1_ffn_setup()
    _d = {'L0_attn_x': _L0_attn_in['x'], 'L0_attn_W': _L0_attn_in['W'], 'L0_ffn_Wr': _L0_ffn_in['Wr'], 'L0_ffn_br': _L0_ffn_in['br'], 'L0_ffn_ln_g': _L0_ffn_in['ln_g'], 'L0_ffn_ln_b': _L0_ffn_in['ln_b'], 'L0_ffn_W1': _L0_ffn_in['W1'], 'L0_ffn_b1': _L0_ffn_in['b1'], 'L0_ffn_W2': _L0_ffn_in['W2'], 'L0_ffn_b2': _L0_ffn_in['b2'], 'L1_attn_wq': _L1_attn_in['wq'], 'L1_attn_wk': _L1_attn_in['wk'], 'L1_attn_wv': _L1_attn_in['wv'], 'L1_attn_wo': _L1_attn_in['wo'], 'L1_ffn_router_w': _L1_ffn_in['router_w'], 'L1_ffn_router_b': _L1_ffn_in['router_b'], 'L1_ffn_w1': _L1_ffn_in['w1'], 'L1_ffn_b1': _L1_ffn_in['b1'], 'L1_ffn_w2': _L1_ffn_in['w2'], 'L1_ffn_b2': _L1_ffn_in['b2']}
    _x0 = _d['L0_attn_x']
    _d['L0_attn_x'] = jax.random.normal(jax.random.fold_in(jax.random.key(seed), 1), (4, 1024, 128), dtype=_x0.dtype)
    del _x0
    return _d

def reference(L0_attn_x, L0_attn_W, L0_ffn_Wr, L0_ffn_br, L0_ffn_ln_g, L0_ffn_ln_b, L0_ffn_W1, L0_ffn_b1, L0_ffn_W2, L0_ffn_b2, L1_attn_wq, L1_attn_wk, L1_attn_wv, L1_attn_wo, L1_ffn_router_w, L1_ffn_router_b, L1_ffn_w1, L1_ffn_b1, L1_ffn_w2, L1_ffn_b2):

    def _L0_attn_ref(x, W):
        import jax, jax.numpy as jnp
        import numpy as np
        B, S, D = (4, 512, 128)

        def log_g(x):
            return jnp.where(x >= 0, jnp.log(jnp.maximum(x, 0.0) + 0.5), -jax.nn.softplus(-x))

        def heinsen_scan_log(log_coeffs, log_values):
            a_star = jnp.cumsum(log_coeffs, axis=1)
            log_h0_plus_b_star = jax.lax.cumlogsumexp(log_values - a_star, axis=1)
            return jnp.exp(a_star + log_h0_plus_b_star)
        hg = jnp.einsum('bsd,de->bse', x, W)
        hidden, gate = jnp.split(hg, 2, axis=-1)
        log_coeffs = -jax.nn.softplus(gate)
        log_z = -jax.nn.softplus(-gate)
        log_values = log_z + log_g(hidden)
        out = heinsen_scan_log(log_coeffs, log_values)
        return out

    def _L0_ffn_ref(x, Wr, br, ln_g, ln_b, W1, b1, W2, b2):
        import jax, jax.numpy as jnp
        import numpy as np
        B, S, D, F, E = (4, 256, 128, 512, 8)
        LN_EPS = 1e-05
        tokens_shape = x.shape[:-1]
        xt = x.reshape(-1, x.shape[-1])
        router_logits = xt @ Wr + br
        router_probs = jax.nn.softmax(router_logits, axis=-1)
        gates = jnp.max(router_probs, axis=-1, keepdims=True)
        idx = jnp.argmax(router_probs, axis=-1)
        onehot = jax.nn.one_hot(idx, E, dtype=xt.dtype)
        mu = jnp.mean(xt, axis=-1, keepdims=True)
        var = jnp.mean(jnp.square(xt - mu), axis=-1, keepdims=True)
        xn = (xt - mu) * jax.lax.rsqrt(var + LN_EPS) * ln_g + ln_b
        h = jnp.einsum('te,td,edf->tf', onehot, xn, W1) + b1[idx]
        h = jax.nn.relu(h)
        y = jnp.einsum('te,tf,efd->td', onehot, h, W2) + b2[idx]
        y = y * gates
        return y.reshape(tokens_shape + (y.shape[-1],))

    def _L1_attn_ref(q, wq, wk, wv, wo):
        import jax, jax.numpy as jnp
        import numpy as np
        D_MODEL = 128
        HEADS = 16
        SCALE = float(np.sqrt(D_MODEL / HEADS))
        B, S, D = q.shape
        Q = jnp.einsum('bsd,ed->bse', q, wq)
        K = jnp.einsum('bsd,ed->bse', q, wk)
        V = jnp.einsum('bsd,ed->bse', q, wv)
        scores = jnp.einsum('bqe,bke->bqk', Q, K) / SCALE
        attn = jax.nn.softmax(scores, axis=-1)
        out = jnp.einsum('bqk,bke->bqe', attn, V)
        out = jnp.transpose(out, (0, 2, 1)).reshape(B, S, D)
        return jnp.einsum('bsd,ed->bse', out, wo)

    def _L1_ffn_ref(hidden_states, router_w, router_b, w1, b1, w2, b2):
        import jax, jax.numpy as jnp
        import numpy as np
        E = 16
        K = 4
        B, S, H, I = (4, 128, 128, 256)
        b, s, h = hidden_states.shape
        logits = hidden_states @ router_w + router_b
        probs = jax.nn.softmax(logits, axis=-1)
        topw, topi = jax.lax.top_k(probs, K)
        topw = topw / jnp.sum(topw, axis=-1, keepdims=True)
        combine = jnp.sum(jax.nn.one_hot(topi, E, dtype=hidden_states.dtype) * topw[..., None], axis=2)
        x = hidden_states.reshape(b * s, h)
        c = combine.reshape(b * s, E)

        def body(acc, expert):
            w1e, b1e, w2e, b2e, ce = expert
            hmid = jax.nn.gelu(x @ w1e + b1e, approximate=False)
            return (acc + (hmid @ w2e + b2e) * ce[:, None], None)
        out, _ = jax.lax.scan(body, jnp.zeros_like(x), (w1, b1, w2, b2, c.T))
        return out.reshape(b, s, h)
    x = L0_attn_x
    x = x + _L0_attn_ref(_layernorm(x, axis=-1), L0_attn_W)
    x = x + _L0_ffn_ref(_layernorm(x, axis=-1), L0_ffn_Wr, L0_ffn_br, L0_ffn_ln_g, L0_ffn_ln_b, L0_ffn_W1, L0_ffn_b1, L0_ffn_W2, L0_ffn_b2)
    x = x + _L1_attn_ref(_layernorm(x, axis=-1), L1_attn_wq, L1_attn_wk, L1_attn_wv, L1_attn_wo)
    x = x + _L1_ffn_ref(_layernorm(x, axis=-1), L1_ffn_router_w, L1_ffn_router_b, L1_ffn_w1, L1_ffn_b1, L1_ffn_w2, L1_ffn_b2)
    return x

_drawn_inputs = setup_inputs


def setup_inputs(seed=0):
    import zlib

    import numpy as np

    out = dict(_drawn_inputs(seed))
    spreads = {'L0_ffn_br': (0.0, 0.49),
     'L0_ffn_ln_g': (1.0, 0.6),
     'L0_ffn_ln_b': (0.0, 0.8),
     'L0_ffn_b1': (0.0, 0.8),
     'L0_ffn_b2': (0.0, 0.584),
     'L1_ffn_router_b': (0.0, 0.329),
     'L1_ffn_b1': (0.0, 0.8),
     'L1_ffn_b2': (0.0, 0.562)}
    factors = {'L0_ffn_Wr': 3.489,
     'L0_ffn_W1': 5.974,
     'L0_ffn_W2': 4.815,
     'L1_attn_wq': 8.0,
     'L1_attn_wk': 8.0,
     'L1_attn_wv': 8.0,
     'L1_attn_wo': 8.0,
     'L1_ffn_w1': 4.064,
     'L1_ffn_w2': 3.68}
    for name, (base, spread) in spreads.items():
        noise = np.random.default_rng([zlib.crc32(name.encode()), seed]).standard_normal(out[name].shape)
        drawn = base * np.exp(spread * noise) if base else spread * noise
        out[name] = jnp.asarray(drawn.astype(out[name].dtype))
    for name, factor in factors.items():
        out[name] = (out[name] * factor).astype(out[name].dtype)
    return out
```

```python
from contextlib import ExitStack

import concourse.bass as bass
from concourse import mybir

ALU = mybir.AluOpType
ACT = mybir.ActivationFunctionType
F32 = mybir.dt.float32
F16 = mybir.dt.float16
BF16 = mybir.dt.bfloat16
U32 = mybir.dt.uint32
AX_X = mybir.AxisListType.X
ds = bass.ds

P = 128
EPS = 1e-5
WS = 64.0
PBIAS = 6.931471805599453


def build(nc, L0_attn_x, L0_attn_W, L0_ffn_Wr, L0_ffn_br, L0_ffn_ln_g, L0_ffn_ln_b, L0_ffn_W1, L0_ffn_b1,
          L0_ffn_W2, L0_ffn_b2, L1_attn_wq, L1_attn_wk, L1_attn_wv, L1_attn_wo, L1_ffn_router_w,
          L1_ffn_router_b, L1_ffn_w1, L1_ffn_b1, L1_ffn_w2, L1_ffn_b2, out):
    B, S, D = L0_attn_x.shape
    NT = B * S // P
    TB = 4
    N = TB * P
    NB = NT // TB
    JT = S // P
    E0, _, F0 = L0_ffn_W1.shape
    E1, _, F1 = L1_ffn_w1.shape
    SCORE = 1.0 / float((D / 16) ** 0.5)
    assert D == P and NB == 2 * B and E0 * F0 == E1 * F1

    x2_dram = nc.dram_tensor("x2_scratch", (B, S, D), F32, kind="Internal").ap()

    with ExitStack() as ctx:
        def sb(name, shape, dt=F32):
            return ctx.enter_context(nc.sbuf_tensor(name, shape, dt))

        def sem(name):
            return ctx.enter_context(nc.semaphore(name))

        ps = ctx.enter_context(nc.psum_tensor("ps", [P, 8, N], F32))

        x = sb("x", [P, NT, D])
        xT_hi = sb("xT_hi", [P, NT * P], F16)
        xT_lo = sb("xT_lo", [P, NT * P], F16)
        ident = sb("ident", [P, P])
        ones_bf = sb("ones_bf", [P, P], BF16)
        iota_i = sb("iota_i", [P, E1], mybir.dt.int32)
        iota_e = sb("iota_e", [P, E1])
        W_raw = sb("W_raw", [P, 2 * D])
        W_hi = sb("W_hi", [P, 2 * D], F16)
        W_lo = sb("W_lo", [P, 2 * D], F16)
        Wr = [sb("Wr0", [P, E0]), sb("Wr1", [P, E1])]
        br = [sb("br0", [P, E0]), sb("br1", [P, E1])]
        b1 = [sb("b10", [P, E0, F0 // P]), sb("b11", [P, E1, F1 // P])]
        b2 = [sb("b20", [E0, D]), sb("b21", [E1, D])]
        ln_g = sb("ln_g", [P, 1])
        ln_b = sb("ln_b", [P, 1])
        half = sb("half", [P, 1])
        eps_c = sb("eps_c", [P, 1])
        pbias_c = sb("pbias_c", [P, 1])
        EF = E0 * F0
        w1_hi = sb("w1_hi", [P, EF], F16)
        w1_lo = sb("w1_lo", [P, EF], F16)
        w2_hi = sb("w2_hi", [P, EF + F0], F16)
        w2_lo = sb("w2_lo", [P, EF + F0], F16)
        stage_a = sb("stage_a", [P, EF])
        stage_b = sb("stage_b", [P, EF])
        pw_raw = sb("pw_raw", [P, 4, D])
        pw_hi = sb("pw_hi", [P, 4, D], F16)
        pw_lo = sb("pw_lo", [P, 4, D], F16)
        st = sb("st", [P, TB, 6])
        held = sb("held", [P, 1])
        agg = sb("agg", [P, TB, 2])
        mv = sb("mv", [P, NT, 2])
        sd = sb("sd", [P, NT])
        r0 = sb("r0", [P, NT])
        nt1 = sb("nt1", [P, NT])
        nt2 = sb("nt2", [P, NT])
        nt3 = sb("nt3", [P, NT])
        rs = sb("rs", [P, NT])
        var2 = sb("var2", [P, NT])
        rs2 = sb("rs2", [P, NT])
        unscale = sb("unscale", [P, NT])
        xh = sb("xh", [P, 2, TB, P])
        xT32 = sb("xT32", [P, 2, N])
        wA = sb("wA", [P, 2, N])
        wB = sb("wB", [P, 2, N])
        wC = sb("wC", [P, 2, N])
        wD = sb("wD", [P, 2, N])
        hT = sb("hT", [P, 2, N])
        lg = sb("lg", [P, TB, E1])
        top = sb("top", [P, TB, 8])
        idx = sb("idx", [P, TB, 8], U32)
        idf = sb("idf", [P, TB, 8])
        eqk = sb("eqk", [P, 4, TB, E1])
        ex = sb("ex", [P, TB, E1])
        exm = sb("exm", [P, TB, E1])
        num = sb("num", [P, TB, E1])
        den = sb("den", [P, TB])
        rden = sb("rden", [P, TB])
        cblk = sb("cblk", [P, TB, E1])
        comb = sb("comb", [P, NB * E1 * TB])
        cT = sb("cT", [E1, TB, P])
        NIM = F0 // P
        h32 = sb("h32", [P, 4, N])
        h_parts = sb("h_parts", [P, 2, 2, NIM, N], F16)
        h_hi, h_lo = h_parts[:, 0], h_parts[:, 1]
        q_hi = sb("q_hi", [P, S], F16)
        q_lo = sb("q_lo", [P, S], F16)
        k_hi = sb("k_hi", [P, S], F16)
        k_lo = sb("k_lo", [P, S], F16)
        VC = D + 2
        v_hi = sb("v_hi", [P, JT, VC], F16)
        v_lo = sb("v_lo", [P, JT, VC], F16)
        nmax = sb("nmax", [P, JT])
        dg = sb("dg", [P, JT, P], BF16)
        osum = sb("osum", [P, JT])
        o32 = sb("o32", [P, JT, P])
        o_hi = sb("o_hi", [P, JT, P], F16)
        o_lo = sb("o_lo", [P, JT, P], F16)

        pr_hi = stage_b[:].bitcast(F16).rearrange("p (a k n) -> p a k n", a=2, k=JT)
        pr_lo = h_parts[:].rearrange("p a q c n -> p (a q c n)").rearrange("p (a k n) -> p a k n", a=2, k=JT)

        in_x = [sem(f"in_x{b}") for b in range(B)]
        in_W = sem("in_W")
        in_small = sem("in_small")
        in_pw = sem("in_pw")
        in_w1 = sem("in_w1")
        in_w2 = sem("in_w2")
        x2_out = sem("x2_out")
        x2_in = sem("x2_in")
        y_out = sem("y_out")
        pool_const = sem("pool_const")
        pool_zero = sem("pool_zero")
        consts = sem("consts")
        W_split = sem("W_split")
        W_hi_done = sem("W_hi_done")
        stats = sem("stats")
        aggr = sem("aggr")
        mv_copied = sem("mv_copied")
        sqrt_done = sem("sqrt_done")
        newton = sem("newton")
        var2_done = sem("var2_done")
        normed = sem("normed")
        transposed = sem("transposed")
        hi_made = sem("hi_made")
        t32_made = sem("t32_made")
        lo_made = sem("lo_made")
        hg_done = sem("hg_done")
        gates = sem("gates")
        g_max = sem("g_max")
        bz = sem("bz")
        scanned = sem("scanned")
        back_t = sem("back_t")
        x_added = sem("x_added")
        routed_mm = sem("routed_mm")
        rt = sem("rt")
        exp_done = sem("exp_done")
        c_ready = sem("c_ready")
        cT_mm = sem("cT_mm")
        cT_cp = sem("cT_cp")
        b2_mm = sem("b2_mm")
        b2_added = sem("b2_added")
        ew_hi = sem("ew_hi")
        ew_lo = sem("ew_lo")
        g1_done = sem("g1_done")
        act_done = sem("act_done")
        hhi_done = sem("hhi_done")
        hlo_done = sem("hlo_done")
        g2_done = sem("g2_done")
        acc_done = sem("acc_done")
        pw_t = sem("pw_t")
        pw_hi_done = sem("pw_hi_done")
        pw_lo_done = sem("pw_lo_done")
        proj_mm = sem("proj_mm")
        proj_hi = sem("proj_hi")
        proj_lo = sem("proj_lo")
        v_const = sem("v_const")
        sn_mm = sem("sn_mm")
        max_done = sem("max_done")
        diag_done = sem("diag_done")
        st_mm = sem("st_mm")
        p_exp = sem("p_exp")
        p_hi = sem("p_hi")
        p_lo = sem("p_lo")
        pv_mm = sem("pv_mm")
        o_rcp = sem("o_rcp")
        o_norm = sem("o_norm")
        o_hi_done = sem("o_hi_done")
        o_lo_done = sem("o_lo_done")
        wo_mm = sem("wo_mm")
        x3_done = sem("x3_done")

        x_in = L0_attn_x.rearrange("b (j p) d -> b p j d", p=P)
        x2_nat = x2_dram.rearrange("b (j p) d -> b p j d", p=P)
        x2_per = x2_dram.rearrange("b (e j) d -> b e (j d)", j=JT)
        out_per = out.rearrange("b (e j) d -> b e (j d)", j=JT)

        block = ctx.enter_context(nc.Block())

        LAYERS = [dict(n=0, E=E0, NI=F0 // P, K=1, func=ACT.Relu), dict(n=1, E=E1, NI=F1 // P, K=4, func=ACT.Gelu)]
        NSM = 13

        chunk0 = [0, NB * E0 * (F0 // P)]
        step0 = [0, NB * E0]

        RT_STEPS = {0: ["logits", "top", "index", "shifted", "idf", "eq", "num", "den", "rden", "c"],
                    1: ["logits", "top", "index", "shifted", "idf", "eq", "sum1", "sum2", "num", "den", "rden", "c"]}

        def rt_at(n, i, step):
            per = [len(RT_STEPS[0]), len(RT_STEPS[1])]
            return (0 if n == 0 else NB * per[0]) + i * per[n] + RT_STEPS[n].index(step) + 1

        @block.sync
        def _(sp):
            for b in range(B):
                sp.dma_start(x[:, JT * b:JT * (b + 1), :], x_in[b]).then_inc(in_x[b], 16)
                if b == 0:
                    sp.dma_start(W_raw[:], L0_attn_W).then_inc(in_W, 16)
            for dst, src in (
                    (Wr[0][:], L0_ffn_Wr), (Wr[1][:], L1_ffn_router_w),
                    (br[0][:], L0_ffn_br.rearrange("(a e) -> a e", a=1).partition_broadcast(P)),
                    (br[1][:], L1_ffn_router_b.rearrange("(a e) -> a e", a=1).partition_broadcast(P)),
                    (b1[0][:], L0_ffn_b1.rearrange("e (p c) -> p e c", p=P)),
                    (b1[1][:], L1_ffn_b1.rearrange("e (p c) -> p e c", p=P)),
                    (b2[0][:], L0_ffn_b2), (b2[1][:], L1_ffn_b2),
                    (ln_g[:], L0_ffn_ln_g.rearrange("(p a) -> p a", a=1)),
                    (ln_b[:], L0_ffn_ln_b.rearrange("(p a) -> p a", a=1))):
                sp.dma_start(dst, src).then_inc(in_small, 16)
            for n, w in enumerate((L1_attn_wq, L1_attn_wk, L1_attn_wv, L1_attn_wo)):
                sp.dma_start(pw_raw[:, n, :], w).then_inc(in_pw, 16)
            for n, (w1, w2) in enumerate(((L0_ffn_W1, L0_ffn_W2), (L1_ffn_w1, L1_ffn_w2))):
                E = LAYERS[n]["E"]
                if n == 1:
                    sp.wait_ge(ew_lo, 3)
                sp.dma_start(stage_a[:].rearrange("p (e f) -> p e f", e=E),
                             w1.rearrange("e d f -> d e f")).then_inc(in_w1, 16)
                sp.dma_start(stage_b[:].rearrange("p (e f) -> p e f", e=E),
                             w2.rearrange("e (p c) d -> p e (c d)", p=P)).then_inc(in_w2, 16)
            sp.wait_ge(acc_done, NB * E0)
            for b in range(B):
                sp.dma_start(x2_nat[b], x[:, JT * b:JT * (b + 1), :]).then_inc(x2_out, 16)
            sp.wait_ge(x2_out, 16 * B)
            sp.wait_ge(ew_lo, 6)
            for b in range(B):
                sp.dma_start(stage_a[:, b * S:(b + 1) * S], x2_per[b]).then_inc(x2_in, 16)
            sp.wait_ge(acc_done, NB * (E0 + E1))
            for b in range(B):
                sp.dma_start(out_per[b], x[:, JT * b:JT * (b + 1), :].rearrange("p j d -> p (j d)")).then_inc(y_out, 16)
            sp.wait_ge(y_out, 16 * B)

        @block.gpsimd
        def _(pool):
            nc.gpsimd.memset(ident[:], 0.0).then_inc(pool_zero, 1)
            nc.gpsimd.memset(ones_bf[:], 1.0).then_inc(pool_const, 1)
            nc.gpsimd.memset(half[:], 0.5).then_inc(pool_const, 1)
            nc.gpsimd.memset(eps_c[:], EPS).then_inc(pool_const, 1)
            nc.gpsimd.memset(pbias_c[:], PBIAS).then_inc(pool_const, 1)
            nc.gpsimd.iota(iota_i[:], [[1, E1]], channel_multiplier=0).then_inc(pool_zero, 1)
            pool.wait_ge(pool_zero, 2)
            nc.gpsimd.affine_select(out=ident[:], in_=ident[:], compare_op=ALU.not_equal, fill=1.0, base=0,
                                    pattern=[[-1, P]], channel_multiplier=1).then_inc(pool_const, 1)
            nc.gpsimd.tensor_copy(iota_e[:], iota_i[:]).then_inc(pool_const, 1)
            nc.gpsimd.memset(v_hi[:, :, D:D + 1], 1.0).then_inc(v_const, 1)
            nc.gpsimd.memset(v_hi[:, :, D + 1:VC], 0.0).then_inc(v_const, 1)
            nc.gpsimd.memset(v_lo[:, :, D:VC], 0.0).then_inc(v_const, 1)

        @block.scalar
        def _(act):
            act.wait_ge(pool_const, 6)
            act.wait_ge(in_W, 16)
            nc.scalar.mul(W_hi[:], W_raw[:], WS).then_inc(W_hi_done, 1)

            def sqrt_of_variance(k):
                act.wait_ge(mv_copied, (k + 1) * NB)
                nc.scalar.activation(sd[:], mv[:, :, 1], ACT.Sqrt, bias=eps_c[:]).then_inc(sqrt_done, 1)

            sqrt_of_variance(0)
            with act.Fori(0, B) as b:
                for h in range(2):
                    i = b * 2 + h
                    act.wait_ge(transposed, i + 1)
                    nc.scalar.copy(xT_hi[:, ds(i * N, N)], ps[:, h, :]).then_inc(hi_made, 1)
                    act.wait_ge(hg_done, i + 1)
                    act.wait_ge(scanned, b * 2)
                    nc.scalar.activation(wA[:, h, :], ps[:, 4 + h, :], ACT.Sigmoid, scale=-1.0 / WS)
                    nc.scalar.activation(wB[:, h, :], ps[:, 4 + h, :], ACT.Sigmoid, scale=1.0 / WS)
                    nc.scalar.activation(wC[:, h, :], ps[:, 2 + h, :], ACT.Sigmoid, scale=1.0 / WS)
                    nc.scalar.activation(wD[:, h, :], ps[:, 2 + h, :], ACT.Identity, scale=1.0 / WS,
                                         bias=half[:]).then_inc(gates, 1)

            def experts(L):
                n, E, NI, func = L["n"], L["E"], L["NI"], L["func"]
                with act.Fori(0, B) as b:
                    for h in range(2):
                        i = b * 2 + h
                        ti = (1 + 2 * n) * NB + i
                        act.wait_ge(transposed, ti + 1)
                        act.wait_ge(routed_mm, n * NB + b * 2)
                        nc.scalar.copy(xT32[:, h, :], ps[:, h, :]).then_inc(t32_made, 1)
                        if n == 0:
                            nc.scalar.activation(wA[:, h, :], ps[:, h, :], ACT.Identity, scale=ln_g[:],
                                                 bias=ln_b[:]).then_inc(gates, 1)
                            act.wait_ge(gates, NB + i + 1)
                            nc.scalar.copy(xT_hi[:, ds(i * N, N)], wA[:, h, :]).then_inc(hi_made, 1)
                        else:
                            nc.scalar.copy(xT_hi[:, ds(i * N, N)], ps[:, h, :]).then_inc(hi_made, 1)
                        act.wait_ge(rt, rt_at(n, i, "shifted"))
                        nc.scalar.activation(ex[:, :, 0:E], exm[:, :, 0:E], ACT.Exp).then_inc(exp_done, 1)
                        act.wait_ge(cT_mm, n * NB + i + 1)
                        nc.scalar.copy(cT[0:E, :, :], ps[0:E, 4 + h, :].rearrange("e (t p) -> e t p", t=TB)).then_inc(cT_cp, 1)

                def pair(f):
                    for q in range(2):
                        s = f * 2 + q
                        for c0 in range(0, NI, 2):
                            for ic in (c0, c0 + 1):
                                ch = s * NI + ic
                                slot = (q * NI + ic) % 4
                                act.wait_ge(g1_done, chunk0[n] + ch + 1)
                                if not (isinstance(f, int) and n == 0 and ch < 4):
                                    act.wait_ge(hlo_done, chunk0[n] + ch - 3)
                                e = (f % (E // 2)) * 2 + q
                                nc.scalar.activation(h32[:, slot, :], ps[:, slot, :], func, scale=1.0 / WS,
                                                     bias=b1[n][:, ds(e, 1), ic]).then_inc(act_done, 1)
                            for ic in (c0, c0 + 1):
                                ch = s * NI + ic
                                slot = (q * NI + ic) % 4
                                act.wait_ge(act_done, chunk0[n] + ch + 1)
                                if not (isinstance(f, int) and s < 2):
                                    act.wait_ge(g2_done, step0[n] + s - 1)
                                nc.scalar.copy(h_hi[:, q, ic, :], h32[:, slot, :]).then_inc(hhi_done, 1)

                pair(0)
                with act.Fori(1, NB * E // 2) as f:
                    pair(f)

            def split_experts(L):
                n, E, NI = L["n"], L["E"], L["NI"]
                w1v = stage_a[:].rearrange("d (e p c) -> d e c p", e=E, c=NI)
                act.wait_ge(in_w1, 16 * (n + 1))
                act.wait_ge(g2_done, step0[n])
                nc.scalar.mul(w1_hi[:].rearrange("d (e c p) -> d e c p", e=E, c=NI), w1v, WS).then_inc(ew_hi, 1)
                act.wait_ge(in_w2, 16 * (n + 1))
                FE = NI * P
                nc.scalar.mul(w2_hi[:, FE:FE + EF], stage_b[:], WS).then_inc(ew_hi, 1)
                nc.scalar.mul(w2_hi[:, 0:FE], stage_b[:, EF - FE:EF], WS).then_inc(ew_hi, 1)

            split_experts(LAYERS[0])
            sqrt_of_variance(1)
            act.wait_ge(var2_done, 1)
            nc.scalar.activation(sd[:], var2[:], ACT.Sqrt, bias=eps_c[:]).then_inc(sqrt_done, 1)
            experts(LAYERS[0])

            split_experts(LAYERS[1])
            act.wait_ge(pw_t, 1)
            nc.scalar.mul(pw_hi[:].rearrange("p n d -> p (n d)"), ps[:, 2, :], WS).then_inc(pw_hi_done, 1)
            sqrt_of_variance(2)
            with act.Fori(0, B) as b:
                for h in range(2):
                    i = b * 2 + h
                    act.wait_ge(transposed, 2 * NB + i + 1)
                    nc.scalar.copy(xT_hi[:, ds(i * N, N)], ps[:, h, :]).then_inc(hi_made, 1)
            with act.Fori(0, B) as b:
                for m in range(6):
                    act.wait_ge(proj_mm, b * 6 + m + 1)
                    bank, hc = ps[:, 6 + m % 2, :], m % 2
                    if m == 0:
                        act.wait_ge(st_mm, b * 16)
                    if m == 4:
                        act.wait_ge(pv_mm, b * JT)
                    if m < 4:
                        dst = (q_hi if m < 2 else k_hi)[:, hc * N:(hc + 1) * N]
                        sc = SCORE / WS if m < 2 else 1.0 / WS
                        nc.scalar.mul(dst, bank, sc).then_inc(proj_hi, 1)
                    else:
                        nc.scalar.mul(v_hi[:, hc * TB:(hc + 1) * TB, 0:D], bank.rearrange("p (t d) -> p t d", t=TB),
                                      1.0 / WS).then_inc(proj_hi, 1)
                for qh in range(2):
                    for kt in range(JT):
                        u = b * 16 + qh * JT + kt
                        k = kt % 2
                        act.wait_ge(st_mm, u + 1)
                        if qh == 0 and kt < 2:
                            act.wait_ge(p_lo, b * 16)
                        else:
                            act.wait_ge(p_lo, u - 1)
                        nc.scalar.activation(wA[:, k, :], ps[:, 4 + k, :], ACT.Exp, bias=pbias_c[:]).then_inc(p_exp, 1)
                act.wait_ge(o_norm, b * JT + JT)
                act.wait_ge(wo_mm, b)
                nc.scalar.copy(o_hi[:], o32[:]).then_inc(o_hi_done, 1)

            sqrt_of_variance(3)
            experts(LAYERS[1])

        @block.vector
        def _(dve):
            dve.wait_ge(W_hi_done, 1)
            nc.vector.scalar_tensor_tensor(out=W_lo[:], in0=W_raw[:], scalar=WS, in1=W_hi[:], op0=ALU.mult,
                                           op1=ALU.subtract).then_inc(W_split, 1)
            nwt = [0]

            def wait_alone(semaphore, value):
                dve.wait_ge(semaphore, value)
                nc.vector.memset(held[:], 0.0)

            def small(ins):
                nwt[0] += 1
                ins.then_inc(newton, 1)
                dve.wait_ge(newton, nwt[0])

            def statistics(k):
                with dve.Fori(0, NB) as i:
                    for t in range(TB):
                        nc.vector.bn_stats(st[:, t, :], x[:, ds(i * TB + t, 1), :].rearrange("p a d -> p (a d)")).then_inc(stats, 1)
                    dve.wait_ge(mv_copied, k * NB + i)
                    wait_alone(stats, (k * NB + i + 1) * TB)
                    for t in range(TB):
                        nc.vector.bn_aggr(agg[:, t, :], st[:, t, :]).then_inc(aggr, 1)
                    dve.wait_ge(aggr, (k * NB + i + 1) * TB)
                    nc.vector.tensor_copy(mv[:, ds(i * TB, TB), :], agg[:]).then_inc(mv_copied, 1)
                dve.wait_ge(mv_copied, (k + 1) * NB)

            def rsqrt(k, var, res):
                dve.wait_ge(sqrt_done, k + 1)
                small(nc.vector.reciprocal(r0[:], sd[:]))
                small(nc.vector.tensor_tensor(nt1[:], r0[:], r0[:], ALU.mult))
                small(nc.vector.scalar_tensor_tensor(out=nt2[:], in0=var, scalar=EPS, in1=nt1[:], op0=ALU.add, op1=ALU.mult))
                small(nc.vector.tensor_scalar(nt3[:], nt2[:], -0.5, 1.5, ALU.mult, ALU.add))
                small(nc.vector.tensor_tensor(res, r0[:], nt3[:], ALU.mult))

            def normalise(k, i, h, scale):
                for t in range(TB):
                    tile = i * TB + t
                    ins = nc.vector.tensor_scalar(xh[:, h, t, :], x[:, ds(tile, 1), :].rearrange("p a d -> p (a d)"),
                                                  mv[:, ds(tile, 1), 0], scale[:, ds(tile, 1)], ALU.subtract, ALU.mult)
                ins.then_inc(normed, 1)

            def xh_free(k, b):
                dve.wait_ge(transposed, k * NB + b * 2)

            for b in range(B):
                dve.wait_ge(in_x[b], 16)
            statistics(0)
            rsqrt(0, mv[:, :, 1], rs[:])
            with dve.Fori(0, B) as b:
                xh_free(0, b)
                for h in range(2):
                    normalise(0, b * 2 + h, h, rs)
                for h in range(2):
                    i = b * 2 + h
                    dve.wait_ge(hi_made, i + 1)
                    nc.vector.tensor_tensor(xT_lo[:, ds(i * N, N)], ps[:, h, :], xT_hi[:, ds(i * N, N)],
                                            ALU.subtract).then_inc(lo_made, 1)
                for h in range(2):
                    i = b * 2 + h
                    dve.wait_ge(gates, i + 1)
                    nc.vector.tensor_tensor(wC[:, h, :], wC[:, h, :], wD[:, h, :], ALU.max).then_inc(g_max, 1)
                    dve.wait_ge(g_max, i + 1)
                    nc.vector.tensor_tensor(wB[:, h, :], wB[:, h, :], wC[:, h, :], ALU.mult).then_inc(bz, 1)
                    dve.wait_ge(bz, i + 1)
                    if h == 0:
                        dve.wait_ge(back_t, b * 2)
                        nc.vector.tensor_tensor_scan(hT[:, h, :], wA[:, h, :], wB[:, h, :], 0.0, ALU.mult, ALU.add).then_inc(scanned, 1)
                    else:
                        dve.wait_ge(scanned, i)
                        nc.vector.tensor_tensor_scan(hT[:, h, :], wA[:, h, :], wB[:, h, :], hT[:, 0, N - 1:N], ALU.mult,
                                                     ALU.add).then_inc(scanned, 1)
                for h in range(2):
                    i = b * 2 + h
                    dve.wait_ge(back_t, i + 1)
                    xb = x[:, ds(i * TB, TB), :].rearrange("p t d -> p (t d)")
                    nc.vector.tensor_tensor(xb, ps[:, 6 + h, :], xb, ALU.add).then_inc(x_added, 1)

            def bc(ap, n):
                return ap.unsqueeze(2).to_broadcast([P, TB, n])

            def prepare(L, k, scale):
                n, E, K = L["n"], L["E"], L["K"]

                def step(ins, i, name):
                    ins.then_inc(rt, 1)
                    (wait_alone if name in ("logits", "top") else dve.wait_ge)(rt, rt_at(n, i, name))

                with dve.Fori(0, B) as b:
                    xh_free(k, b)
                    for h in range(2):
                        normalise(k, b * 2 + h, h, scale)
                    for h in range(2):
                        i = b * 2 + h
                        dve.wait_ge(hi_made, k * NB + i + 1)
                        src = wA[:, h, :] if n == 0 else ps[:, h, :]
                        nc.vector.tensor_tensor(xT_lo[:, ds(i * N, N)], src, xT_hi[:, ds(i * N, N)],
                                                ALU.subtract).then_inc(lo_made, 1)
                        dve.wait_ge(routed_mm, n * NB + i + 1)
                        lgE = lg[:, :, 0:E]
                        raw = ps[:, 2 + h, 0:TB * E].rearrange("p (t e) -> p t e", t=TB)
                        brb = br[n][:].unsqueeze(1).to_broadcast([P, TB, E])
                        if n == 0:
                            nc.vector.tensor_tensor(num[:, :, 0:E], raw, bc(unscale[:, ds(i * TB, TB)], E), ALU.mult).then_inc(g_max, 1)
                            dve.wait_ge(g_max, NB + i + 1)
                            step(nc.vector.tensor_tensor(lgE, num[:, :, 0:E], brb, ALU.add), i, "logits")
                        else:
                            step(nc.vector.tensor_tensor(lgE, raw, brb, ALU.add), i, "logits")
                        for t in range(TB):
                            ins = nc.vector.max(top[:, t, :], lg[:, t, 0:E])
                        step(ins, i, "top")
                        for t in range(TB):
                            ins = nc.vector.max_index(idx[:, t, :], top[:, t, :], lg[:, t, 0:E])
                        step(ins, i, "index")
                        step(nc.vector.tensor_tensor(exm[:, :, 0:E], lgE, bc(top[:, :, 0], E), ALU.subtract), i, "shifted")
                        step(nc.vector.tensor_copy(idf[:], idx[:]), i, "idf")
                        iob = iota_e[:, 0:E].unsqueeze(1).to_broadcast([P, TB, E])
                        for kk in range(K):
                            ins = nc.vector.tensor_tensor(eqk[:, kk, :, 0:E], iob, bc(idf[:, :, kk], E), ALU.is_equal)
                        step(ins, i, "eq")
                        if K == 4:
                            step(nc.vector.tensor_tensor(eqk[:, 0:2, :, 0:E], eqk[:, 0:2, :, 0:E], eqk[:, 2:4, :, 0:E], ALU.add), i, "sum1")
                            step(nc.vector.tensor_tensor(eqk[:, 0, :, 0:E], eqk[:, 0, :, 0:E], eqk[:, 1, :, 0:E], ALU.add), i, "sum2")
                        dve.wait_ge(exp_done, n * NB + i + 1)
                        step(nc.vector.tensor_tensor(num[:, :, 0:E], ex[:, :, 0:E], eqk[:, 0, :, 0:E], ALU.mult), i, "num")
                        step(nc.vector.tensor_reduce(den[:], (ex if K == 1 else num)[:, :, 0:E], AX_X, ALU.add), i, "den")
                        step(nc.vector.reciprocal(rden[:], den[:]), i, "rden")
                        dve.wait_ge(cT_mm, n * NB + i)
                        step(nc.vector.tensor_tensor(cblk[:, :, 0:E], num[:, :, 0:E], bc(rden[:], E), ALU.mult), i, "c")
                        cv = comb[:, ds(i * (E * TB), E * TB)].rearrange("p (e t) -> p t e", t=TB)
                        nc.vector.tensor_scalar(cv, cblk[:, :, 0:E], 1.0 / WS, None, ALU.mult).then_inc(c_ready, 1)
                        dve.wait_ge(b2_mm, n * NB + i + 1)
                        xb = x[:, ds(i * TB, TB), :].rearrange("p t d -> p (t d)")
                        nc.vector.tensor_tensor(xb, ps[:, 6 + h, :], xb, ALU.add).then_inc(b2_added, 1)
                dve.wait_ge(b2_added, (n + 1) * NB)

            def split_experts(L):
                n, E, NI = L["n"], L["E"], L["NI"]
                FE = NI * P
                w1v = stage_a[:].rearrange("d (e p c) -> d e c p", e=E, c=NI)
                dve.wait_ge(ew_hi, 3 * (n + 1))
                for e in range(E):
                    sl = slice(e * FE, (e + 1) * FE)
                    ins = nc.vector.scalar_tensor_tensor(
                        out=w1_lo[:, sl].rearrange("d (c p) -> d c p", c=NI), in0=w1v[:, e], scalar=WS,
                        in1=w1_hi[:, sl].rearrange("d (c p) -> d c p", c=NI), op0=ALU.mult, op1=ALU.subtract)
                ins.then_inc(ew_lo, 1)
                nc.vector.scalar_tensor_tensor(out=w2_lo[:, FE:FE + EF], in0=stage_b[:], scalar=WS, in1=w2_hi[:, FE:FE + EF],
                                               op0=ALU.mult, op1=ALU.subtract).then_inc(ew_lo, 1)
                nc.vector.scalar_tensor_tensor(out=w2_lo[:, 0:FE], in0=stage_b[:, EF - FE:EF], scalar=WS, in1=w2_hi[:, 0:FE],
                                               op0=ALU.mult, op1=ALU.subtract).then_inc(ew_lo, 1)

            def experts(L):
                n, E, NI = L["n"], L["E"], L["NI"]

                def accumulate(s, q):
                    dve.wait_ge(g2_done, step0[n] + s + 1)
                    if not (isinstance(s, int) and s == 0):
                        dve.wait_ge(acc_done, step0[n] + s)
                    for t in range(TB):
                        tile = (s // E) * TB + t
                        xt = x[:, ds(tile, 1), :].rearrange("p a d -> p (a d)")
                        ins = nc.vector.scalar_tensor_tensor(out=xt, in0=ps[:, 4 + q, t * P:(t + 1) * P],
                                                             scalar=comb[:, ds(s * TB + t, 1)], in1=xt,
                                                             op0=ALU.mult, op1=ALU.add)
                    ins.then_inc(acc_done, 1)

                def pair(f):
                    for q in range(2):
                        s = f * 2 + q
                        for ic in range(NI):
                            ch = s * NI + ic
                            slot = (q * NI + ic) % 4
                            dve.wait_ge(hhi_done, chunk0[n] + ch + 1)
                            nc.vector.tensor_tensor(h_lo[:, q, ic, :], h32[:, slot, :], h_hi[:, q, ic, :],
                                                    ALU.subtract).then_inc(hlo_done, 1)
                        if not (isinstance(f, int) and s == 0):
                            accumulate(s - 1, 1 - q)

                pair(0)
                with dve.Fori(1, NB * E // 2) as f:
                    pair(f)
                accumulate(NB * E - 1, 1)
                dve.wait_ge(acc_done, step0[n] + NB * E)

            split_experts(LAYERS[0])
            dve.wait_ge(x_added, NB)
            statistics(1)
            rsqrt(1, mv[:, :, 1], rs[:])
            small(nc.vector.tensor_tensor(nt1[:], rs[:], rs[:], ALU.mult))
            nc.vector.tensor_tensor(var2[:], mv[:, :, 1], nt1[:], ALU.mult).then_inc(var2_done, 1)
            dve.wait_ge(var2_done, 1)
            rsqrt(2, var2[:], rs2[:])
            small(nc.vector.scalar_tensor_tensor(out=unscale[:], in0=var2[:], scalar=EPS, in1=rs2[:], op0=ALU.add,
                                                 op1=ALU.mult))
            small(nc.vector.tensor_tensor(rs[:], rs[:], rs2[:], ALU.mult))
            prepare(LAYERS[0], 1, rs)
            experts(LAYERS[0])

            split_experts(LAYERS[1])
            dve.wait_ge(pw_hi_done, 1)
            nc.vector.scalar_tensor_tensor(out=pw_lo[:].rearrange("p n d -> p (n d)"), in0=ps[:, 2, :], scalar=WS,
                                           in1=pw_hi[:].rearrange("p n d -> p (n d)"), op0=ALU.mult,
                                           op1=ALU.subtract).then_inc(pw_lo_done, 1)
            statistics(2)
            rsqrt(3, mv[:, :, 1], rs[:])
            with dve.Fori(0, B) as b:
                xh_free(2, b)
                for h in range(2):
                    normalise(2, b * 2 + h, h, rs)
                for h in range(2):
                    i = b * 2 + h
                    dve.wait_ge(hi_made, 2 * NB + i + 1)
                    nc.vector.tensor_tensor(xT_lo[:, ds(i * N, N)], ps[:, h, :], xT_hi[:, ds(i * N, N)],
                                            ALU.subtract).then_inc(lo_made, 1)
            dve.wait_ge(x2_in, 16 * B)
            dve.wait_ge(v_const, 3)
            with dve.Fori(0, B) as b:
                for m in range(6):
                    dve.wait_ge(proj_hi, b * 6 + m + 1)
                    bank, hc = ps[:, 6 + m % 2, :], m % 2
                    if m < 4:
                        cols = slice(hc * N, (hc + 1) * N)
                        hi, lo = (q_hi, q_lo) if m < 2 else (k_hi, k_lo)
                        hi, lo = hi[:, cols], lo[:, cols]
                    else:
                        bank = bank.rearrange("p (t d) -> p t d", t=TB)
                        hi, lo = v_hi[:, hc * TB:(hc + 1) * TB, 0:D], v_lo[:, hc * TB:(hc + 1) * TB, 0:D]
                    nc.vector.scalar_tensor_tensor(out=lo, in0=bank, scalar=SCORE / WS if m < 2 else 1.0 / WS, in1=hi,
                                                   op0=ALU.mult, op1=ALU.subtract).then_inc(proj_lo, 1)
                dve.wait_ge(st_mm, b * 2 * JT)
                for qt in range(JT):
                    dve.wait_ge(sn_mm, b * JT + qt + 1)
                    pair = 2 * (qt % 2)
                    nc.vector.tensor_reduce(nmax[:, qt:qt + 1], ps[:, pair:pair + 2, :].rearrange("p a n -> p (a n)"),
                                            AX_X, ALU.max).then_inc(max_done, 1)
                    dve.wait_ge(max_done, b * JT + qt + 1)
                    nc.vector.tensor_scalar(dg[:, qt, :], ident[:], nmax[:, qt:qt + 1], -1.0, ALU.mult,
                                            ALU.mult).then_inc(diag_done, 1)
                dve.wait_ge(pv_mm, b * JT)
                for qh in range(2):
                    for kt in range(JT):
                        u = b * 2 * JT + qh * JT + kt
                        dve.wait_ge(p_exp, u + 1)
                        nc.vector.tensor_copy(pr_hi[:, qh, kt, :], wA[:, kt % 2, :]).then_inc(p_hi, 1)
                        dve.wait_ge(p_hi, u + 1)
                        nc.vector.tensor_tensor(pr_lo[:, qh, kt, :], wA[:, kt % 2, :], pr_hi[:, qh, kt, :],
                                                ALU.subtract).then_inc(p_lo, 1)
                dve.wait_ge(o_hi_done, b)
                for qt in range(JT):
                    dve.wait_ge(pv_mm, b * JT + qt + 1)
                    nc.vector.reciprocal(osum[:, qt:qt + 1], ps[:, 6 + qt % 2, D:D + 1]).then_inc(o_rcp, 1)
                    dve.wait_ge(o_rcp, b * JT + qt + 1)
                    nc.vector.tensor_scalar(o32[:, qt, :], ps[:, 6 + qt % 2, 0:D], osum[:, qt:qt + 1], None,
                                            ALU.mult).then_inc(o_norm, 1)
                dve.wait_ge(o_hi_done, b + 1)
                nc.vector.tensor_tensor(o_lo[:], o32[:], o_hi[:], ALU.subtract).then_inc(o_lo_done, 1)
                dve.wait_ge(wo_mm, b + 1)
                nc.vector.scalar_tensor_tensor(out=x[:, ds(b * JT, JT), :].rearrange("p j d -> p (j d)"),
                                               in0=ps[:, 0:2, :].rearrange("p a n -> p (a n)"), scalar=1.0 / WS,
                                               in1=stage_a[:, ds(b * S, S)], op0=ALU.mult, op1=ALU.add).then_inc(x3_done, 1)

            dve.wait_ge(x3_done, B)
            statistics(3)
            rsqrt(4, mv[:, :, 1], rs[:])
            prepare(LAYERS[1], 3, rs)
            experts(LAYERS[1])

        @block.tensor
        def _(pe):
            mm = nc.tensor.matmul

            def product(out, a, b, last=True):
                mm(out, a[0], b[0], start=True, stop=False)
                mm(out, a[0], b[1], start=False, stop=False)
                return mm(out, a[1], b[0], start=False, stop=last)

            def transposes(k, b):
                for h in range(2):
                    i = b * 2 + h
                    pe.wait_ge(normed, k * NB + i + 1)
                    pe.wait_ge(lo_made, k * NB + b * 2)
                    for t in range(TB):
                        ins = nc.tensor.transpose(ps[:, h, t * P:(t + 1) * P], xh[:, h, t, :], ident[:])
                    ins.then_inc(transposed, 1)

            pe.wait_ge(pool_const, 6)
            pe.wait_ge(W_split, 1)
            with pe.Fori(0, B) as b:
                transposes(0, b)
                for h in range(2):
                    i = b * 2 + h
                    pe.wait_ge(lo_made, i + 1)
                    pe.wait_ge(gates, b * 2)
                    xi = (xT_hi[:, ds(i * N, N)], xT_lo[:, ds(i * N, N)])
                    product(ps[:, 2 + h, :], (W_hi[:, 0:D], W_lo[:, 0:D]), xi)
                    product(ps[:, 4 + h, :], (W_hi[:, D:2 * D], W_lo[:, D:2 * D]), xi).then_inc(hg_done, 1)
                for h in range(2):
                    i = b * 2 + h
                    pe.wait_ge(scanned, i + 1)
                    pe.wait_ge(x_added, b * 2)
                    for t in range(TB):
                        ins = nc.tensor.transpose(ps[:, 6 + h, t * P:(t + 1) * P], hT[:, h, t * P:(t + 1) * P], ident[:])
                    ins.then_inc(back_t, 1)

            def prepare(L, k):
                n, E = L["n"], L["E"]
                with pe.Fori(0, B) as b:
                    transposes(k, b)
                    for h in range(2):
                        i = b * 2 + h
                        pe.wait_ge(t32_made, n * NB + i + 1)
                        for t in range(TB):
                            ins = mm(ps[:, 2 + h, t * E:(t + 1) * E], xT32[:, h, t * P:(t + 1) * P], Wr[n][:],
                                     start=True, stop=True)
                        ins.then_inc(routed_mm, 1)
                        pe.wait_ge(c_ready, n * NB + i + 1)
                        for t in range(TB):
                            ins = nc.tensor.transpose(ps[0:E, 4 + h, t * P:(t + 1) * P], cblk[:, t, 0:E], ident[:])
                        ins.then_inc(cT_mm, 1)
                        pe.wait_ge(cT_cp, n * NB + i + 1)
                        pe.wait_ge(b2_added, n * NB + b * 2)
                        for t in range(TB):
                            ins = mm(ps[:, 6 + h, t * P:(t + 1) * P], cT[0:E, t, :], b2[n][:], start=True, stop=True)
                        ins.then_inc(b2_mm, 1)

            def experts(L):
                n, E, NI = L["n"], L["E"], L["NI"]

                def first(f, q):
                    blk = f // (E // 2)
                    e = (f % (E // 2)) * 2 + q
                    xi = (xT_hi[:, ds(blk * N, N)], xT_lo[:, ds(blk * N, N)])
                    for ic in range(NI):
                        ch = (f * 2 + q) * NI + ic
                        slot = (q * NI + ic) % 4
                        if not (isinstance(f, int) and ch < 4):
                            pe.wait_ge(act_done, chunk0[n] + ch - 3)
                        w = ds((e * NI + ic) * P, P)
                        product(ps[:, slot, :], (w1_hi[:, w], w1_lo[:, w]), xi).then_inc(g1_done, 1)

                def second(slot_e, s, q):
                    pe.wait_ge(hlo_done, chunk0[n] + (s + 1) * NI)
                    if not (isinstance(s, int) and s < 2):
                        pe.wait_ge(acc_done, step0[n] + s - 1)
                    for t in range(TB):
                        tok = slice(t * P, (t + 1) * P)
                        o = ps[:, 4 + q, tok]
                        for ic in range(NI):
                            w = ds((slot_e * NI + ic) * P, P)
                            mm(o, h_hi[:, q, ic, tok], w2_hi[:, w], start=ic == 0, stop=False)
                            mm(o, h_hi[:, q, ic, tok], w2_lo[:, w], start=False, stop=False)
                            ins = mm(o, h_lo[:, q, ic, tok], w2_hi[:, w], start=False, stop=ic == NI - 1)
                    ins.then_inc(g2_done, 1)

                def pair(f):
                    e = (f % (E // 2)) * 2
                    first(f, 0)
                    if not isinstance(f, int):
                        second(e, f * 2 - 1, 1)
                    first(f, 1)
                    second(e + 1, f * 2, 0)

                pe.wait_ge(b2_added, (n + 1) * NB)
                pair(0)
                with pe.Fori(1, NB * E // 2) as f:
                    pair(f)
                second(E, NB * E - 1, 1)

            pe.wait_ge(in_small, 16 * 10)
            pe.wait_ge(x_added, NB)
            prepare(LAYERS[0], 1)
            pe.wait_ge(ew_lo, 3)
            experts(LAYERS[0])

            pe.wait_ge(in_pw, 16 * 4)
            pe.wait_ge(act_done, chunk0[1])
            for n in range(4):
                ins = nc.tensor.transpose(ps[:, 2, n * P:(n + 1) * P], pw_raw[:, n, :], ident[:])
            ins.then_inc(pw_t, 1)
            with pe.Fori(0, B) as b:
                transposes(2, b)
            pe.wait_ge(pw_lo_done, 1)
            pe.wait_ge(lo_made, 3 * NB)
            with pe.Fori(0, B) as b:
                for m in range(6):
                    hc = m % 2
                    bank = ps[:, 6 + hc, :]
                    if m < 2:
                        pe.wait_ge(o_norm, b * JT)
                    else:
                        pe.wait_ge(proj_lo, b * 6 + m - 1)
                    if m < 4:
                        cols = ds(b * S + hc * N, N)
                        w = m // 2
                        ins = product(bank, (pw_hi[:, w, :], pw_lo[:, w, :]), (xT_hi[:, cols], xT_lo[:, cols]))
                    else:
                        for t in range(TB):
                            cols = ds(b * S + (hc * TB + t) * P, P)
                            ins = product(bank[:, t * P:(t + 1) * P], (xT_hi[:, cols], xT_lo[:, cols]),
                                          (pw_hi[:, 2, :], pw_lo[:, 2, :]))
                    ins.then_inc(proj_mm, 1)
                pe.wait_ge(proj_hi, b * 6 + 4)
                pe.wait_ge(x3_done, b)
                for qt in range(JT):
                    if qt >= 2:
                        pe.wait_ge(max_done, b * JT + qt - 1)
                    for h in range(2):
                        ins = mm(ps[:, 2 * (qt % 2) + h, :], q_hi[:, qt * P:(qt + 1) * P], k_hi[:, h * N:(h + 1) * N],
                                 start=True, stop=True)
                    ins.then_inc(sn_mm, 1)
                pe.wait_ge(proj_lo, b * 6 + 4)
                for qh in range(2):
                    pe.wait_ge(diag_done, b * JT + (qh + 1) * TB)
                    for kt in range(JT):
                        u = b * 2 * JT + qh * JT + kt
                        if qh == 0 and kt < 2:
                            pe.wait_ge(p_exp, b * 2 * JT)
                        else:
                            pe.wait_ge(p_exp, u - 1)
                        o = ps[:, 4 + kt % 2, :]
                        kk, qq = slice(kt * P, (kt + 1) * P), slice(qh * N, (qh + 1) * N)
                        product(o, (k_hi[:, kk], k_lo[:, kk]), (q_hi[:, qq], q_lo[:, qq]), last=False)
                        mm(o, ones_bf[:], dg[:, qh * TB:(qh + 1) * TB, :].rearrange("p t q -> p (t q)"), start=False,
                           stop=True).then_inc(st_mm, 1)
                pe.wait_ge(proj_lo, b * 6 + 6)
                for qt in range(JT):
                    qh, t = qt // TB, qt % TB
                    if t == 0:
                        pe.wait_ge(p_lo, b * 2 * JT + (qh + 1) * JT)
                    if qt >= 2:
                        pe.wait_ge(o_norm, b * JT + qt - 1)
                    o = ps[:, 6 + qt % 2, 0:VC]
                    for kt in range(JT):
                        ph, pl = pr_hi[:, qh, kt, t * P:(t + 1) * P], pr_lo[:, qh, kt, t * P:(t + 1) * P]
                        mm(o, ph, v_hi[:, kt, :], start=kt == 0, stop=False)
                        mm(o, ph, v_lo[:, kt, :], start=False, stop=False)
                        ins = mm(o, pl, v_hi[:, kt, :], start=False, stop=kt == JT - 1)
                    ins.then_inc(pv_mm, 1)
                pe.wait_ge(o_lo_done, b + 1)
                for j in range(JT):
                    ins = product(ps[:, j // TB, (j % TB) * P:(j % TB + 1) * P], (o_hi[:, j, :], o_lo[:, j, :]),
                                  (pw_hi[:, 3, :], pw_lo[:, 3, :]))
                ins.then_inc(wo_mm, 1)

            prepare(LAYERS[1], 3)
            pe.wait_ge(ew_lo, 6)
            experts(LAYERS[1])


_INS = ["L0_attn_x", "L0_attn_W", "L0_ffn_Wr", "L0_ffn_br", "L0_ffn_ln_g", "L0_ffn_ln_b", "L0_ffn_W1", "L0_ffn_b1",
        "L0_ffn_W2", "L0_ffn_b2", "L1_attn_wq", "L1_attn_wk", "L1_attn_wv", "L1_attn_wo", "L1_ffn_router_w",
        "L1_ffn_router_b", "L1_ffn_w1", "L1_ffn_b1", "L1_ffn_w2", "L1_ffn_b2"]
_OUTS = [((4, 1024, 128), "float32")]


def kernel(**inputs):
    import numpy as _np
    import concourse.bacc as _bacc
    from concourse import mybir as _mybir
    from concourse.bass_utils import run_bass_kernel_spmd as _run

    nc = _bacc.Bacc("TRN2", target_bir_lowering=False, num_devices=1)
    arrays, args = {}, []
    for name in _INS:
        a = _np.ascontiguousarray(inputs[name])
        arrays[f"in_{name}_dram"] = a
        args.append(nc.dram_tensor(f"in_{name}_dram", a.shape, _mybir.dt.from_np(a.dtype), kind="ExternalInput").ap())
    for i, (shape, dtype) in enumerate(_OUTS):
        dt = _mybir.dt.from_np(_np.dtype(dtype))
        args.append(nc.dram_tensor(f"out_{i}_dram", shape, dt, kind="ExternalOutput").ap())
    build(nc, *args)
    r = _run(nc, [arrays], core_ids=[0])
    return r.results[0]["out_0_dram"]
```

```python
from contextlib import ExitStack

import concourse.bass as bass
from concourse import mybir

ALU = mybir.AluOpType
ACT = mybir.ActivationFunctionType
F32 = mybir.dt.float32
F16 = mybir.dt.float16
BF16 = mybir.dt.bfloat16
U32 = mybir.dt.uint32
AX_X = mybir.AxisListType.X
ds = bass.ds

P = 128
EPS = 1e-5
WS = 8.0
PBIAS = 6.931471805599453


def build(nc, L0_attn_x, L0_attn_W, L0_ffn_Wr, L0_ffn_br, L0_ffn_ln_g, L0_ffn_ln_b, L0_ffn_W1, L0_ffn_b1,
          L0_ffn_W2, L0_ffn_b2, L1_attn_wq, L1_attn_wk, L1_attn_wv, L1_attn_wo, L1_ffn_router_w,
          L1_ffn_router_b, L1_ffn_w1, L1_ffn_b1, L1_ffn_w2, L1_ffn_b2, out):
    B, S, D = L0_attn_x.shape
    NT = B * S // P
    TB = 4
    N = TB * P
    NB = NT // TB
    JT = S // P
    E0, _, F0 = L0_ffn_W1.shape
    E1, _, F1 = L1_ffn_w1.shape
    SCORE = 1.0 / float((D / 16) ** 0.5)
    assert D == P and NB == 2 * B and JT == 2 * TB and E0 * F0 == E1 * F1 and E0 == JT

    G = 2
    GT = NT // G
    GB = GT // TB
    QG = -(-(GT + E0 - 1) // TB)
    ST = QG * TB
    QUADS = G * QG
    NI0 = F0 // P
    NI1 = F1 // P
    LAG = 2
    QS = 4
    STEPS = NB * E1

    xs_dram = [nc.dram_tensor(f"xs_scratch{g}", (ST * P, D), F32, kind="Internal").ap() for g in range(G)]
    ys_dram = [nc.dram_tensor(f"ys_scratch{g}", (ST * P, D), F32, kind="Internal").ap() for g in range(G)]
    x2_dram = nc.dram_tensor("x2_scratch", (B, S, D), F32, kind="Internal").ap()

    with ExitStack() as ctx:
        def sb(name, shape, dt=F32):
            return ctx.enter_context(nc.sbuf_tensor(name, shape, dt))

        def sem(name):
            return ctx.enter_context(nc.semaphore(name))

        ps = ctx.enter_context(nc.psum_tensor("ps", [P, 8, N], F32))

        x = sb("x", [P, NT, D])
        xT_hi = sb("xT_hi", [P, NT * P], F16)
        xT_lo = sb("xT_lo", [P, NT * P], F16)
        ident = sb("ident", [P, P])
        ones_bf = sb("ones_bf", [P, P], BF16)
        iota_i = sb("iota_i", [P, E1], mybir.dt.int32)
        iota_e = sb("iota_e", [P, E1])
        W_raw = sb("W_raw", [P, 2 * D])
        W_hi = sb("W_hi", [P, 2 * D], F16)
        W_lo = sb("W_lo", [P, 2 * D], F16)
        Wr = [sb("Wr0", [P, E0]), sb("Wr1", [P, E1])]
        br = [sb("br0", [P, E0]), sb("br1", [P, E1])]
        b1 = sb("b1", [P, E1, F1 // P])
        b2 = sb("b2", [E1, D])
        ln_g = sb("ln_g", [P, 1])
        ln_b = sb("ln_b", [P, 1])
        half = sb("half", [P, 1])
        eps_c = sb("eps_c", [P, 1])
        pbias_c = sb("pbias_c", [P, 1])
        EF = E0 * F0
        W2_AT = LAG * F1
        w1_hi = sb("w1_hi", [P, EF], F16)
        w1_lo = sb("w1_lo", [P, EF], F16)
        w2_hi = sb("w2_hi", [P, EF + W2_AT], F16)
        w2_lo = sb("w2_lo", [P, EF + W2_AT], F16)
        stage_a = sb("stage_a", [P, EF])
        stage_b = sb("stage_b", [P, EF])
        pw_raw = sb("pw_raw", [P, 4, D])
        pw_hi = sb("pw_hi", [P, 4, D], F16)
        pw_lo = sb("pw_lo", [P, 4, D], F16)
        st = sb("st", [P, TB, 6])
        held = sb("held", [P, 1])
        agg = sb("agg", [P, TB, 2])
        mv = sb("mv", [P, NT, 2])
        sd = sb("sd", [P, NT])
        r0 = sb("r0", [P, NT])
        nt1 = sb("nt1", [P, NT])
        nt2 = sb("nt2", [P, NT])
        nt3 = sb("nt3", [P, NT])
        rs = sb("rs", [P, NT])
        rs2 = sb("rs2", [P, NT])
        ve = sb("ve", [P, NT])
        rp = sb("rp", [P, NT])
        unscale = sb("unscale", [P, NT])
        mhalf = sb("mhalf", [P, NT])
        xh = sb("xh", [P, 2, TB, P])
        agg8 = sb("agg8", [P, JT, 2])
        st8 = sb("st8", [P, JT, 6])
        xn = sb("xn", [P, JT, P])
        tri_bf = sb("tri_bf", [P, P], BF16)
        oh_bf = sb("oh_bf", [P, GT, E0], BF16)
        ji = sb("ji", [P, ST], mybir.dt.int32)
        jf = sb("jf", [P, ST])
        ki = sb("ki", [P, GT], mybir.dt.int32)
        kf = sb("kf", [P, GT])
        iom = sb("iom", [P, E0])
        erow_i = sb("erow_i", [P, 1], mybir.dt.int32)
        erow = sb("erow", [P, 1])
        notfirst = sb("notfirst", [P, E0, GT])
        ones8 = sb("ones8", [P, E0])
        lg0, num0, exm0, ex0, eq0 = (sb(n, [P, GT, E0]) for n in ("lg0", "num0", "exm0", "ex0", "eq0"))
        top0, first0, den0, rden0 = (sb(n, [P, GT]) for n in ("top0", "first0", "den0", "rden0"))
        tot = sb("tot", [P, E0, GT])
        cum = sb("cum", [P, E0, GT])
        rank = sb("rank", [P, E0, GT])
        big = sb("big", [P, E0, ST])
        ntile = sb("ntile", [P, E0])
        ends = sb("ends", [P, E0])
        starts = sb("starts", [P, E0])
        posf = sb("posf", [P, GT])
        texf = sb("texf", [P, G * ST])
        pos = sb("pos", [P, NT], U32)
        tex = sb("tex", [P, G * ST], mybir.dt.int32)
        gate = sb("gate", [P, NT])
        ROW_LO = 32
        b1_rows = sb("b1_rows", [P, F0], F16)
        b2_rows = sb("b2_rows", [P, D], F16)
        qk_room = sb("qk_room", [P, 4 * S], F16)
        xs_t = sb("xs_t", [P, 2, TB, P])
        s_hi = sb("s_hi", [P, TB, NI0, P], F16)
        s_lo = sb("s_lo", [P, TB, NI0, P], F16)
        ysb = sb("ysb", [P, 2, N])
        xT32 = sb("xT32", [P, 2, N])
        wA = sb("wA", [P, 2, N])
        wB = sb("wB", [P, 2, N])
        wC = sb("wC", [P, 2, N])
        wD = sb("wD", [P, 2, N])
        hT = sb("hT", [P, 2, N])
        lg = sb("lg", [P, TB, E1])
        top = sb("top", [P, TB, 8])
        idx = sb("idx", [P, TB, 8], U32)
        idf = sb("idf", [P, TB, 8])
        eqk = sb("eqk", [P, 4, TB, E1])
        ex = sb("ex", [P, TB, E1])
        exm = sb("exm", [P, TB, E1])
        num = sb("num", [P, TB, E1])
        den = sb("den", [P, TB])
        rden = sb("rden", [P, TB])
        cblk = sb("cblk", [P, TB, E1])
        comb = sb("comb", [P, NB * E1 * TB])
        cT = sb("cT", [E1, TB, P])
        h32 = sb("h32", [P, 4, N])
        h_parts = sb("h_parts", [P, 2, QS, NI1, N], F16)
        h_hi, h_lo = h_parts[:, 0], h_parts[:, 1]
        qk = qk_room
        q_hi, q_lo, k_hi, k_lo = (qk[:, n * S:(n + 1) * S] for n in range(4))
        VC = D + 2
        v_hi = sb("v_hi", [P, JT, VC], F16)
        v_lo = sb("v_lo", [P, JT, VC], F16)
        nmax = sb("nmax", [P, JT])
        dg = wD[:, 0, :].bitcast(BF16).rearrange("p (j n) -> p j n", j=JT)
        osum = sb("osum", [P, JT])
        o32 = xn
        o_parts = ysb[:].rearrange("p a n -> p (a n)").bitcast(F16).rearrange("p (a j n) -> p a j n", a=2, j=JT)
        o_hi, o_lo = o_parts[:, 0], o_parts[:, 1]

        b1_raw = qk_room[:].bitcast(F32)[:, 0:F0]
        b1_rawv = b1_raw.rearrange("e (p c) -> e c p", c=NI0)
        b1_rowsv = b1_rows[:].rearrange("e (c p) -> e c p", c=NI0)
        b2_raw = qk_room[:].bitcast(F32)[:, F0:F0 + D]
        zeros = ysb[:].rearrange("p a n -> p (a n)")
        yg = h_parts[:].rearrange("p a q c n -> p (a q c n)").bitcast(F32).rearrange("p (t d) -> p t d", d=D)
        xg = wA
        xg_hi, xg_lo = (wB[:].rearrange("p a n -> p (a n)").bitcast(F16).rearrange("p (a q n) -> p a q n", a=2, q=2)[:, k]
                        for k in range(2))
        selq = wC[:, 0, :].bitcast(F16).rearrange("p (q n) -> p q n", q=2)

        def xn_tile(t):
            if t < GT:
                return h32[:].rearrange("p a n -> p (a n)")[:, t * P:(t + 1) * P]
            t -= GT
            return xn[:, t, :] if t < JT else xh[:].rearrange("p h t n -> p (h t) n")[:, t - JT, :]

        pr_hi = stage_b[:].bitcast(F16).rearrange("p (a k n) -> p a k n", a=2, k=JT)
        pr_lo = h_parts[:].rearrange("p a q c n -> p (a q c n)").rearrange("p (a k n) -> p a k n", a=2, k=JT)

        in_x = [sem(f"in_x{b}") for b in range(B)]
        in_rows = sem("in_rows")
        rows_zero = sem("rows_zero")
        rows_hi = sem("rows_hi")
        rows_lo = sem("rows_lo")
        zeroed = sem("zeroed")
        zinit = sem("zinit")
        ve_ready = sem("ve_ready")
        pow_done = sem("pow_done")
        chain = sem("chain")
        n1 = sem("n1")
        n2 = sem("n2")
        a_t = sem("a_t")
        a_hi = sem("a_hi")
        a_lo = sem("a_lo")
        p_t = sem("p_t")
        p_t32 = sem("p_t32")
        rt_mm = sem("rt_mm")
        shifted = sem("shifted")
        r_exp = sem("r_exp")
        oh_done = sem("oh_done")
        pre_mm = sem("pre_mm")
        pos_done = sem("pos_done")
        tex_done = sem("tex_done")
        scattered = [sem(f"scattered{g}") for g in range(G)]
        gath = [sem(f"gath{g}") for g in range(G)]
        in_xs = [sem("in_xs0"), sem("in_xs1")]
        y_st = [sem("y_st0"), sem("y_st1")]
        xs_tr = sem("xs_tr")
        xg_done = sem("xg_done")
        xghi_done = sem("xghi_done")
        xglo_done = sem("xglo_done")
        sel_done = sem("sel_done")
        s1_mm = sem("s1_mm")
        shi_done = sem("shi_done")
        slo_done = sem("slo_done")
        s2_mm = sem("s2_mm")
        y_cp = sem("y_cp")
        yadd = sem("yadd")
        in_W = sem("in_W")
        in_small = sem("in_small")
        in_pw = sem("in_pw")
        in_w1 = sem("in_w1")
        in_w2 = sem("in_w2")
        x2_out = sem("x2_out")
        x2_in = sem("x2_in")
        y_out = sem("y_out")
        pool_const = sem("pool_const")
        pool_zero = sem("pool_zero")
        consts = sem("consts")
        W_split = sem("W_split")
        W_hi_done = sem("W_hi_done")
        stats = sem("stats")
        aggr = sem("aggr")
        mv_copied = sem("mv_copied")
        sqrt_done = sem("sqrt_done")
        newton = sem("newton")
        var2_done = sem("var2_done")
        normed = sem("normed")
        transposed = sem("transposed")
        hi_made = sem("hi_made")
        t32_made = sem("t32_made")
        lo_made = sem("lo_made")
        hg_done = sem("hg_done")
        gates = sem("gates")
        g_max = sem("g_max")
        bz = sem("bz")
        scanned = sem("scanned")
        back_t = sem("back_t")
        x_added = sem("x_added")
        routed_mm = sem("routed_mm")
        rt = sem("rt")
        exp_done = sem("exp_done")
        c_ready = sem("c_ready")
        cT_mm = sem("cT_mm")
        cT_cp = sem("cT_cp")
        b2_mm = sem("b2_mm")
        b2_added = sem("b2_added")
        ew_hi = sem("ew_hi")
        ew_lo = sem("ew_lo")
        g1_done = sem("g1_done")
        act_done = sem("act_done")
        hhi_done = sem("hhi_done")
        hlo_done = sem("hlo_done")
        hhi_odd = sem("hhi_odd")
        hlo_odd = sem("hlo_odd")
        g2_done = sem("g2_done")
        acc_done = sem("acc_done")
        pw_t = sem("pw_t")
        pw_hi_done = sem("pw_hi_done")
        pw_lo_done = sem("pw_lo_done")
        proj_mm = sem("proj_mm")
        proj_hi = sem("proj_hi")
        proj_lo = sem("proj_lo")
        v_const = sem("v_const")
        sn_mm = sem("sn_mm")
        max_done = sem("max_done")
        diag_done = sem("diag_done")
        st_mm = sem("st_mm")
        p_exp = sem("p_exp")
        p_hi = sem("p_hi")
        p_lo = sem("p_lo")
        pv_mm = sem("pv_mm")
        o_rcp = sem("o_rcp")
        o_norm = sem("o_norm")
        o_hi_done = sem("o_hi_done")
        o_lo_done = sem("o_lo_done")
        wo_mm = sem("wo_mm")
        x3_done = sem("x3_done")

        x_in = L0_attn_x.rearrange("b (j p) d -> b p j d", p=P)
        x2_nat = x2_dram.rearrange("b (j p) d -> b p j d", p=P)
        x2_per = x2_dram.rearrange("b (e j) d -> b e (j d)", j=JT)
        out_per = out.rearrange("b (e j) d -> b e (j d)", j=JT)

        block = ctx.enter_context(nc.Block())

        POOL_CONSTS = 13
        LAYERS = [dict(n=0, E=E0, NI=F0 // P, K=1, func=ACT.Relu), dict(n=1, E=E1, NI=F1 // P, K=4, func=ACT.Gelu)]

        def after(engine, semaphore, count):
            if not (isinstance(count, int) and count <= 0):
                engine.wait_ge(semaphore, count)

        PAIRS = QUADS // 2


        RT_STEPS = {0: ["logits", "top", "index", "shifted", "idf", "eq", "num", "den", "rden", "c"],
                    1: ["logits", "top", "index", "shifted", "idf", "eq", "sum1", "sum2", "num", "den", "rden", "c"]}

        def rt_at(n, i, step):
            per = [len(RT_STEPS[0]), len(RT_STEPS[1])]
            return i * per[n] + RT_STEPS[n].index(step) + 1

        @block.sync
        def _(sp):
            for b in range(B):
                sp.dma_start(x[:, JT * b:JT * (b + 1), :], x_in[b]).then_inc(in_x[b], 16)
                if b == 0:
                    sp.dma_start(W_raw[:], L0_attn_W).then_inc(in_W, 16)
            for dst, src in (
                    (Wr[0][:], L0_ffn_Wr), (Wr[1][:], L1_ffn_router_w),
                    (br[0][:], L0_ffn_br.rearrange("(a e) -> a e", a=1).partition_broadcast(P)),
                    (br[1][:], L1_ffn_router_b.rearrange("(a e) -> a e", a=1).partition_broadcast(P)),
                    (b1[:], L1_ffn_b1.rearrange("e (p c) -> p e c", p=P)),
                    (b2[:], L1_ffn_b2),
                    (ln_g[:], L0_ffn_ln_g.rearrange("(p a) -> p a", a=1)),
                    (ln_b[:], L0_ffn_ln_b.rearrange("(p a) -> p a", a=1))):
                sp.dma_start(dst, src).then_inc(in_small, 16)
            sp.wait_ge(rows_zero, 1)
            for row in (0, ROW_LO):
                sp.dma_start(b1_raw[row:row + E0], L0_ffn_b1).then_inc(in_rows, 16)
                sp.dma_start(b2_raw[row:row + E0], L0_ffn_b2).then_inc(in_rows, 16)
            sp.dma_start(stage_a[:].rearrange("p (e f) -> p e f", e=E0), L0_ffn_W1.rearrange("e d f -> d e f")).then_inc(in_w1, 16)
            sp.dma_start(stage_b[:].rearrange("p (e f) -> p e f", e=E0),
                         L0_ffn_W2.rearrange("e (p c) d -> p e (c d)", p=P)).then_inc(in_w2, 16)
            sp.wait_ge(zeroed, 4)
            for g in range(G):
                for k in range(ST // JT):
                    sp.dma_start(xs_dram[g].rearrange("(k p r) d -> k p (r d)", p=P, r=JT)[k], zeros).then_inc(zinit, 16)
            for n, w in enumerate((L1_attn_wq, L1_attn_wk, L1_attn_wv, L1_attn_wo)):
                sp.dma_start(pw_raw[:, n, :], w).then_inc(in_pw, 16)
            sp.wait_ge(ew_lo, 2)
            sp.dma_start(stage_a[:].rearrange("p (e f) -> p e f", e=E1), L1_ffn_w1.rearrange("e d f -> d e f")).then_inc(in_w1, 16)
            sp.dma_start(stage_b[:].rearrange("p (e f) -> p e f", e=E1),
                         L1_ffn_w2.rearrange("e (p c) d -> p e (c d)", p=P)).then_inc(in_w2, 16)
            for q in range(QUADS + 2):
                if q < QUADS:
                    g, k = q // QG, q % QG
                    if k == 0:
                        sp.wait_ge(scattered[g], 16 * GT)
                    if q >= 2:
                        sp.wait_ge(xs_tr, q - 1)
                    sp.dma_start(xs_t[:, q % 2], xs_dram[g][k * N:(k + 1) * N, :].rearrange("(t p) d -> p t d", p=P)).then_inc(in_xs[q % 2], 16)
                if q >= 2:
                    g, k = (q - 2) // QG, (q - 2) % QG
                    sp.wait_ge(y_cp, q - 1)
                    sp.dma_start(ys_dram[g][k * N:(k + 1) * N, :].rearrange("(t p) d -> p t d", p=P),
                                 ysb[:, q % 2, :].rearrange("p (t d) -> p t d", t=TB)).then_inc(y_st[q % 2], 16)
            sp.wait_ge(yadd, G)
            for b in range(B):
                sp.dma_start(x2_nat[b], x[:, JT * b:JT * (b + 1), :]).then_inc(x2_out, 16)
            sp.wait_ge(x2_out, 16 * B)
            sp.wait_ge(ew_lo, 5)
            for b in range(B):
                sp.dma_start(stage_a[:, b * S:(b + 1) * S], x2_per[b]).then_inc(x2_in, 16)
            sp.wait_ge(acc_done, NB * E1)
            for b in range(B):
                sp.dma_start(out_per[b], x[:, JT * b:JT * (b + 1), :].rearrange("p j d -> p (j d)")).then_inc(y_out, 16)
            sp.wait_ge(y_out, 16 * B)

        @block.gpsimd
        def _(pool):
            I32 = mybir.dt.int32
            nc.gpsimd.memset(ident[:], 0.0).then_inc(pool_zero, 1)
            nc.gpsimd.memset(tri_bf[:], 1.0).then_inc(pool_zero, 1)
            nc.gpsimd.memset(notfirst[:], 1.0).then_inc(pool_zero, 1)
            nc.gpsimd.memset(qk_room[:], 0.0).then_inc(rows_zero, 1)
            nc.gpsimd.iota(iota_i[:], [[1, E1]], channel_multiplier=0).then_inc(pool_zero, 1)
            nc.gpsimd.iota(ji[:], [[1, ST]], channel_multiplier=0).then_inc(pool_zero, 1)
            nc.gpsimd.iota(ki[:], [[P, GT]], channel_multiplier=0).then_inc(pool_zero, 1)
            nc.gpsimd.iota(erow_i[:], [[1, 1]], channel_multiplier=1).then_inc(pool_zero, 1)
            nc.gpsimd.memset(mhalf[:], -0.5).then_inc(pool_const, 1)
            nc.gpsimd.memset(half[:], 0.5).then_inc(pool_const, 1)
            nc.gpsimd.memset(eps_c[:], EPS).then_inc(pool_const, 1)
            nc.gpsimd.memset(pbias_c[:], PBIAS).then_inc(pool_const, 1)
            nc.gpsimd.memset(ones_bf[:], 1.0).then_inc(pool_const, 1)
            nc.gpsimd.memset(ones8[:], 1.0).then_inc(pool_const, 1)
            pool.wait_ge(pool_zero, 7)
            nc.gpsimd.affine_select(out=ident[:], in_=ident[:], compare_op=ALU.not_equal, fill=1.0, base=0,
                                    pattern=[[-1, P]], channel_multiplier=1).then_inc(pool_const, 1)
            nc.gpsimd.affine_select(out=tri_bf[:], in_=tri_bf[:], compare_op=ALU.is_gt, fill=0.0, base=0,
                                    pattern=[[1, P]], channel_multiplier=-1).then_inc(pool_const, 1)
            nc.gpsimd.memset(notfirst[:, :, 0:1], 0.0).then_inc(pool_const, 1)
            nc.gpsimd.tensor_copy(iota_e[:], iota_i[:]).then_inc(pool_const, 1)
            nc.gpsimd.tensor_copy(jf[:], ji[:]).then_inc(pool_const, 1)
            nc.gpsimd.tensor_copy(kf[:], ki[:]).then_inc(pool_const, 1)
            nc.gpsimd.tensor_copy(erow[:], erow_i[:]).then_inc(pool_const, 1)
            nc.gpsimd.memset(zeros, 0.0).then_inc(zeroed, 4)
            nc.gpsimd.memset(v_hi[:, :, D:D + 1], 1.0).then_inc(v_const, 1)
            nc.gpsimd.memset(v_hi[:, :, D + 1:VC], 0.0).then_inc(v_const, 1)
            nc.gpsimd.memset(v_lo[:, :, D:VC], 0.0).then_inc(v_const, 1)

            for n in range(3):
                pool.wait_ge(ve_ready, n + 1)
                nc.gpsimd.tensor_tensor(rp[:], ve[:], mhalf[:], ALU.pow).then_inc(pow_done, 1)
            pool.wait_ge(zinit, 16 * G * (ST // JT))
            for g in range(G):
                pool.wait_ge(pos_done, g + 1)
                for t in range(g * GT, (g + 1) * GT):
                    nc.gpsimd.indirect_dma_start(xs_dram[g], bass.IndirectOffsetOnAxis(pos[:, t:t + 1], 0), xn_tile(t),
                                                 None).then_inc(scattered[g], 16)
            for g in range(G):
                for par in range(2):
                    pool.wait_ge(y_st[par], 16 * (QG // 2) * (g + 1))
                for t in range(g * GT, (g + 1) * GT):
                    nc.gpsimd.indirect_dma_start(yg[:, t, :], None, ys_dram[g],
                                                 bass.IndirectOffsetOnAxis(pos[:, t:t + 1], 0)).then_inc(gath[g], 16)

            def low_parts(f):
                for q in range(QS):
                    s = f * QS + q
                    pool.wait_ge(hhi_odd, s + 1)
                    if not (isinstance(f, int) and s < QS):
                        pool.wait_ge(g2_done, s - QS + 1)
                    nc.gpsimd.tensor_tensor(h_lo[:, q, 1, :], h32[:, (q % 2) * 2 + 1, :], h_hi[:, q, 1, :],
                                            ALU.subtract).then_inc(hlo_odd, 1)
            low_parts(0)
            with pool.Fori(1, STEPS // QS) as f:
                low_parts(f)

        @block.scalar
        def _(act):
            act.wait_ge(pool_const, POOL_CONSTS)
            act.wait_ge(in_W, 16)
            nc.scalar.mul(W_hi[:], W_raw[:], WS).then_inc(W_hi_done, 1)

            def sqrt_of_variance(k):
                act.wait_ge(mv_copied, (k + 1) * NB)
                nc.scalar.activation(sd[:], mv[:, :, 1], ACT.Sqrt, bias=eps_c[:]).then_inc(sqrt_done, 1)

            for i in range(-3, NB):
                j = i + 1
                if 0 <= j < NB:
                    h = j % 2
                    act.wait_ge(hg_done, j + 1)
                    after(act, scanned, j - 1)
                    hidden, gates_in = ps[:, 4 + 2 * h, :], ps[:, 5 + 2 * h, :]
                    nc.scalar.activation(wA[:, h, :], gates_in, ACT.Sigmoid, scale=-1.0 / WS)
                    nc.scalar.activation(wB[:, h, :], gates_in, ACT.Sigmoid, scale=1.0 / WS)
                    nc.scalar.activation(wC[:, h, :], hidden, ACT.Sigmoid, scale=1.0 / WS)
                    nc.scalar.activation(wD[:, h, :], hidden, ACT.Identity, scale=1.0 / WS, bias=half[:]).then_inc(gates, 1)
                j = i + 3
                if j < NB:
                    act.wait_ge(a_t, j + 1)
                    nc.scalar.copy(xT_hi[:, j * N:(j + 1) * N], ps[:, j % 2, :]).then_inc(a_hi, 1)

            for i in range(NB):
                act.wait_ge(p_t, i + 1)
                after(act, rt_mm, i - 1)
                nc.scalar.copy(xT32[:, i % 2, :], ps[:, i % 2, :]).then_inc(p_t32, 1)
            for g in range(G):
                act.wait_ge(shifted, g + 1)
                nc.scalar.activation(ex0[:], exm0[:], ACT.Exp).then_inc(r_exp, 1)

            def features(q, par):
                act.wait_ge(xs_tr, q + 1)
                after(act, xglo_done, q - 1)
                nc.scalar.activation(xg[:, par, :], ps[:, par, :], ACT.Identity, scale=ln_g[:], bias=ln_b[:]).then_inc(xg_done, 1)
                act.wait_ge(xg_done, q + 1)
                after(act, s1_mm, (q - 1) * TB)
                nc.scalar.copy(xg_hi[:, par], xg[:, par, :]).then_inc(xghi_done, 1)

            def output(q, par):
                act.wait_ge(s2_mm, (q + 1) * TB)
                after(act, y_st[par], 16 * (q // 2) if isinstance(q, int) else (q - par) * 8)
                nc.scalar.copy(ysb[:, par, :], ps[:, 6 + par, :]).then_inc(y_cp, 1)

            def quad(q, par, next_features=True):
                for t in range(TB):
                    if t == LAG:
                        if not (isinstance(q, int) and q == 0):
                            output(q - 1, 1 - par)
                        if next_features:
                            features(q + 1, 1 - par)
                    act.wait_ge(s1_mm, q * TB + t + 1)
                    after(act, s2_mm, q * TB + t - TB + 1)
                    nc.scalar.activation(s_hi[:, t].rearrange("p c n -> p (c n)"), ps[:, 2 + t, :],
                                         ACT.Relu).then_inc(shi_done, 1)

            def split_first(n, E, NI):
                w1v = stage_a[:].rearrange("d (e p c) -> d e c p", e=E, c=NI)
                act.wait_ge(in_w1, 16 * (n + 1))
                nc.scalar.mul(w1_hi[:].rearrange("d (e c p) -> d e c p", e=E, c=NI), w1v, WS).then_inc(ew_hi, 1)
                act.wait_ge(in_w2, 16 * (n + 1))
                nc.scalar.mul(w2_hi[:, W2_AT:], stage_b[:], WS).then_inc(ew_hi, 1)
                if n == 1:
                    nc.scalar.mul(w2_hi[:, 0:W2_AT], stage_b[:, EF - W2_AT:EF], WS).then_inc(ew_hi, 1)

            split_first(0, E0, NI0)
            act.wait_ge(in_rows, 64)
            nc.scalar.mul(b1_rowsv, b1_rawv, WS).then_inc(rows_hi, 1)
            nc.scalar.mul(b2_rows[:], b2_raw, WS * WS).then_inc(rows_hi, 1)
            features(0, 0)
            quad(0, 0)
            quad(1, 1)
            with act.Fori(1, PAIRS - 1) as p:
                for par in range(2):
                    quad(p * 2 + par, par)
            quad(QUADS - 2, 0)
            quad(QUADS - 1, 1, next_features=False)
            output(QUADS - 1, 1)

            def experts():
                n, E = 1, E1
                with act.Fori(0, B) as b:
                    for h in range(2):
                        i = b * 2 + h
                        act.wait_ge(transposed, NB + i + 1)
                        act.wait_ge(routed_mm, b * 2)
                        nc.scalar.copy(xT32[:, h, :], ps[:, h, :]).then_inc(t32_made, 1)
                        nc.scalar.copy(xT_hi[:, ds(i * N, N)], ps[:, h, :]).then_inc(hi_made, 1)
                        act.wait_ge(rt, rt_at(n, i, "shifted"))
                        nc.scalar.activation(ex[:, :, 0:E], exm[:, :, 0:E], ACT.Exp).then_inc(exp_done, 1)
                        act.wait_ge(cT_mm, i + 1)
                        nc.scalar.copy(cT[0:E, :, :], ps[0:E, 4 + h, :].rearrange("e (t p) -> e t p", t=TB)).then_inc(cT_cp, 1)

                def steps(f):
                    for q in range(QS):
                        s = f * QS + q
                        for ic in range(NI1):
                            slot = (q % 2) * 2 + ic
                            act.wait_ge(g1_done, s * NI1 + ic + 1)
                            if not (isinstance(f, int) and s < 2):
                                act.wait_ge((hlo_done, hlo_odd)[ic], s - 1)
                            e = (f % (E1 // QS)) * QS + q
                            nc.scalar.activation(h32[:, slot, :], ps[:, slot, :], ACT.Gelu, scale=1.0 / WS,
                                                 bias=b1[:, ds(e, 1), ic]).then_inc(act_done, 1)
                        act.wait_ge(act_done, s * NI1 + 1)
                        if not (isinstance(f, int) and s < QS):
                            act.wait_ge(g2_done, s - QS + 1)
                        nc.scalar.copy(h_hi[:, q, 0, :], h32[:, (q % 2) * 2, :]).then_inc(hhi_done, 1)

                steps(0)
                with act.Fori(1, STEPS // QS) as f:
                    steps(f)

            act.wait_ge(s2_mm, QUADS * TB)
            split_first(1, E1, NI1)
            act.wait_ge(pw_t, 1)
            nc.scalar.mul(pw_hi[:].rearrange("p n d -> p (n d)"), ps[:, 2, :], WS).then_inc(pw_hi_done, 1)
            sqrt_of_variance(0)
            with act.Fori(0, B) as b:
                for h in range(2):
                    i = b * 2 + h
                    act.wait_ge(transposed, i + 1)
                    nc.scalar.copy(xT_hi[:, ds(i * N, N)], ps[:, h, :]).then_inc(hi_made, 1)
            with act.Fori(0, B) as b:
                for m in range(6):
                    act.wait_ge(proj_mm, b * 6 + m + 1)
                    bank, hc = ps[:, 6 + m % 2, :], m % 2
                    if m == 0:
                        act.wait_ge(st_mm, b * 16)
                    if m == 4:
                        act.wait_ge(pv_mm, b * JT)
                    if m < 4:
                        dst = (q_hi if m < 2 else k_hi)[:, hc * N:(hc + 1) * N]
                        sc = SCORE / WS if m < 2 else 1.0 / WS
                        nc.scalar.mul(dst, bank, sc).then_inc(proj_hi, 1)
                    else:
                        nc.scalar.mul(v_hi[:, hc * TB:(hc + 1) * TB, 0:D], bank.rearrange("p (t d) -> p t d", t=TB),
                                      1.0 / WS).then_inc(proj_hi, 1)
                for qh in range(2):
                    for kt in range(JT):
                        u = b * 16 + qh * JT + kt
                        k = kt % 2
                        act.wait_ge(st_mm, u + 1)
                        if qh == 0 and kt < 2:
                            act.wait_ge(p_lo, b * 16)
                        else:
                            act.wait_ge(p_lo, u - 1)
                        nc.scalar.activation(wA[:, k, :], ps[:, 4 + k, :], ACT.Exp, bias=pbias_c[:]).then_inc(p_exp, 1)
                act.wait_ge(o_norm, b * JT + JT)
                act.wait_ge(wo_mm, b)
                nc.scalar.copy(o_hi, o32[:]).then_inc(o_hi_done, 1)

            sqrt_of_variance(1)
            experts()

        @block.vector
        def _(dve):
            dve.wait_ge(W_hi_done, 1)
            nc.vector.scalar_tensor_tensor(out=W_lo[:], in0=W_raw[:], scalar=WS, in1=W_hi[:], op0=ALU.mult,
                                           op1=ALU.subtract).then_inc(W_split, 1)
            nwt = [0]

            def wait_alone(semaphore, value):
                dve.wait_ge(semaphore, value)
                nc.vector.memset(held[:], 0.0)

            def small(ins):
                nwt[0] += 1
                ins.then_inc(newton, 1)
                dve.wait_ge(newton, nwt[0])

            def statistics(k):
                with dve.Fori(0, NB) as i:
                    for t in range(TB):
                        nc.vector.bn_stats(st[:, t, :], x[:, ds(i * TB + t, 1), :].rearrange("p a d -> p (a d)")).then_inc(stats, 1)
                    dve.wait_ge(mv_copied, k * NB + i)
                    wait_alone(stats, (k * NB + i + 1) * TB)
                    for t in range(TB):
                        nc.vector.bn_aggr(agg[:, t, :], st[:, t, :]).then_inc(aggr, 1)
                    dve.wait_ge(aggr, (k * NB + i + 1) * TB)
                    nc.vector.tensor_copy(mv[:, ds(i * TB, TB), :], agg[:]).then_inc(mv_copied, 1)
                dve.wait_ge(mv_copied, (k + 1) * NB)

            def rsqrt(k, var, res):
                dve.wait_ge(sqrt_done, k + 1)
                small(nc.vector.reciprocal(r0[:], sd[:]))
                small(nc.vector.tensor_tensor(nt1[:], r0[:], r0[:], ALU.mult))
                small(nc.vector.scalar_tensor_tensor(out=nt2[:], in0=var, scalar=EPS, in1=nt1[:], op0=ALU.add, op1=ALU.mult))
                small(nc.vector.tensor_scalar(nt3[:], nt2[:], -0.5, 1.5, ALU.mult, ALU.add))
                small(nc.vector.tensor_tensor(res, r0[:], nt3[:], ALU.mult))

            def normalise(k, i, h, scale):
                for t in range(TB):
                    tile = i * TB + t
                    ins = nc.vector.tensor_scalar(xh[:, h, t, :], x[:, ds(tile, 1), :].rearrange("p a d -> p (a d)"),
                                                  mv[:, ds(tile, 1), 0], scale[:, ds(tile, 1)], ALU.subtract, ALU.mult)
                ins.then_inc(normed, 1)

            def xh_free(k, b):
                dve.wait_ge(transposed, k * NB + b * 2)

            def split_experts(n, E, NI):
                FE = NI * P
                w1v = stage_a[:].rearrange("d (e p c) -> d e c p", e=E, c=NI)
                dve.wait_ge(ew_hi, 2 if n == 0 else 5)
                for e in range(E):
                    sl = slice(e * FE, (e + 1) * FE)
                    ins = nc.vector.scalar_tensor_tensor(
                        out=w1_lo[:, sl].rearrange("d (c p) -> d c p", c=NI), in0=w1v[:, e], scalar=WS,
                        in1=w1_hi[:, sl].rearrange("d (c p) -> d c p", c=NI), op0=ALU.mult, op1=ALU.subtract)
                ins.then_inc(ew_lo, 1)
                nc.vector.scalar_tensor_tensor(out=w2_lo[:, W2_AT:], in0=stage_b[:], scalar=WS, in1=w2_hi[:, W2_AT:],
                                               op0=ALU.mult, op1=ALU.subtract).then_inc(ew_lo, 1)
                if n == 1:
                    nc.vector.scalar_tensor_tensor(out=w2_lo[:, 0:W2_AT], in0=stage_b[:, EF - W2_AT:EF], scalar=WS,
                                                   in1=w2_hi[:, 0:W2_AT], op0=ALU.mult, op1=ALU.subtract).then_inc(ew_lo, 1)

            made = [0]

            def link(ins):
                made[0] += 1
                ins.then_inc(chain, 1)
                dve.wait_ge(chain, made[0])

            TT, TS, STT = nc.vector.tensor_tensor, nc.vector.tensor_scalar, nc.vector.scalar_tensor_tensor

            def token_statistics(b):
                for t in range(JT):
                    ins = nc.vector.bn_stats(st8[:, t, :], x[:, b * JT + t, :])
                link(ins)
                for t in range(JT):
                    ins = nc.vector.bn_aggr(mv[:, b * JT + t, :], st8[:, t, :])
                link(ins)

            def refined(res, n):
                dve.wait_ge(pow_done, n)
                link(TT(nt1[:], rp[:], rp[:], ALU.mult))
                link(TT(nt2[:], ve[:], nt1[:], ALU.mult))
                link(TS(nt3[:], nt2[:], -0.5, 1.5, ALU.mult, ALU.add))
                link(TT(res, rp[:], nt3[:], ALU.mult))

            def normal(dst, t, scale):
                return TS(dst, x[:, t, :], mv[:, t, 0:1], scale[:, t:t + 1], ALU.subtract, ALU.mult)

            for b in range(B):
                dve.wait_ge(in_x[b], 16)
                token_statistics(b)
            TS(ve[:], mv[:, :, 1], EPS, None, ALU.add).then_inc(ve_ready, 1)
            refined(rs[:], 1)
            for i in range(-3, NB + 1):
                if 0 <= i < NB:
                    h = i % 2
                    dve.wait_ge(gates, i + 1)
                    link(TT(wC[:, h, :], wC[:, h, :], wD[:, h, :], ALU.max))
                    link(TT(wB[:, h, :], wB[:, h, :], wC[:, h, :], ALU.mult))
                    after(dve, back_t, i - 1)
                    nc.vector.tensor_tensor_scan(hT[:, h, :], wA[:, h, :], wB[:, h, :], 0.0 if h == 0 else hT[:, 0, N - 1:N],
                                                 ALU.mult, ALU.add).then_inc(scanned, 1)
                    dve.wait_ge(scanned, i + 1)
                j = i + 2
                if 0 <= j < NB:
                    cols = slice(j * N, (j + 1) * N)
                    dve.wait_ge(a_hi, j + 1)
                    TT(xT_lo[:, cols], ps[:, j % 2, :], xT_hi[:, cols], ALU.subtract).then_inc(a_lo, 1)
                j = i + 3
                if j < NB:
                    after(dve, a_t, j - 1)
                    for t in range(TB):
                        ins = normal(xh[:, j % 2, t, :], j * TB + t, rs)
                    ins.then_inc(n1, 1)
                j = i - 1
                if j >= 0:
                    dve.wait_ge(back_t, j + 1)
                    xb = x[:, j * TB:(j + 1) * TB, :].rearrange("p t d -> p (t d)")
                    TT(xb, ps[:, 2 + j % 2, :], xb, ALU.add).then_inc(x_added, 1)
                    dve.wait_ge(x_added, j + 1)
                    if j % 2 == 1:
                        token_statistics(j // 2)

            TS(ve[:], mv[:, :, 1], EPS, None, ALU.add).then_inc(ve_ready, 1)
            refined(rs[:], 2)
            link(TT(nt1[:], rs[:], rs[:], ALU.mult))
            link(TT(nt2[:], mv[:, :, 1], nt1[:], ALU.mult))
            TS(ve[:], nt2[:], EPS, None, ALU.add).then_inc(ve_ready, 1)
            refined(rs2[:], 3)
            link(TT(unscale[:], ve[:], rs2[:], ALU.mult))
            link(TT(rs[:], rs[:], rs2[:], ALU.mult))
            dve.wait_ge(a_t, NB)
            for i in range(NB):
                for t in range(i * TB, (i + 1) * TB):
                    ins = normal(xn_tile(t), t, rs)
                ins.then_inc(n2, 1)

            def over(ap, n, like):
                return ap.unsqueeze(2).to_broadcast([P, n, like])

            def route(g):
                tiles = slice(g * GT, (g + 1) * GT)
                dve.wait_ge(rt_mm, GB * (g + 1))
                raw = ps[:, 2 + g, 0:GT * E0].rearrange("p (t e) -> p t e", t=GT)
                link(TT(num0[:], raw, over(unscale[:, tiles], GT, E0), ALU.mult))
                link(TT(lg0[:], num0[:], br[0][:].unsqueeze(1).to_broadcast([P, GT, E0]), ALU.add))
                link(nc.vector.tensor_reduce(top0[:], lg0[:], AX_X, ALU.max))
                TT(exm0[:], lg0[:], over(top0[:], GT, E0), ALU.subtract).then_inc(shifted, 1)
                link(TT(eq0[:], lg0[:], over(top0[:], GT, E0), ALU.is_equal))
                iob = iom[:].unsqueeze(1).to_broadcast([P, GT, E0])
                link(TT(num0[:], eq0[:], iob, ALU.mult))
                link(nc.vector.tensor_reduce(first0[:], num0[:], AX_X, ALU.min))
                TT(oh_bf[:], iob, over(first0[:], GT, E0), ALU.is_equal).then_inc(oh_done, 1)
                dve.wait_ge(oh_done, g + 1)
                dve.wait_ge(r_exp, g + 1)
                link(nc.vector.tensor_reduce(den0[:], ex0[:], AX_X, ALU.add))
                link(nc.vector.reciprocal(rden0[:], den0[:]))
                link(TS(gate[:, tiles], rden0[:], 1.0 / (WS * WS), None, ALU.mult))

            def sort_positions(g):
                dve.wait_ge(pre_mm, g + 1)
                before = ps[:, 2 + g, 128:128 + GT * E0].rearrange("p (t e) -> p e t", t=GT)
                total = ps[:, 2 + g, 256:256 + GT * E0].rearrange("p (t e) -> p e t", t=GT)
                flat = lambda a: a.rearrange("p e t -> p (e t)")
                link(nc.vector.tensor_copy(tot[:], total))
                link(nc.vector.tensor_tensor_scan(flat(cum[:]), flat(notfirst[:]), flat(tot[:]), 0.0, ALU.mult, ALU.add))
                link(TT(big[:, :, 0:GT], cum[:, :, GT - 1:GT].to_broadcast([P, E0, GT]),
                        kf[:].unsqueeze(1).to_broadcast([P, E0, GT]), ALU.is_gt))
                link(nc.vector.tensor_reduce(ntile[:], big[:, :, 0:GT], AX_X, ALU.add))
                link(nc.vector.tensor_tensor_scan(ends[:], ones8[:], ntile[:], 0.0, ALU.mult, ALU.add))
                link(TT(starts[:], ends[:], ntile[:], ALU.subtract))
                link(TT(rank[:], cum[:], tot[:], ALU.subtract))
                link(TT(rank[:], before, rank[:], ALU.add))
                link(STT(out=rank[:], in0=starts[:].unsqueeze(2).to_broadcast([P, E0, GT]), scalar=float(P), in1=rank[:],
                         op0=ALU.mult, op1=ALU.add))
                link(TT(cum[:].rearrange("p e t -> p t e"), oh_bf[:], rank[:].rearrange("p e t -> p t e"), ALU.mult))
                link(nc.vector.tensor_reduce(posf[:], cum[:].rearrange("p e t -> p t e"), AX_X, ALU.add))
                nc.vector.tensor_copy(pos[:, g * GT:(g + 1) * GT], posf[:]).then_inc(pos_done, 1)
                link(TT(big[:].rearrange("p e j -> p j e"), ends[:].unsqueeze(1).to_broadcast([P, ST, E0]),
                        jf[:].unsqueeze(2).to_broadcast([P, ST, E0]), ALU.is_le))
                tiles = slice(g * ST, (g + 1) * ST)
                link(nc.vector.tensor_reduce(texf[:, tiles], big[:].rearrange("p e j -> p j e"), AX_X, ALU.add))
                link(TS(texf[:, tiles], texf[:, tiles], float(E0 - 1), None, ALU.min))
                nc.vector.tensor_copy(tex[:, tiles], texf[:, tiles]).then_inc(tex_done, 1)

            dve.wait_ge(in_small, 16 * 8)
            dve.wait_ge(pool_const, POOL_CONSTS)
            link(TS(iom[:], iota_e[:, 0:E0], float(E0), None, ALU.subtract))
            link(TS(erow[ROW_LO:ROW_LO + E0, :], erow[ROW_LO:ROW_LO + E0, :], float(ROW_LO), None, ALU.subtract))
            for g in range(G):
                route(g)
                sort_positions(g)
            split_experts(0, E0, NI0)
            dve.wait_ge(rows_hi, 2)
            low = slice(ROW_LO, ROW_LO + E0)
            STT(out=b1_rowsv[low], in0=b1_rawv[low], scalar=WS, in1=b1_rowsv[low], op0=ALU.mult,
                op1=ALU.subtract).then_inc(rows_lo, 1)
            STT(out=b2_rows[low], in0=b2_raw[low], scalar=WS * WS, in1=b2_rows[low], op0=ALU.mult,
                op1=ALU.subtract).then_inc(rows_lo, 1)

            def features(q, par):
                dve.wait_ge(xghi_done, q + 1)
                TT(xg_lo[:, par], xg[:, par, :], xg_hi[:, par], ALU.subtract).then_inc(xglo_done, 1)
                after(dve, s2_mm, (q - 1) * TB)
                TS(selq[:, par].rearrange("p (t n) -> p t n", t=TB), over(texf[:, ds(q * TB, TB)], TB, P), erow[:], None,
                   ALU.is_equal).then_inc(sel_done, 1)

            def quad(q, par, next_features=True):
                for t in range(TB):
                    if t == LAG and next_features:
                        features(q + 1, 1 - par)
                    dve.wait_ge(shi_done, q * TB + t + 1)
                    STT(out=s_lo[:, t].rearrange("p c n -> p (c n)"), in0=ps[:, 2 + t, :], scalar=0.0,
                        in1=s_hi[:, t].rearrange("p c n -> p (c n)"), op0=ALU.max, op1=ALU.subtract).then_inc(slo_done, 1)

            dve.wait_ge(tex_done, G)
            features(0, 0)
            quad(0, 0)
            quad(1, 1)
            with dve.Fori(1, PAIRS - 1) as p:
                for par in range(2):
                    quad(p * 2 + par, par)
            quad(QUADS - 2, 0)
            quad(QUADS - 1, 1, next_features=False)
            for g in range(G):
                dve.wait_ge(gath[g], 16 * GT)
                for t in range(g * GT, (g + 1) * GT):
                    ins = STT(out=x[:, t, :], in0=yg[:, t, :], scalar=gate[:, t:t + 1], in1=x[:, t, :], op0=ALU.mult, op1=ALU.add)
                ins.then_inc(yadd, 1)
            dve.wait_ge(yadd, G)

            def bc(ap, n):
                return ap.unsqueeze(2).to_broadcast([P, TB, n])

            def prepare(L, k, scale):
                n, E, K = L["n"], L["E"], L["K"]

                def step(ins, i, name):
                    ins.then_inc(rt, 1)
                    (wait_alone if name in ("logits", "top") else dve.wait_ge)(rt, rt_at(n, i, name))

                with dve.Fori(0, B) as b:
                    xh_free(k, b)
                    for h in range(2):
                        normalise(k, b * 2 + h, h, scale)
                    for h in range(2):
                        i = b * 2 + h
                        dve.wait_ge(hi_made, k * NB + i + 1)
                        src = ps[:, h, :]
                        nc.vector.tensor_tensor(xT_lo[:, ds(i * N, N)], src, xT_hi[:, ds(i * N, N)],
                                                ALU.subtract).then_inc(lo_made, 1)
                        dve.wait_ge(routed_mm, i + 1)
                        lgE = lg[:, :, 0:E]
                        raw = ps[:, 2 + h, 0:TB * E].rearrange("p (t e) -> p t e", t=TB)
                        brb = br[n][:].unsqueeze(1).to_broadcast([P, TB, E])
                        step(nc.vector.tensor_tensor(lgE, raw, brb, ALU.add), i, "logits")
                        for t in range(TB):
                            ins = nc.vector.max(top[:, t, :], lg[:, t, 0:E])
                        step(ins, i, "top")
                        for t in range(TB):
                            ins = nc.vector.max_index(idx[:, t, :], top[:, t, :], lg[:, t, 0:E])
                        step(ins, i, "index")
                        step(nc.vector.tensor_tensor(exm[:, :, 0:E], lgE, bc(top[:, :, 0], E), ALU.subtract), i, "shifted")
                        step(nc.vector.tensor_copy(idf[:], idx[:]), i, "idf")
                        iob = iota_e[:, 0:E].unsqueeze(1).to_broadcast([P, TB, E])
                        for kk in range(K):
                            ins = nc.vector.tensor_tensor(eqk[:, kk, :, 0:E], iob, bc(idf[:, :, kk], E), ALU.is_equal)
                        step(ins, i, "eq")
                        if K == 4:
                            step(nc.vector.tensor_tensor(eqk[:, 0:2, :, 0:E], eqk[:, 0:2, :, 0:E], eqk[:, 2:4, :, 0:E], ALU.add), i, "sum1")
                            step(nc.vector.tensor_tensor(eqk[:, 0, :, 0:E], eqk[:, 0, :, 0:E], eqk[:, 1, :, 0:E], ALU.add), i, "sum2")
                        dve.wait_ge(exp_done, i + 1)
                        step(nc.vector.tensor_tensor(num[:, :, 0:E], ex[:, :, 0:E], eqk[:, 0, :, 0:E], ALU.mult), i, "num")
                        step(nc.vector.tensor_reduce(den[:], (ex if K == 1 else num)[:, :, 0:E], AX_X, ALU.add), i, "den")
                        step(nc.vector.reciprocal(rden[:], den[:]), i, "rden")
                        dve.wait_ge(cT_mm, i)
                        step(nc.vector.tensor_tensor(cblk[:, :, 0:E], num[:, :, 0:E], bc(rden[:], E), ALU.mult), i, "c")
                        cv = comb[:, ds(i * (E * TB), E * TB)].rearrange("p (e t) -> p t e", t=TB)
                        nc.vector.tensor_scalar(cv, cblk[:, :, 0:E], 1.0 / WS, None, ALU.mult).then_inc(c_ready, 1)
                        dve.wait_ge(b2_mm, i + 1)
                        xb = x[:, ds(i * TB, TB), :].rearrange("p t d -> p (t d)")
                        nc.vector.tensor_tensor(xb, ps[:, 6 + h, :], xb, ALU.add).then_inc(b2_added, 1)
                dve.wait_ge(b2_added, NB)

            def experts():
                def accumulate(s, q):
                    dve.wait_ge(g2_done, s + 1)
                    if not (isinstance(s, int) and s == 0):
                        dve.wait_ge(acc_done, s)
                    for t in range(TB):
                        tile = (s // E1) * TB + t
                        xt = x[:, ds(tile, 1), :].rearrange("p a d -> p (a d)")
                        ins = nc.vector.scalar_tensor_tensor(out=xt, in0=ps[:, 4 + q, t * P:(t + 1) * P],
                                                             scalar=comb[:, ds(s * TB + t, 1)], in1=xt,
                                                             op0=ALU.mult, op1=ALU.add)
                    ins.then_inc(acc_done, 1)

                def steps(f):
                    for q in range(QS):
                        s = f * QS + q
                        dve.wait_ge(act_done, s * NI1 + 2)
                        if not (isinstance(f, int) and s < QS):
                            dve.wait_ge(g2_done, s - QS + 1)
                        nc.vector.tensor_copy(h_hi[:, q, 1, :], h32[:, (q % 2) * 2 + 1, :]).then_inc(hhi_odd, 1)
                        dve.wait_ge(hhi_done, s + 1)
                        nc.vector.tensor_tensor(h_lo[:, q, 0, :], h32[:, (q % 2) * 2, :], h_hi[:, q, 0, :],
                                                ALU.subtract).then_inc(hlo_done, 1)
                        if not (isinstance(f, int) and s < LAG):
                            accumulate(s - LAG, q % 2)

                steps(0)
                with dve.Fori(1, STEPS // QS) as f:
                    steps(f)
                for s in range(STEPS - LAG, STEPS):
                    accumulate(s, s % 2)
                dve.wait_ge(acc_done, STEPS)

            split_experts(1, E1, NI1)
            dve.wait_ge(pw_hi_done, 1)
            nc.vector.scalar_tensor_tensor(out=pw_lo[:].rearrange("p n d -> p (n d)"), in0=ps[:, 2, :], scalar=WS,
                                           in1=pw_hi[:].rearrange("p n d -> p (n d)"), op0=ALU.mult,
                                           op1=ALU.subtract).then_inc(pw_lo_done, 1)
            statistics(0)
            rsqrt(0, mv[:, :, 1], rs[:])
            with dve.Fori(0, B) as b:
                xh_free(0, b)
                for h in range(2):
                    normalise(0, b * 2 + h, h, rs)
                for h in range(2):
                    i = b * 2 + h
                    dve.wait_ge(hi_made, i + 1)
                    nc.vector.tensor_tensor(xT_lo[:, ds(i * N, N)], ps[:, h, :], xT_hi[:, ds(i * N, N)],
                                            ALU.subtract).then_inc(lo_made, 1)
            dve.wait_ge(x2_in, 16 * B)
            dve.wait_ge(v_const, 3)
            with dve.Fori(0, B) as b:
                for m in range(6):
                    dve.wait_ge(proj_hi, b * 6 + m + 1)
                    bank, hc = ps[:, 6 + m % 2, :], m % 2
                    if m < 4:
                        cols = slice(hc * N, (hc + 1) * N)
                        hi, lo = (q_hi, q_lo) if m < 2 else (k_hi, k_lo)
                        hi, lo = hi[:, cols], lo[:, cols]
                    else:
                        bank = bank.rearrange("p (t d) -> p t d", t=TB)
                        hi, lo = v_hi[:, hc * TB:(hc + 1) * TB, 0:D], v_lo[:, hc * TB:(hc + 1) * TB, 0:D]
                    nc.vector.scalar_tensor_tensor(out=lo, in0=bank, scalar=SCORE / WS if m < 2 else 1.0 / WS, in1=hi,
                                                   op0=ALU.mult, op1=ALU.subtract).then_inc(proj_lo, 1)
                dve.wait_ge(st_mm, b * 2 * JT)
                for qt in range(JT):
                    dve.wait_ge(sn_mm, b * JT + qt + 1)
                    pair = 2 * (qt % 2)
                    nc.vector.tensor_reduce(nmax[:, qt:qt + 1], ps[:, pair:pair + 2, :].rearrange("p a n -> p (a n)"),
                                            AX_X, ALU.max).then_inc(max_done, 1)
                    dve.wait_ge(max_done, b * JT + qt + 1)
                    nc.vector.tensor_scalar(dg[:, qt, :], ident[:], nmax[:, qt:qt + 1], -1.0, ALU.mult,
                                            ALU.mult).then_inc(diag_done, 1)
                dve.wait_ge(pv_mm, b * JT)
                for qh in range(2):
                    for kt in range(JT):
                        u = b * 2 * JT + qh * JT + kt
                        dve.wait_ge(p_exp, u + 1)
                        nc.vector.tensor_copy(pr_hi[:, qh, kt, :], wA[:, kt % 2, :]).then_inc(p_hi, 1)
                        dve.wait_ge(p_hi, u + 1)
                        nc.vector.tensor_tensor(pr_lo[:, qh, kt, :], wA[:, kt % 2, :], pr_hi[:, qh, kt, :],
                                                ALU.subtract).then_inc(p_lo, 1)
                dve.wait_ge(o_hi_done, b)
                for qt in range(JT):
                    dve.wait_ge(pv_mm, b * JT + qt + 1)
                    nc.vector.reciprocal(osum[:, qt:qt + 1], ps[:, 6 + qt % 2, D:D + 1]).then_inc(o_rcp, 1)
                    dve.wait_ge(o_rcp, b * JT + qt + 1)
                    nc.vector.tensor_scalar(o32[:, qt, :], ps[:, 6 + qt % 2, 0:D], osum[:, qt:qt + 1], None,
                                            ALU.mult).then_inc(o_norm, 1)
                dve.wait_ge(o_hi_done, b + 1)
                nc.vector.tensor_tensor(o_lo, o32[:], o_hi, ALU.subtract).then_inc(o_lo_done, 1)
                dve.wait_ge(wo_mm, b + 1)
                nc.vector.scalar_tensor_tensor(out=x[:, ds(b * JT, JT), :].rearrange("p j d -> p (j d)"),
                                               in0=ps[:, 0:2, :].rearrange("p a n -> p (a n)"), scalar=1.0 / WS,
                                               in1=stage_a[:, ds(b * S, S)], op0=ALU.mult, op1=ALU.add).then_inc(x3_done, 1)

            dve.wait_ge(x3_done, B)
            statistics(1)
            rsqrt(1, mv[:, :, 1], rs[:])
            prepare(LAYERS[1], 1, rs)
            experts()

        @block.tensor
        def _(pe):
            mm = nc.tensor.matmul

            def product(out, a, b, last=True):
                mm(out, a[0], b[0], start=True, stop=False)
                mm(out, a[0], b[1], start=False, stop=False)
                return mm(out, a[1], b[0], start=False, stop=last)

            def transposes(k, b):
                for h in range(2):
                    i = b * 2 + h
                    pe.wait_ge(normed, k * NB + i + 1)
                    pe.wait_ge(lo_made, k * NB + b * 2)
                    for t in range(TB):
                        ins = nc.tensor.transpose(ps[:, h, t * P:(t + 1) * P], xh[:, h, t, :], ident[:])
                    ins.then_inc(transposed, 1)

            pe.wait_ge(pool_const, POOL_CONSTS)
            def turn(src, bank, counted):
                for t in range(TB):
                    ins = nc.tensor.transpose(ps[:, bank, t * P:(t + 1) * P], src[t], ident[:])
                ins.then_inc(counted, 1)

            pe.wait_ge(W_split, 1)
            for i in range(-3, NB):
                if i >= 0:
                    pe.wait_ge(scanned, i + 1)
                    after(pe, x_added, i - 1)
                    turn([hT[:, i % 2, t * P:(t + 1) * P] for t in range(TB)], 2 + i % 2, back_t)
                j = i + 2
                if 0 <= j < NB:
                    pe.wait_ge(a_lo, j + 1)
                    after(pe, gates, j - 1)
                    xi = (xT_hi[:, j * N:(j + 1) * N], xT_lo[:, j * N:(j + 1) * N])
                    bank = 4 + 2 * (j % 2)
                    product(ps[:, bank, :], (W_hi[:, 0:D], W_lo[:, 0:D]), xi)
                    product(ps[:, bank + 1, :], (W_hi[:, D:2 * D], W_lo[:, D:2 * D]), xi).then_inc(hg_done, 1)
                j = i + 3
                if j < NB:
                    pe.wait_ge(n1, j + 1)
                    after(pe, a_lo, j - 1)
                    turn([xh[:, j % 2, t, :] for t in range(TB)], j % 2, a_t)

            pe.wait_ge(in_small, 16 * 8)
            pe.wait_ge(x_added, NB)
            for i in range(NB + 1):
                if i < NB:
                    pe.wait_ge(n2, i + 1)
                    after(pe, p_t32, i - 1)
                    turn([xn_tile(i * TB + t) for t in range(TB)], i % 2, p_t)
                j = i - 1
                if j >= 0:
                    pe.wait_ge(p_t32, j + 1)
                    for t in range(TB):
                        k = (j % GB) * TB + t
                        ins = mm(ps[:, 2 + j // GB, k * E0:(k + 1) * E0], xT32[:, j % 2, t * P:(t + 1) * P], Wr[0][:],
                                 start=True, stop=True)
                    ins.then_inc(rt_mm, 1)
            for g in range(G):
                pe.wait_ge(oh_done, g + 1)
                oh = oh_bf[:].rearrange("p t e -> p (t e)")
                mm(ps[:, 2 + g, 128:128 + GT * E0], tri_bf[:], oh, start=True, stop=True)
                mm(ps[:, 2 + g, 256:256 + GT * E0], ones_bf[:], oh, start=True, stop=True).then_inc(pre_mm, 1)

            def turned(q, par):
                pe.wait_ge(in_xs[par], 16 * (q // 2 + 1) if isinstance(q, int) else (q - par) * 8 + 16)
                after(pe, xg_done, q - 1)
                turn([xs_t[:, par, t, :] for t in range(TB)], par, xs_tr)

            def expert_of(q, t):
                return pe.value_load(tex[0:1, ds(q * TB + t, 1)], min_val=0, max_val=E0 - 1)

            def hidden(q, t, par, expert):
                if t == 0:
                    pe.wait_ge(xglo_done, q + 1)
                    pe.wait_ge(sel_done, q + 1)
                after(pe, slo_done, q * TB + t - TB + 1)
                tok = slice(t * P, (t + 1) * P)
                for c in range(NI0):
                    w = ds((expert * NI0 + c) * P, P)
                    o = ps[:, 2 + t, c * P:(c + 1) * P]
                    product(o, (w1_hi[:, w], w1_lo[:, w]), (xg_hi[:, par, tok], xg_lo[:, par, tok]), last=False)
                    ins = mm(o, b1_rows[:, c * P:(c + 1) * P], selq[:, par, tok], start=False, stop=True)
                ins.then_inc(s1_mm, 1)

            def output(q, t, par, expert):
                pe.wait_ge(slo_done, q * TB + t + 1)
                if t == 0:
                    after(pe, y_cp, q - 1)
                tok = slice(t * P, (t + 1) * P)
                o = ps[:, 6 + par, tok]
                mm(o, selq[:, par, tok], b2_rows[:], start=True, stop=False)
                for c in range(NI0):
                    w = ds((expert * NI0 + c) * P + W2_AT, P)
                    mm(o, s_hi[:, t, c], w2_hi[:, w], start=False, stop=False)
                    mm(o, s_hi[:, t, c], w2_lo[:, w], start=False, stop=False)
                    ins = mm(o, s_lo[:, t, c], w2_hi[:, w], start=False, stop=c == NI0 - 1)
                ins.then_inc(s2_mm, 1)

            def quad(q, par, next_quad=True):
                experts_of = [expert_of(q, t) for t in range(TB)]
                for t in range(TB):
                    if t == 1 and next_quad:
                        turned(q + 1, 1 - par)
                    hidden(q, t, par, experts_of[t])
                    if t >= LAG:
                        output(q, t - LAG, par, experts_of[t - LAG])
                    elif not (isinstance(q, int) and q == 0):
                        output(q - 1, t + TB - LAG, 1 - par, expert_of(q - 1, t + TB - LAG))

            pe.wait_ge(rows_lo, 2)
            pe.wait_ge(tex_done, G)
            pe.wait_ge(ew_lo, 2)
            turned(0, 0)
            quad(0, 0)
            quad(1, 1)
            with pe.Fori(1, PAIRS - 1) as p:
                for par in range(2):
                    quad(p * 2 + par, par)
            quad(QUADS - 2, 0)
            quad(QUADS - 1, 1, next_quad=False)
            for t in range(TB - LAG, TB):
                output(QUADS - 1, t, 1, expert_of(QUADS - 1, t))

            def prepare(L, k):
                n, E = L["n"], L["E"]
                with pe.Fori(0, B) as b:
                    transposes(k, b)
                    for h in range(2):
                        i = b * 2 + h
                        pe.wait_ge(t32_made, i + 1)
                        for t in range(TB):
                            ins = mm(ps[:, 2 + h, t * E:(t + 1) * E], xT32[:, h, t * P:(t + 1) * P], Wr[n][:],
                                     start=True, stop=True)
                        ins.then_inc(routed_mm, 1)
                        pe.wait_ge(c_ready, i + 1)
                        for t in range(TB):
                            ins = nc.tensor.transpose(ps[0:E, 4 + h, t * P:(t + 1) * P], cblk[:, t, 0:E], ident[:])
                        ins.then_inc(cT_mm, 1)
                        pe.wait_ge(cT_cp, i + 1)
                        pe.wait_ge(b2_added, b * 2)
                        for t in range(TB):
                            ins = mm(ps[:, 6 + h, t * P:(t + 1) * P], cT[0:E, t, :], b2[:], start=True, stop=True)
                        ins.then_inc(b2_mm, 1)

            def experts():
                def first(f, q):
                    s = f * QS + q
                    blk = f // (E1 // QS)
                    e = (f % (E1 // QS)) * QS + q
                    xi = (xT_hi[:, ds(blk * N, N)], xT_lo[:, ds(blk * N, N)])
                    for ic in range(NI1):
                        if not (isinstance(f, int) and s < 2):
                            pe.wait_ge(act_done, s * NI1 + ic - 3)
                        w = ds((e * NI1 + ic) * P, P)
                        product(ps[:, (q % 2) * 2 + ic, :], (w1_hi[:, w], w1_lo[:, w]), xi).then_inc(g1_done, 1)

                def second(f, q):
                    s = f * QS + q - LAG
                    e = (f % (E1 // QS)) * QS + q
                    buf = (q - LAG) % QS
                    pe.wait_ge(hlo_done, s + 1)
                    pe.wait_ge(hlo_odd, s + 1)
                    if not (isinstance(s, int) and s < 2):
                        pe.wait_ge(acc_done, s - 1)
                    for t in range(TB):
                        tok = slice(t * P, (t + 1) * P)
                        o = ps[:, 4 + q % 2, tok]
                        for ic in range(NI1):
                            w = ds((e * NI1 + ic) * P, P)
                            mm(o, h_hi[:, buf, ic, tok], w2_hi[:, w], start=ic == 0, stop=False)
                            mm(o, h_hi[:, buf, ic, tok], w2_lo[:, w], start=False, stop=False)
                            ins = mm(o, h_lo[:, buf, ic, tok], w2_hi[:, w], start=False, stop=ic == NI1 - 1)
                    ins.then_inc(g2_done, 1)

                pe.wait_ge(b2_added, NB)
                for q in range(QS):
                    first(0, q)
                    if q >= LAG:
                        second(0, q)
                with pe.Fori(1, STEPS // QS) as f:
                    for q in range(QS):
                        first(f, q)
                        second(f, q)
                for q in range(LAG):
                    second(STEPS // QS, q)

            pe.wait_ge(in_pw, 16 * 4)
            pe.wait_ge(yadd, G)
            for n in range(4):
                ins = nc.tensor.transpose(ps[:, 2, n * P:(n + 1) * P], pw_raw[:, n, :], ident[:])
            ins.then_inc(pw_t, 1)
            with pe.Fori(0, B) as b:
                transposes(0, b)
            pe.wait_ge(pw_lo_done, 1)
            pe.wait_ge(lo_made, NB)
            with pe.Fori(0, B) as b:
                for m in range(6):
                    hc = m % 2
                    bank = ps[:, 6 + hc, :]
                    if m < 2:
                        pe.wait_ge(o_norm, b * JT)
                    else:
                        pe.wait_ge(proj_lo, b * 6 + m - 1)
                    if m < 4:
                        cols = ds(b * S + hc * N, N)
                        w = m // 2
                        ins = product(bank, (pw_hi[:, w, :], pw_lo[:, w, :]), (xT_hi[:, cols], xT_lo[:, cols]))
                    else:
                        for t in range(TB):
                            cols = ds(b * S + (hc * TB + t) * P, P)
                            ins = product(bank[:, t * P:(t + 1) * P], (xT_hi[:, cols], xT_lo[:, cols]),
                                          (pw_hi[:, 2, :], pw_lo[:, 2, :]))
                    ins.then_inc(proj_mm, 1)
                pe.wait_ge(proj_hi, b * 6 + 4)
                pe.wait_ge(x3_done, b)
                for qt in range(JT):
                    if qt >= 2:
                        pe.wait_ge(max_done, b * JT + qt - 1)
                    for h in range(2):
                        ins = mm(ps[:, 2 * (qt % 2) + h, :], q_hi[:, qt * P:(qt + 1) * P], k_hi[:, h * N:(h + 1) * N],
                                 start=True, stop=True)
                    ins.then_inc(sn_mm, 1)
                pe.wait_ge(proj_lo, b * 6 + 4)
                for qh in range(2):
                    pe.wait_ge(diag_done, b * JT + (qh + 1) * TB)
                    for kt in range(JT):
                        u = b * 2 * JT + qh * JT + kt
                        if qh == 0 and kt < 2:
                            pe.wait_ge(p_exp, b * 2 * JT)
                        else:
                            pe.wait_ge(p_exp, u - 1)
                        o = ps[:, 4 + kt % 2, :]
                        kk, qq = slice(kt * P, (kt + 1) * P), slice(qh * N, (qh + 1) * N)
                        product(o, (k_hi[:, kk], k_lo[:, kk]), (q_hi[:, qq], q_lo[:, qq]), last=False)
                        mm(o, ones_bf[:], dg[:, qh * TB:(qh + 1) * TB, :].rearrange("p t q -> p (t q)"), start=False,
                           stop=True).then_inc(st_mm, 1)
                pe.wait_ge(proj_lo, b * 6 + 6)
                for qt in range(JT):
                    qh, t = qt // TB, qt % TB
                    if t == 0:
                        pe.wait_ge(p_lo, b * 2 * JT + (qh + 1) * JT)
                    if qt >= 2:
                        pe.wait_ge(o_norm, b * JT + qt - 1)
                    o = ps[:, 6 + qt % 2, 0:VC]
                    for kt in range(JT):
                        ph, pl = pr_hi[:, qh, kt, t * P:(t + 1) * P], pr_lo[:, qh, kt, t * P:(t + 1) * P]
                        mm(o, ph, v_hi[:, kt, :], start=kt == 0, stop=False)
                        mm(o, ph, v_lo[:, kt, :], start=False, stop=False)
                        ins = mm(o, pl, v_hi[:, kt, :], start=False, stop=kt == JT - 1)
                    ins.then_inc(pv_mm, 1)
                pe.wait_ge(o_lo_done, b + 1)
                for j in range(JT):
                    ins = product(ps[:, j // TB, (j % TB) * P:(j % TB + 1) * P], (o_hi[:, j, :], o_lo[:, j, :]),
                                  (pw_hi[:, 3, :], pw_lo[:, 3, :]))
                ins.then_inc(wo_mm, 1)

            prepare(LAYERS[1], 1)
            pe.wait_ge(ew_lo, 5)
            experts()


_INS = ["L0_attn_x", "L0_attn_W", "L0_ffn_Wr", "L0_ffn_br", "L0_ffn_ln_g", "L0_ffn_ln_b", "L0_ffn_W1", "L0_ffn_b1",
        "L0_ffn_W2", "L0_ffn_b2", "L1_attn_wq", "L1_attn_wk", "L1_attn_wv", "L1_attn_wo", "L1_ffn_router_w",
        "L1_ffn_router_b", "L1_ffn_w1", "L1_ffn_b1", "L1_ffn_w2", "L1_ffn_b2"]
_OUTS = [((4, 1024, 128), "float32")]


def kernel(**inputs):
    import numpy as _np
    import concourse.bacc as _bacc
    from concourse import mybir as _mybir
    from concourse.bass_utils import run_bass_kernel_spmd as _run

    nc = _bacc.Bacc("TRN2", target_bir_lowering=False, num_devices=1)
    arrays, args = {}, []
    for name in _INS:
        a = _np.ascontiguousarray(inputs[name])
        arrays[f"in_{name}_dram"] = a
        args.append(nc.dram_tensor(f"in_{name}_dram", a.shape, _mybir.dt.from_np(a.dtype), kind="ExternalInput").ap())
    for i, (shape, dtype) in enumerate(_OUTS):
        dt = _mybir.dt.from_np(_np.dtype(dtype))
        args.append(nc.dram_tensor(f"out_{i}_dram", shape, dt, kind="ExternalOutput").ap())
    build(nc, *args)
    r = _run(nc, [arrays], core_ids=[0])
    return r.results[0]["out_0_dram"]
```

```python
from contextlib import ExitStack

import concourse.bass as bass
from concourse import mybir

ALU = mybir.AluOpType
ACT = mybir.ActivationFunctionType
F32 = mybir.dt.float32
F16 = mybir.dt.float16
BF16 = mybir.dt.bfloat16
U32 = mybir.dt.uint32
AX_X = mybir.AxisListType.X
ds = bass.ds

P = 128
EPS = 1e-5
WS = 8.0
PBIAS = 6.931471805599453


def build(nc, L0_attn_x, L0_attn_W, L0_ffn_Wr, L0_ffn_br, L0_ffn_ln_g, L0_ffn_ln_b, L0_ffn_W1, L0_ffn_b1,
          L0_ffn_W2, L0_ffn_b2, L1_attn_wq, L1_attn_wk, L1_attn_wv, L1_attn_wo, L1_ffn_router_w,
          L1_ffn_router_b, L1_ffn_w1, L1_ffn_b1, L1_ffn_w2, L1_ffn_b2, out):
    B, S, D = L0_attn_x.shape
    NT = B * S // P
    TB = 4
    N = TB * P
    NB = NT // TB
    JT = S // P
    E0, _, F0 = L0_ffn_W1.shape
    E1, _, F1 = L1_ffn_w1.shape
    SCORE = 1.0 / float((D / 16) ** 0.5)
    assert D == P and NB == 2 * B and JT == 2 * TB and E0 * F0 == E1 * F1 and E0 == JT

    G = 2
    GT = NT // G
    GB = GT // TB
    QG = -(-(GT + E0 - 1) // TB)
    ST = QG * TB
    QUADS = G * QG
    NI0 = F0 // P
    NI1 = F1 // P
    LAG = 2
    QS = 4
    STEPS = NB * E1

    xs_dram = [nc.dram_tensor(f"xs_scratch{g}", (ST * P, D), F32, kind="Internal").ap() for g in range(G)]
    ys_dram = [nc.dram_tensor(f"ys_scratch{g}", (ST * P, D), F32, kind="Internal").ap() for g in range(G)]
    x2_dram = nc.dram_tensor("x2_scratch", (B, S, D), F32, kind="Internal").ap()

    with ExitStack() as ctx:
        def sb(name, shape, dt=F32):
            return ctx.enter_context(nc.sbuf_tensor(name, shape, dt))

        def sem(name):
            return ctx.enter_context(nc.semaphore(name))

        ps = ctx.enter_context(nc.psum_tensor("ps", [P, 8, N], F32))

        x = sb("x", [P, NT, D])
        xT_hi = sb("xT_hi", [P, NT * P], F16)
        xT_lo = sb("xT_lo", [P, NT * P], F16)
        ident = sb("ident", [P, P])
        ident16 = sb("ident16", [P, P], F16)
        ones_bf = sb("ones_bf", [P, P], BF16)
        iota_i = sb("iota_i", [P, E1], mybir.dt.int32)
        iota_e = sb("iota_e", [P, E1])
        W_raw = sb("W_raw", [P, 2 * D])
        W_hi = sb("W_hi", [P, 2 * D], F16)
        W_lo = sb("W_lo", [P, 2 * D], F16)
        Wr = [sb("Wr0", [P, E0]), sb("Wr1", [P, E1])]
        br = [sb("br0", [P, E0]), sb("br1", [P, E1])]
        b1 = sb("b1", [P, E1, F1 // P])
        b2 = sb("b2", [E1, D])
        ln_g = sb("ln_g", [P, 1])
        ln_b = sb("ln_b", [P, 1])
        half = sb("half", [P, 1])
        eps_c = sb("eps_c", [P, 1])
        pbias_c = sb("pbias_c", [P, 1])
        EF = E0 * F0
        W2_AT = LAG * NI1
        w1_hi = sb("w1_hi", [P, EF], F16)
        w1_lo = sb("w1_lo", [P, EF], F16)
        w2_parts = sb("w2_parts", [P, W2_AT + EF // P, 2, P], F16)
        w2_hi, w2_lo = w2_parts[:, :, 0], w2_parts[:, :, 1]
        stage_a = sb("stage_a", [P, EF])
        stage_b = sb("stage_b", [P, EF])
        pw_raw = sb("pw_raw", [P, 4, D])
        pw_hi = sb("pw_hi", [P, 4, D], F16)
        pw_lo = sb("pw_lo", [P, 4, D], F16)
        held = sb("held", [P, 1])
        mv = sb("mv", [P, NT, 2])
        sd = sb("sd", [P, NT])
        r0 = sb("r0", [P, NT])
        nt1 = sb("nt1", [P, NT])
        nt2 = sb("nt2", [P, NT])
        nt3 = sb("nt3", [P, NT])
        rs = sb("rs", [P, NT])
        rs2 = sb("rs2", [P, NT])
        nmr = sb("nmr", [P, NT])
        ve = sb("ve", [P, NT])
        unscale = sb("unscale", [P, NT])
        xh = sb("xh", [P, 2, TB, P])
        agg8 = sb("agg8", [P, JT, 2])
        st8 = sb("st8", [P, JT, 6])
        xn = sb("xn", [P, JT, P])
        tri_bf = sb("tri_bf", [P, P], BF16)
        oh_bf = sb("oh_bf", [P, GT, E0], BF16)
        ji = sb("ji", [P, ST], mybir.dt.int32)
        jf = sb("jf", [P, ST])
        ki = sb("ki", [P, GT], mybir.dt.int32)
        kf = sb("kf", [P, GT])
        iom = sb("iom", [P, E0])
        erow_i = sb("erow_i", [P, 1], mybir.dt.int32)
        erow = sb("erow", [P, 1])
        notfirst = sb("notfirst", [P, E0, GT])
        ones8 = sb("ones8", [P, E0])
        lg0, num0, exm0, ex0, eq0 = (sb(n, [P, GT, E0]) for n in ("lg0", "num0", "exm0", "ex0", "eq0"))
        top0, first0, den0, rden0 = (sb(n, [P, GT]) for n in ("top0", "first0", "den0", "rden0"))
        tot = sb("tot", [P, E0, GT])
        cum = sb("cum", [P, E0, GT])
        rank = sb("rank", [P, E0, GT])
        big = sb("big", [P, E0, ST])
        ntile = sb("ntile", [P, E0])
        ends = sb("ends", [P, E0])
        starts = sb("starts", [P, E0])
        posf = sb("posf", [P, GT])
        texf = sb("texf", [P, G * ST])
        pos = sb("pos", [P, NT], U32)
        tex = sb("tex", [P, G * ST], mybir.dt.int32)
        gate = sb("gate", [P, NT])
        ROW_LO = 32
        b1_rows = sb("b1_rows", [P, F0], F16)
        b2_rows = sb("b2_rows", [P, D], F16)
        qk_room = sb("qk_room", [P, 4 * S], F16)
        xs_t = sb("xs_t", [P, 2, TB, P])
        s_hi = sb("s_hi", [P, TB, NI0, P], F16)
        s_lo = sb("s_lo", [P, TB, NI0, P], F16)
        ysb = sb("ysb", [P, 2, N])
        xT32 = sb("xT32", [P, 2, N])
        wA = sb("wA", [P, 2, N])
        wB = sb("wB", [P, 2, N])
        wC = sb("wC", [P, 2, N])
        wD = sb("wD", [P, 2, N])
        hT = sb("hT", [P, 2, N])
        top = sb("top", [P, GT, 8])
        idx = sb("idx", [P, GT, 8], U32)
        idf = sb("idf", [P, GT, 8])
        den = sb("den", [P, GT])
        rden = sb("rden", [P, GT])
        lg, exm, ex, num = (wC[:].rearrange("p a n -> p (a n)")[:, k * GT * E1:(k + 1) * GT * E1].rearrange("p (t e) -> p t e", e=E1)
                            for k in range(4))
        cw = wD[:].rearrange("p a n -> p (a n)")[:, 0:2 * GT * E1].rearrange("p (g t e) -> p g t e", g=2, e=E1)
        cw_parts = wA[:, 0, :].bitcast(F16).rearrange("p (g a t e) -> p g a t e", g=2, a=2, e=E1)
        eqk = hT[:].rearrange("p a n -> p (a n)")[:, 0:4 * GT * E1].rearrange("p (k t e) -> p k t e", k=4, e=E1)
        comb = sb("comb", [P, NB * E1 * TB])
        cT = xT32
        h32 = sb("h32", [P, 4, N])
        h_parts = sb("h_parts", [P, 2, QS, NI1, N], F16)
        h_hi, h_lo = h_parts[:, 0], h_parts[:, 1]
        qk = qk_room
        q_hi, q_lo, k_hi, k_lo = (qk[:, n * S:(n + 1) * S] for n in range(4))
        VC = D + 2
        v_hi = sb("v_hi", [P, JT, VC], F16)
        v_lo = sb("v_lo", [P, JT, VC], F16)
        nmax = sb("nmax", [P, JT])
        dg = wD[:, 0, :].bitcast(BF16).rearrange("p (j n) -> p j n", j=JT)
        osum = sb("osum", [P, JT])
        o32 = xn
        o_parts = ysb[:].rearrange("p a n -> p (a n)").bitcast(F16).rearrange("p (a j n) -> p a j n", a=2, j=JT)
        o_hi, o_lo = o_parts[:, 0], o_parts[:, 1]

        b1_raw = qk_room[:].bitcast(F32)[:, 0:F0]
        b1_rawv = b1_raw.rearrange("e (p c) -> e c p", c=NI0)
        b1_rowsv = b1_rows[:].rearrange("e (c p) -> e c p", c=NI0)
        b2_raw = qk_room[:].bitcast(F32)[:, F0:F0 + D]
        raw_w2 = stage_b[:].rearrange("p (k n) -> p k n", n=P)
        zeros = ysb[:].rearrange("p a n -> p (a n)")
        yg = h_parts[:].rearrange("p a q c n -> p (a q c n)").bitcast(F32).rearrange("p (t d) -> p t d", d=D)
        xg = wA
        prob32 = [wA[:, 0, :], wA[:, 1, :], wB[:, 0, :], wB[:, 1, :]]
        xg_hi, xg_lo = (wB[:].rearrange("p a n -> p (a n)").bitcast(F16).rearrange("p (a q n) -> p a q n", a=2, q=2)[:, k]
                        for k in range(2))
        selq = wC[:, 0, :].bitcast(F16).rearrange("p (q n) -> p q n", q=2)

        def xn_tile(t):
            if t < GT:
                return h32[:].rearrange("p a n -> p (a n)")[:, t * P:(t + 1) * P]
            t -= GT
            return xn[:, t, :] if t < JT else xh[:].rearrange("p h t n -> p (h t) n")[:, t - JT, :]

        pr_hi = stage_b[:].bitcast(F16).rearrange("p (a k n) -> p a k n", a=2, k=JT)
        pr_lo = h_parts[:].rearrange("p a q c n -> p (a q c n)").rearrange("p (a k n) -> p a k n", a=2, k=JT)

        in_x = [sem(f"in_x{b}") for b in range(B)]
        in_rows = sem("in_rows")
        rows_zero = sem("rows_zero")
        rows_hi = sem("rows_hi")
        rows_lo = sem("rows_lo")
        zeroed = sem("zeroed")
        zinit = sem("zinit")
        ve_ready = sem("ve_ready")
        chain = sem("chain")
        n1 = sem("n1")
        n2 = sem("n2")
        a_t = sem("a_t")
        a_hi = sem("a_hi")
        a_lo = sem("a_lo")
        p_t = sem("p_t")
        p_t32 = sem("p_t32")
        rt_mm = sem("rt_mm")
        shifted = sem("shifted")
        r_exp = sem("r_exp")
        oh_done = sem("oh_done")
        pre_mm = sem("pre_mm")
        pos_done = sem("pos_done")
        tex_done = sem("tex_done")
        scattered = [sem(f"scattered{g}") for g in range(G)]
        gath = [sem(f"gath{b}") for b in range(B)]
        in_xs = [sem("in_xs0"), sem("in_xs1")]
        y_st = [sem("y_st0"), sem("y_st1")]
        xs_tr = sem("xs_tr")
        xg_done = sem("xg_done")
        xghi_done = sem("xghi_done")
        xglo_done = sem("xglo_done")
        sel_done = sem("sel_done")
        s1_mm = sem("s1_mm")
        shi_done = sem("shi_done")
        slo_done = sem("slo_done")
        s2_mm = sem("s2_mm")
        y_low = sem("y_low")
        y_cp = sem("y_cp")
        yadd = sem("yadd")
        in_W = sem("in_W")
        in_small = sem("in_small")
        in_pw = sem("in_pw")
        in_w1 = sem("in_w1")
        in_w2 = sem("in_w2")
        x2_out = sem("x2_out")
        x2_in = sem("x2_in")
        y_out = sem("y_out")
        pool_const = sem("pool_const")
        pool_zero = sem("pool_zero")
        W_split = sem("W_split")
        W_hi_done = sem("W_hi_done")
        mv_ready = sem("mv_ready")
        scale_ready = sem("scale_ready")
        stats = sem("stats")
        aggr = sem("aggr")
        mv_copied = sem("mv_copied")
        sqrt_done = sem("sqrt_done")
        normed = sem("normed")
        transposed = sem("transposed")
        hi_made = sem("hi_made")
        t32_made = sem("t32_made")
        lo_made = sem("lo_made")
        hg_done = sem("hg_done")
        gates = sem("gates")
        scanned = sem("scanned")
        back_t = sem("back_t")
        x_added = sem("x_added")
        routed_mm = sem("routed_mm")
        shifted1 = sem("shifted1")
        exp_done = sem("exp_done")
        c_ready = sem("c_ready")
        cT_mm = sem("cT_mm")
        cT_cp = sem("cT_cp")
        b2_mm = sem("b2_mm")
        b2_added = sem("b2_added")
        ew_hi = sem("ew_hi")
        ew_lo = sem("ew_lo")
        ew_scaled = sem("ew_scaled")
        g1_done = sem("g1_done")
        act_done = sem("act_done")
        hhi_done = sem("hhi_done")
        hlo_done = sem("hlo_done")
        hhi_odd = sem("hhi_odd")
        hlo_odd = sem("hlo_odd")
        g2_done = sem("g2_done")
        acc_done = sem("acc_done")
        pw_t = sem("pw_t")
        pw_hi_done = sem("pw_hi_done")
        pw_lo_done = sem("pw_lo_done")
        qk_mm = sem("qk_mm")
        qk_hi = sem("qk_hi")
        qk_lo = sem("qk_lo")
        v_const = sem("v_const")
        sn_mm = sem("sn_mm")
        max_done = sem("max_done")
        diag_done = sem("diag_done")
        st_mm = sem("st_mm")
        p_exp = sem("p_exp")
        p_hi_even = sem("p_hi_even")
        p_hi_odd = sem("p_hi_odd")
        vp_mm = sem("vp_mm")
        vp_hi = sem("vp_hi")
        vp_lo = sem("vp_lo")
        p_lo_even = sem("p_lo_even")
        p_lo_odd = sem("p_lo_odd")
        pv_mm = sem("pv_mm")
        o_rcp = sem("o_rcp")
        o_norm = sem("o_norm")
        o_hi_done = sem("o_hi_done")
        o_lo_done = sem("o_lo_done")
        wo_mm = sem("wo_mm")
        x3_done = sem("x3_done")

        x_in = L0_attn_x.rearrange("b (j p) d -> b p j d", p=P)
        x2_nat = x2_dram.rearrange("b (j p) d -> b p j d", p=P)
        x2_per = x2_dram.rearrange("b (e j) d -> b e (j d)", j=JT)
        out_per = out.rearrange("b (e j) d -> b e (j d)", j=JT)

        block = ctx.enter_context(nc.Block())

        POOL_CONSTS = 13
        assert NB == E0 and G == 2
        AHEAD = GB + 1

        def turn_bank(i, k):
            return i if k == 0 else i % 4

        def qk_bank(m):
            return 4 + m if m < 2 else m

        def b2_bank(i):
            return i if i < GB else 4 + i % 2

        def after(engine, semaphore, count):
            if not (isinstance(count, int) and count <= 0):
                engine.wait_ge(semaphore, count)

        PAIRS = QUADS // 2
        assert 2 * (PAIRS - 2) * N == EF

        @block.sync
        def _(sp):
            for b in range(B):
                sp.dma_start(x[:, JT * b:JT * (b + 1), :], x_in[b]).then_inc(in_x[b], 16)
                if b == 0:
                    sp.dma_start(W_raw[:], L0_attn_W).then_inc(in_W, 16)
            for dst, src in (
                    (Wr[0][:], L0_ffn_Wr), (Wr[1][:], L1_ffn_router_w),
                    (br[0][:], L0_ffn_br.rearrange("(a e) -> a e", a=1).partition_broadcast(P)),
                    (br[1][:], L1_ffn_router_b.rearrange("(a e) -> a e", a=1).partition_broadcast(P)),
                    (b1[:], L1_ffn_b1.rearrange("e (p c) -> p e c", p=P)),
                    (b2[:], L1_ffn_b2),
                    (ln_g[:], L0_ffn_ln_g.rearrange("(p a) -> p a", a=1)),
                    (ln_b[:], L0_ffn_ln_b.rearrange("(p a) -> p a", a=1))):
                sp.dma_start(dst, src).then_inc(in_small, 16)
            sp.wait_ge(rows_zero, 1)
            for row in (0, ROW_LO):
                sp.dma_start(b1_raw[row:row + E0], L0_ffn_b1).then_inc(in_rows, 16)
                sp.dma_start(b2_raw[row:row + E0], L0_ffn_b2).then_inc(in_rows, 16)
            sp.dma_start(stage_a[:].rearrange("p (e f) -> p e f", e=E0), L0_ffn_W1.rearrange("e d f -> d e f")).then_inc(in_w1, 16)
            sp.dma_start(stage_b[:].rearrange("p (e f) -> p e f", e=E0),
                         L0_ffn_W2.rearrange("e (p c) d -> p e (c d)", p=P)).then_inc(in_w2, 16)
            sp.wait_ge(zeroed, 4)
            for g in range(G):
                for k in range(ST // JT):
                    sp.dma_start(xs_dram[g].rearrange("(k p r) d -> k p (r d)", p=P, r=JT)[k], zeros).then_inc(zinit, 16)
            for n, w in enumerate((L1_attn_wq, L1_attn_wk, L1_attn_wv, L1_attn_wo)):
                sp.dma_start(pw_raw[:, n, :], w).then_inc(in_pw, 16)
            for q in range(QUADS + 2):
                if q < QUADS:
                    g, k = q // QG, q % QG
                    if k == 0:
                        sp.wait_ge(scattered[g], 16 * GT)
                    if q >= 2:
                        sp.wait_ge(xs_tr, q - 1)
                    sp.dma_start(xs_t[:, q % 2], xs_dram[g][k * N:(k + 1) * N, :].rearrange("(t p) d -> p t d", p=P)).then_inc(in_xs[q % 2], 16)
                if q == 1:
                    sp.wait_ge(ew_lo, E0)
                    sp.dma_start(stage_a[:].rearrange("p (e f) -> p e f", e=E1), L1_ffn_w1.rearrange("e d f -> d e f")).then_inc(in_w1, 16)
                    sp.dma_start(stage_b[:].rearrange("p (e f) -> p e f", e=E1),
                                 L1_ffn_w2.rearrange("e (p c) d -> p e (c d)", p=P)).then_inc(in_w2, 16)
                if q >= 2:
                    g, k = (q - 2) // QG, (q - 2) % QG
                    sp.wait_ge(y_cp, 2 * (q - 1))
                    sp.dma_start(ys_dram[g][k * N:(k + 1) * N, :].rearrange("(t p) d -> p t d", p=P),
                                 ysb[:, q % 2, :].rearrange("p (t d) -> p t d", t=TB)).then_inc(y_st[q % 2], 16)
            sp.wait_ge(yadd, B)
            for b in range(B):
                sp.dma_start(x2_nat[b], x[:, JT * b:JT * (b + 1), :]).then_inc(x2_out, 16)
            sp.wait_ge(x2_out, 16 * B)
            sp.wait_ge(ew_lo, E0 + 3)
            for b in range(B):
                sp.dma_start(stage_a[:, b * S:(b + 1) * S], x2_per[b]).then_inc(x2_in, 16)
            for i in range(NB):
                sp.wait_ge(acc_done, (i + 1) * E1)
                sp.dma_start(out_per[i // 2][:, (i % 2) * N:(i % 2 + 1) * N],
                             x[:, TB * i:TB * (i + 1), :].rearrange("p j d -> p (j d)")).then_inc(y_out, 16)
            sp.wait_ge(y_out, 16 * NB)

        @block.gpsimd
        def _(pool):
            I32 = mybir.dt.int32
            nc.gpsimd.memset(ident[:], 0.0).then_inc(pool_zero, 1)
            nc.gpsimd.memset(tri_bf[:], 1.0).then_inc(pool_zero, 1)
            nc.gpsimd.memset(notfirst[:], 1.0).then_inc(pool_zero, 1)
            nc.gpsimd.memset(qk_room[:], 0.0).then_inc(rows_zero, 1)
            nc.gpsimd.iota(iota_i[:], [[1, E1]], channel_multiplier=0).then_inc(pool_zero, 1)
            nc.gpsimd.iota(ji[:], [[1, ST]], channel_multiplier=0).then_inc(pool_zero, 1)
            nc.gpsimd.iota(ki[:], [[P, GT]], channel_multiplier=0).then_inc(pool_zero, 1)
            nc.gpsimd.iota(erow_i[:], [[1, 1]], channel_multiplier=1).then_inc(pool_zero, 1)
            nc.gpsimd.memset(half[:], 0.5).then_inc(pool_const, 1)
            nc.gpsimd.memset(eps_c[:], EPS).then_inc(pool_const, 1)
            nc.gpsimd.memset(pbias_c[:], PBIAS).then_inc(pool_const, 1)
            nc.gpsimd.memset(ones_bf[:], 1.0).then_inc(pool_const, 1)
            nc.gpsimd.memset(ones8[:], 1.0).then_inc(pool_const, 1)
            pool.wait_ge(pool_zero, 7)
            nc.gpsimd.affine_select(out=ident[:], in_=ident[:], compare_op=ALU.not_equal, fill=1.0, base=0,
                                    pattern=[[-1, P]], channel_multiplier=1).then_inc(pool_const, 1)
            nc.gpsimd.affine_select(out=tri_bf[:], in_=tri_bf[:], compare_op=ALU.is_gt, fill=0.0, base=0,
                                    pattern=[[1, P]], channel_multiplier=-1).then_inc(pool_const, 1)
            nc.gpsimd.memset(notfirst[:, :, 0:1], 0.0).then_inc(pool_const, 1)
            nc.gpsimd.tensor_copy(iota_e[:], iota_i[:]).then_inc(pool_const, 1)
            nc.gpsimd.tensor_copy(jf[:], ji[:]).then_inc(pool_const, 1)
            nc.gpsimd.tensor_copy(kf[:], ki[:]).then_inc(pool_const, 1)
            nc.gpsimd.tensor_copy(erow[:], erow_i[:]).then_inc(pool_const, 1)
            pool.wait_ge(pool_const, 12)
            nc.gpsimd.tensor_copy(ident16[:], ident[:]).then_inc(pool_const, 1)
            nc.gpsimd.memset(zeros, 0.0).then_inc(zeroed, 4)
            nc.gpsimd.memset(v_hi[:, :, D:D + 1], 1.0).then_inc(v_const, 1)
            nc.gpsimd.memset(v_hi[:, :, D + 1:VC], 0.0).then_inc(v_const, 1)
            nc.gpsimd.memset(v_lo[:, :, D:VC], 0.0).then_inc(v_const, 1)

            pool.wait_ge(zinit, 16 * G * (ST // JT))
            for g in range(G):
                pool.wait_ge(pos_done, g + 1)
                for t in range(g * GT, (g + 1) * GT):
                    nc.gpsimd.indirect_dma_start(xs_dram[g], bass.IndirectOffsetOnAxis(pos[:, t:t + 1], 0), xn_tile(t),
                                                 None).then_inc(scattered[g], 16)
            for g in range(G):
                for par in range(2):
                    pool.wait_ge(y_st[par], 16 * (QG // 2) * (g + 1))
                for t in range(g * GT, (g + 1) * GT):
                    nc.gpsimd.indirect_dma_start(yg[:, t, :], None, ys_dram[g],
                                                 bass.IndirectOffsetOnAxis(pos[:, t:t + 1], 0)).then_inc(gath[t // JT], 16)

            pool.wait_ge(ew_hi, E0 + 3)
            nc.gpsimd.tensor_tensor(w1_lo[:].rearrange("d (e c p) -> d e c p", e=E1, c=NI1),
                                    stage_a[:].rearrange("d (e p c) -> d e c p", e=E1, c=NI1),
                                    w1_hi[:].rearrange("d (e c p) -> d e c p", e=E1, c=NI1), ALU.subtract).then_inc(ew_lo, 1)
            nc.gpsimd.tensor_tensor(w2_lo[:, W2_AT:], raw_w2, w2_hi[:, W2_AT:], ALU.subtract).then_inc(ew_lo, 1)
            nc.gpsimd.tensor_tensor(w2_lo[:, 0:W2_AT], raw_w2[:, EF // P - W2_AT:], w2_hi[:, 0:W2_AT],
                                    ALU.subtract).then_inc(ew_lo, 1)

            def probabilities(b):
                for v in range(1, 2 * JT, 2):
                    pool.wait_ge(p_hi_odd, b * JT + v // 2 + 1)
                    nc.gpsimd.tensor_tensor(pr_lo[:, v // JT, v % JT, :], prob32[v % 4], pr_hi[:, v // JT, v % JT, :],
                                            ALU.subtract).then_inc(p_lo_odd, 1)
            probabilities(0)
            with pool.Fori(1, B) as b:
                probabilities(b)

            def low_parts(f):
                for q in range(QS):
                    s = f * QS + q
                    pool.wait_ge(hhi_odd, s + 1)
                    if not (isinstance(f, int) and s < QS):
                        pool.wait_ge(g2_done, s - QS + 1)
                    nc.gpsimd.tensor_tensor(h_lo[:, q, 1, :], h32[:, (q % 2) * 2 + 1, :], h_hi[:, q, 1, :],
                                            ALU.subtract).then_inc(hlo_odd, 1)
            low_parts(0)
            with pool.Fori(1, STEPS // QS) as f:
                low_parts(f)

        @block.scalar
        def _(act):
            act.wait_ge(pool_const, POOL_CONSTS)
            act.wait_ge(in_W, 16)
            nc.scalar.mul(W_hi[:], W_raw[:], WS).then_inc(W_hi_done, 1)

            def deviations(variance, cols):
                nc.scalar.activation(sd[:, cols], variance, ACT.Sqrt, bias=eps_c[:]).then_inc(sqrt_done, 1)

            def normals(i, n):
                act.wait_ge(scale_ready, n)
                for t in range(TB):
                    tile = i * TB + t
                    ins = nc.scalar.activation(xh[:, i % 2, t, :], x[:, tile, :], ACT.Identity, bias=nmr[:, tile:tile + 1],
                                               scale=rs[:, tile:tile + 1])
                return ins

            everything = slice(0, NT)
            act.wait_ge(mv_ready, 1)
            deviations(mv[:, 0:JT, 1], slice(0, JT))

            for i in range(-4, NB):
                j = i + 1
                if 0 <= j < NB:
                    h = j % 2
                    act.wait_ge(hg_done, j + 1)
                    after(act, scanned, j - 1)
                    hidden, gates_in = ps[:, 4 + 2 * h, :], ps[:, 5 + 2 * h, :]
                    nc.scalar.activation(wA[:, h, :], gates_in, ACT.Sigmoid, scale=-1.0 / WS)
                    nc.scalar.activation(wB[:, h, :], gates_in, ACT.Sigmoid, scale=1.0 / WS)
                    nc.scalar.activation(wC[:, h, :], hidden, ACT.Sigmoid, scale=1.0 / WS)
                    nc.scalar.activation(wD[:, h, :], hidden, ACT.Identity, scale=1.0 / WS, bias=half[:]).then_inc(gates, 1)
                j = i + 3
                if 0 <= j < NB:
                    act.wait_ge(a_t, j + 1)
                    nc.scalar.copy(xT_hi[:, j * N:(j + 1) * N], ps[:, j % 2, :]).then_inc(a_hi, 1)
                j = i + 4
                if j == 2:
                    act.wait_ge(mv_ready, B)
                    deviations(mv[:, JT:, 1], slice(JT, NT))
                if j < NB:
                    after(act, a_t, j - 1)
                    normals(j, 1 if j < 2 else 2).then_inc(n1, 1)

            act.wait_ge(mv_ready, 2 * B)
            deviations(mv[:, :, 1], everything)
            act.wait_ge(ve_ready, 1)
            deviations(ve[:], everything)
            for i in range(NB):
                act.wait_ge(p_t, i + 1)
                after(act, rt_mm, i - 1)
                nc.scalar.copy(xT32[:, i % 2, :], ps[:, i % 2, :]).then_inc(p_t32, 1)
                if i == 0:
                    act.wait_ge(in_w1, 16)
                    act.wait_ge(in_w2, 16)
                e = slice(i * F0, (i + 1) * F0)
                nc.scalar.mul(w1_hi[:, e].rearrange("d (c p) -> d c p", c=NI0), stage_a[:, e].rearrange("d (p c) -> d c p", c=NI0), WS)
                nc.scalar.mul(w2_hi[:, W2_AT + i * NI0:W2_AT + (i + 1) * NI0], raw_w2[:, i * NI0:(i + 1) * NI0],
                              WS).then_inc(ew_hi, 1)
                if i == AHEAD:
                    act.wait_ge(shifted, 1)
                    nc.scalar.activation(ex0[:], exm0[:], ACT.Exp).then_inc(r_exp, 1)
            act.wait_ge(shifted, 2)
            nc.scalar.activation(ex0[:], exm0[:], ACT.Exp).then_inc(r_exp, 1)

            def features(q, par):
                act.wait_ge(xs_tr, q + 1)
                after(act, xglo_done, q - 1)
                nc.scalar.activation(xg[:, par, :], ps[:, par, :], ACT.Identity, scale=ln_g[:], bias=ln_b[:]).then_inc(xg_done, 1)
                act.wait_ge(xg_done, q + 1)
                after(act, s1_mm, (q - 1) * TB)
                nc.scalar.copy(xg_hi[:, par], xg[:, par, :]).then_inc(xghi_done, 1)

            def quad(q, par, next_features=True):
                for t in range(TB):
                    if t == LAG and next_features:
                        features(q + 1, 1 - par)
                    act.wait_ge(s1_mm, q * TB + t + 1)
                    after(act, s2_mm, q * TB + t - TB + 1)
                    nc.scalar.activation(s_hi[:, t].rearrange("p c n -> p (c n)"), ps[:, 2 + t, :],
                                         ACT.Relu).then_inc(shi_done, 1)

            def scaled_weights(k):
                for weights, loaded in ((stage_a, in_w1), (stage_b, in_w2)):
                    act.wait_ge(loaded, 32)
                    nc.scalar.mul(weights[:, ds(k * N, N)], weights[:, ds(k * N, N)], WS).then_inc(ew_scaled, 1)

            act.wait_ge(in_rows, 64)
            nc.scalar.mul(b1_rowsv, b1_rawv, WS).then_inc(rows_hi, 1)
            nc.scalar.mul(b2_rows[:], b2_raw, WS * WS).then_inc(rows_hi, 1)
            features(0, 0)
            quad(0, 0)
            quad(1, 1)
            with act.Fori(1, PAIRS - 1) as p:
                for par in range(2):
                    quad(p * 2 + par, par)
                    scaled_weights(p * 2 + par - 2)
            quad(QUADS - 2, 0)
            quad(QUADS - 1, 1, next_features=False)

            def experts():
                def steps(f):
                    for q in range(QS):
                        s = f * QS + q
                        for ic in range(NI1):
                            slot = (q % 2) * 2 + ic
                            act.wait_ge(g1_done, s * NI1 + ic + 1)
                            if not (isinstance(f, int) and s < 2):
                                act.wait_ge((hlo_done, hlo_odd)[ic], s - 1)
                            e = (f % (E1 // QS)) * QS + q
                            nc.scalar.activation(h32[:, slot, :], ps[:, slot, :], ACT.Gelu, scale=1.0 / WS,
                                                 bias=b1[:, ds(e, 1), ic]).then_inc(act_done, 1)
                        act.wait_ge(act_done, s * NI1 + 1)
                        if not (isinstance(f, int) and s < QS):
                            act.wait_ge(g2_done, s - QS + 1)
                        nc.scalar.copy(h_hi[:, q, 0, :], h32[:, (q % 2) * 2, :]).then_inc(hhi_done, 1)

                steps(0)
                with act.Fori(1, STEPS // QS) as f:
                    steps(f)

            act.wait_ge(pw_t, 1)
            nc.scalar.mul(pw_hi[:].rearrange("p n d -> p (n d)"), ps[:, 7, :], WS).then_inc(pw_hi_done, 1)

            def features_of(first, last, n):
                for i in range(first, last + 1):
                    if i < last:
                        after(act, transposed, i - 1 if i >= 2 else 0)
                        normals(i, n).then_inc(normed, 1)
                    j = i - 1
                    if j >= first:
                        act.wait_ge(transposed, j + 1)
                        nc.scalar.copy(xT_hi[:, j * N:(j + 1) * N], ps[:, turn_bank(j, 0), :]).then_inc(hi_made, 1)

            act.wait_ge(s2_mm, QUADS * TB)
            act.wait_ge(ew_scaled, 2 * EF // N)
            nc.scalar.copy(w1_hi[:].rearrange("d (e c p) -> d e c p", e=E1, c=NI1),
                           stage_a[:].rearrange("d (e p c) -> d e c p", e=E1, c=NI1)).then_inc(ew_hi, 1)
            nc.scalar.copy(w2_hi[:, W2_AT:], raw_w2).then_inc(ew_hi, 1)
            nc.scalar.copy(w2_hi[:, 0:W2_AT], raw_w2[:, EF // P - W2_AT:]).then_inc(ew_hi, 1)
            def group_features(g):
                tiles = slice(g * GT, (g + 1) * GT)
                act.wait_ge(mv_ready, 2 * B + (g + 1) * (B // G))
                deviations(mv[:, tiles, 1], tiles)
                features_of(g * GB, (g + 1) * GB, g + 3)

            def queries_keys(b):
                for m in range(4):
                    act.wait_ge(qk_mm, b * 4 + m + 1)
                    hc = m % 2
                    if m == 0:
                        after(act, st_mm, b * 2 * JT)
                    nc.scalar.mul((q_hi if m < 2 else k_hi)[:, hc * N:(hc + 1) * N], ps[:, qk_bank(m), :],
                                  SCORE / WS if m < 2 else 1.0 / WS).then_inc(qk_hi, 1)

            def normalised(b):
                after(act, o_lo_done, b)
                for qt in range(JT):
                    act.wait_ge(o_rcp, b * JT + qt + 1)
                    nc.scalar.activation(o32[:, qt, :], ps[:, 6 + qt % 2, 0:D], ACT.Identity,
                                         scale=osum[:, qt:qt + 1]).then_inc(o_norm, 1)
                act.wait_ge(o_norm, b * JT + JT)
                after(act, wo_mm, b)
                nc.scalar.copy(o_hi, o32[:]).then_inc(o_hi_done, 1)

            def probabilities(b):
                for u in range(2 * JT + 1):
                    if u < 2 * JT:
                        act.wait_ge(st_mm, b * 2 * JT + u + 1)
                        after(act, (p_lo_even, p_lo_odd)[u % 2], b * JT + u // 2 - 1)
                        nc.scalar.activation(prob32[u % 4], ps[:, u % 4, :], ACT.Exp, bias=pbias_c[:]).then_inc(p_exp, 1)
                    if u % 2 == 1:
                        v = u - 1
                        act.wait_ge(p_exp, b * 2 * JT + v + 1)
                        if v == 0:
                            after(act, pv_mm, b * JT)
                        nc.scalar.copy(pr_hi[:, v // JT, v % JT, :], prob32[v % 4]).then_inc(p_hi_even, 1)
                    if u in (5, 7):
                        hc = (u - 5) // 2
                        act.wait_ge(vp_mm, b * 2 + hc + 1)
                        nc.scalar.mul(v_hi[:, hc * TB:(hc + 1) * TB, 0:D], ps[:, 4 + hc, :].rearrange("p (t d) -> p t d", t=TB),
                                      1.0 / WS).then_inc(vp_hi, 1)

            group_features(0)
            queries_keys(0)
            group_features(1)
            act.wait_ge(ew_lo, E0 + 3)
            probabilities(0)

            def batch(b):
                queries_keys(b)
                normalised(b - 1)
                probabilities(b)
            batch(1)
            with act.Fori(2, B) as b:
                batch(b)

            act.wait_ge(mv_copied, B - 1)
            deviations(mv[:, 0:NT - JT, 1], slice(0, NT - JT))
            for i in range(2):
                normals(i, 5).then_inc(normed, 1)
            normalised(B - 1)
            for i in range(NB):
                act.wait_ge(transposed, NB + i + 1)
                after(act, routed_mm, i - 1)
                nc.scalar.copy(xT32[:, i % 2, :], ps[:, turn_bank(i, 1), :]).then_inc(t32_made, 1)
                nc.scalar.copy(xT_hi[:, i * N:(i + 1) * N], ps[:, turn_bank(i, 1), :]).then_inc(hi_made, 1)
                if i == 2:
                    act.wait_ge(mv_copied, B)
                    deviations(mv[:, NT - JT:, 1], slice(NT - JT, NT))
                if i + 2 < NB:
                    normals(i + 2, 5 if i + 2 < NB - 2 else 6).then_inc(normed, 1)

            def transposed_weights(g):
                for i in range(g * GB, (g + 1) * GB):
                    act.wait_ge(cT_mm, i + 1)
                    after(act, b2_mm, i - 1)
                    nc.scalar.copy(cT[0:E1, i % 2, :], ps[0:E1, 6 + i % 2, :]).then_inc(cT_cp, 1)

            for g in range(G):
                act.wait_ge(shifted1, g + 1)
                nc.scalar.activation(ex, exm, ACT.Exp).then_inc(exp_done, 1)
                if g > 0:
                    transposed_weights(g - 1)
            transposed_weights(G - 1)
            experts()

        @block.vector
        def _(dve):
            def wait_alone(semaphore, value):
                dve.wait_ge(semaphore, value)
                nc.vector.memset(held[:], 0.0)

            def split_experts(first, last):
                for e in range(first, last):
                    sl, slots = slice(e * F0, (e + 1) * F0), slice(W2_AT + e * NI0, W2_AT + (e + 1) * NI0)
                    dve.wait_ge(ew_hi, e + 1)
                    STT(out=w1_lo[:, sl].rearrange("d (c p) -> d c p", c=NI0),
                        in0=stage_a[:, sl].rearrange("d (p c) -> d c p", c=NI0), scalar=WS,
                        in1=w1_hi[:, sl].rearrange("d (c p) -> d c p", c=NI0), op0=ALU.mult, op1=ALU.subtract)
                    STT(out=w2_lo[:, slots], in0=raw_w2[:, e * NI0:(e + 1) * NI0], scalar=WS, in1=w2_hi[:, slots], op0=ALU.mult,
                        op1=ALU.subtract).then_inc(ew_lo, 1)

            made, counted = [0], [0]

            def link(ins):
                made[0] += 1
                ins.then_inc(chain, 1)
                dve.wait_ge(chain, made[0])

            TT, TS, STT = nc.vector.tensor_tensor, nc.vector.tensor_scalar, nc.vector.scalar_tensor_tensor

            def token_statistics(b):
                for t in range(JT):
                    ins = nc.vector.bn_stats(st8[:, t, :], x[:, b * JT + t, :])
                link(ins)
                for t in range(JT):
                    ins = nc.vector.bn_aggr(mv[:, b * JT + t, :], st8[:, t, :])
                counted[0] += 1
                ins.then_inc(mv_ready, 1)
                dve.wait_ge(mv_ready, counted[0])

            def inverse_root(res, variance, cols, n):
                dve.wait_ge(sqrt_done, n)
                link(nc.vector.reciprocal(r0[:, cols], sd[:, cols]))
                link(TT(nt1[:, cols], r0[:, cols], r0[:, cols], ALU.mult))
                link(STT(out=nt2[:, cols], in0=variance, scalar=EPS, in1=nt1[:, cols], op0=ALU.add, op1=ALU.mult))
                link(TS(nt3[:, cols], nt2[:, cols], -0.5, 1.5, ALU.mult, ALU.add))
                link(TT(res[:, cols], r0[:, cols], nt3[:, cols], ALU.mult))

            def shift(cols):
                STT(out=nmr[:, cols], in0=mv[:, cols, 0], scalar=-1.0, in1=rs[:, cols], op0=ALU.mult,
                    op1=ALU.mult).then_inc(scale_ready, 1)

            everything = slice(0, NT)

            def normal(dst, t, scale):
                return TS(dst, x[:, t, :], mv[:, t, 0:1], scale[:, t:t + 1], ALU.subtract, ALU.mult)

            def low_block(j):
                cols = slice(j * N, (j + 1) * N)
                dve.wait_ge(a_hi, j + 1)
                TT(xT_lo[:, cols], ps[:, j % 2, :], xT_hi[:, cols], ALU.subtract).then_inc(a_lo, 1)

            for b in range(B):
                dve.wait_ge(in_x[b], 16)
                token_statistics(b)
                if b == 0:
                    inverse_root(rs, mv[:, 0:JT, 1], slice(0, JT), 1)
                    shift(slice(0, JT))
                    dve.wait_ge(W_hi_done, 1)
                    STT(out=W_lo[:], in0=W_raw[:], scalar=WS, in1=W_hi[:], op0=ALU.mult, op1=ALU.subtract).then_inc(W_split, 1)
                elif b <= 2:
                    low_block(b - 1)
            inverse_root(rs, mv[:, JT:, 1], slice(JT, NT), 2)
            shift(slice(JT, NT))
            for i in range(NB + 1):
                if i < NB:
                    h = i % 2
                    dve.wait_ge(gates, i + 1)
                    link(TT(wC[:, h, :], wC[:, h, :], wD[:, h, :], ALU.max))
                    link(TT(wB[:, h, :], wB[:, h, :], wC[:, h, :], ALU.mult))
                    after(dve, back_t, i - 1)
                    nc.vector.tensor_tensor_scan(hT[:, h, :], wA[:, h, :], wB[:, h, :], 0.0 if h == 0 else hT[:, 0, N - 1:N],
                                                 ALU.mult, ALU.add).then_inc(scanned, 1)
                    dve.wait_ge(scanned, i + 1)
                if i + 2 < NB:
                    low_block(i + 2)
                j = i - 1
                if j >= 0:
                    dve.wait_ge(back_t, j + 1)
                    xb = x[:, j * TB:(j + 1) * TB, :].rearrange("p t d -> p (t d)")
                    TT(xb, ps[:, 2 + j % 2, :], xb, ALU.add).then_inc(x_added, 1)
                    dve.wait_ge(x_added, j + 1)
                    if j % 2 == 1:
                        token_statistics(j // 2)

            inverse_root(rs, mv[:, :, 1], everything, 3)
            link(TT(nt1[:], rs[:], rs[:], ALU.mult))
            TT(ve[:], mv[:, :, 1], nt1[:], ALU.mult).then_inc(ve_ready, 1)
            inverse_root(rs2, ve[:], everything, 4)
            link(STT(out=unscale[:], in0=ve[:], scalar=EPS, in1=rs2[:], op0=ALU.add, op1=ALU.mult))
            link(TT(rs[:], rs[:], rs2[:], ALU.mult))
            dve.wait_ge(a_t, NB)
            for i in range(NB):
                for t in range(i * TB, (i + 1) * TB):
                    ins = normal(xn_tile(t), t, rs)
                ins.then_inc(n2, 1)

            def over(ap, n, like):
                return ap.unsqueeze(2).to_broadcast([P, n, like])

            def route(g):
                tiles = slice(g * GT, (g + 1) * GT)
                dve.wait_ge(rt_mm, GB * (g + 1))
                raw = ps[:, 2 + g, 0:GT * E0].rearrange("p (t e) -> p t e", t=GT)
                link(TT(num0[:], raw, over(unscale[:, tiles], GT, E0), ALU.mult))
                link(TT(lg0[:], num0[:], br[0][:].unsqueeze(1).to_broadcast([P, GT, E0]), ALU.add))
                link(nc.vector.tensor_reduce(top0[:], lg0[:], AX_X, ALU.max))
                TT(exm0[:], lg0[:], over(top0[:], GT, E0), ALU.subtract).then_inc(shifted, 1)
                link(TT(eq0[:], lg0[:], over(top0[:], GT, E0), ALU.is_equal))
                iob = iom[:].unsqueeze(1).to_broadcast([P, GT, E0])
                link(TT(num0[:], eq0[:], iob, ALU.mult))
                link(nc.vector.tensor_reduce(first0[:], num0[:], AX_X, ALU.min))
                TT(oh_bf[:], iob, over(first0[:], GT, E0), ALU.is_equal).then_inc(oh_done, 1)
                dve.wait_ge(oh_done, g + 1)
                dve.wait_ge(r_exp, g + 1)
                link(nc.vector.tensor_reduce(den0[:], ex0[:], AX_X, ALU.add))
                link(nc.vector.reciprocal(rden0[:], den0[:]))
                link(TS(gate[:, tiles], rden0[:], 1.0 / (WS * WS), None, ALU.mult))

            def sort_positions(g):
                dve.wait_ge(pre_mm, g + 1)
                before = ps[:, 2 + g, 128:128 + GT * E0].rearrange("p (t e) -> p e t", t=GT)
                total = ps[:, 2 + g, 256:256 + GT * E0].rearrange("p (t e) -> p e t", t=GT)
                flat = lambda a: a.rearrange("p e t -> p (e t)")
                link(nc.vector.tensor_copy(tot[:], total))
                link(nc.vector.tensor_tensor_scan(flat(cum[:]), flat(notfirst[:]), flat(tot[:]), 0.0, ALU.mult, ALU.add))
                link(TT(big[:, :, 0:GT], cum[:, :, GT - 1:GT].to_broadcast([P, E0, GT]),
                        kf[:].unsqueeze(1).to_broadcast([P, E0, GT]), ALU.is_gt))
                link(nc.vector.tensor_reduce(ntile[:], big[:, :, 0:GT], AX_X, ALU.add))
                link(nc.vector.tensor_tensor_scan(ends[:], ones8[:], ntile[:], 0.0, ALU.mult, ALU.add))
                link(TT(starts[:], ends[:], ntile[:], ALU.subtract))
                link(TT(rank[:], cum[:], tot[:], ALU.subtract))
                link(TT(rank[:], before, rank[:], ALU.add))
                link(STT(out=rank[:], in0=starts[:].unsqueeze(2).to_broadcast([P, E0, GT]), scalar=float(P), in1=rank[:],
                         op0=ALU.mult, op1=ALU.add))
                link(TT(cum[:].rearrange("p e t -> p t e"), oh_bf[:], rank[:].rearrange("p e t -> p t e"), ALU.mult))
                link(nc.vector.tensor_reduce(posf[:], cum[:].rearrange("p e t -> p t e"), AX_X, ALU.add))
                nc.vector.tensor_copy(pos[:, g * GT:(g + 1) * GT], posf[:]).then_inc(pos_done, 1)
                link(TT(big[:].rearrange("p e j -> p j e"), ends[:].unsqueeze(1).to_broadcast([P, ST, E0]),
                        jf[:].unsqueeze(2).to_broadcast([P, ST, E0]), ALU.is_le))
                tiles = slice(g * ST, (g + 1) * ST)
                link(nc.vector.tensor_reduce(texf[:, tiles], big[:].rearrange("p e j -> p j e"), AX_X, ALU.add))
                link(TS(texf[:, tiles], texf[:, tiles], float(E0 - 1), None, ALU.min))
                nc.vector.tensor_copy(tex[:, tiles], texf[:, tiles]).then_inc(tex_done, 1)

            dve.wait_ge(in_small, 16 * 8)
            dve.wait_ge(pool_const, POOL_CONSTS)
            link(TS(iom[:], iota_e[:, 0:E0], float(E0), None, ALU.subtract))
            link(TS(erow[ROW_LO:ROW_LO + E0, :], erow[ROW_LO:ROW_LO + E0, :], float(ROW_LO), None, ALU.subtract))
            split_experts(0, 3)
            for g in range(G):
                route(g)
                sort_positions(g)
                if g == 0:
                    split_experts(3, 5)
            split_experts(5, E0)
            dve.wait_ge(rows_hi, 2)
            low = slice(ROW_LO, ROW_LO + E0)
            STT(out=b1_rowsv[low], in0=b1_rawv[low], scalar=WS, in1=b1_rowsv[low], op0=ALU.mult,
                op1=ALU.subtract).then_inc(rows_lo, 1)
            STT(out=b2_rows[low], in0=b2_raw[low], scalar=WS * WS, in1=b2_rows[low], op0=ALU.mult,
                op1=ALU.subtract).then_inc(rows_lo, 1)

            def features(q, par):
                dve.wait_ge(xghi_done, q + 1)
                TT(xg_lo[:, par], xg[:, par, :], xg_hi[:, par], ALU.subtract).then_inc(xglo_done, 1)
                after(dve, s2_mm, (q - 1) * TB)
                TS(selq[:, par].rearrange("p (t n) -> p t n", t=TB), over(texf[:, ds(q * TB, TB)], TB, P), erow[:], None,
                   ALU.is_equal).then_inc(sel_done, 1)

            def output(q, par, pair):
                dve.wait_ge(s2_mm, q * TB + 2 * pair + 2)
                if pair == 0:
                    after(dve, y_st[par], 16 * (q // 2) if isinstance(q, int) else (q - par) * 8)
                y = ps[:, 6 + pair, :].rearrange("p (t h n) -> p t h n", t=2, h=2)
                low = ysb[:, par, pair * 2 * P:(pair + 1) * 2 * P].rearrange("p (t n) -> p t n", t=2)
                nc.vector.tensor_copy(low, y[:, :, 1]).then_inc(y_low, 1)
                dve.wait_ge(y_low, q * 2 + pair + 1)
                TT(low, y[:, :, 0], low, ALU.add).then_inc(y_cp, 1)

            def quad(q, par, next_features=True):
                for t in range(TB):
                    if t % 2 == 0 and not (isinstance(q, int) and q == 0):
                        output(q - 1, 1 - par, t // 2)
                    if t == LAG and next_features:
                        features(q + 1, 1 - par)
                    dve.wait_ge(shi_done, q * TB + t + 1)
                    STT(out=s_lo[:, t].rearrange("p c n -> p (c n)"), in0=ps[:, 2 + t, :], scalar=0.0,
                        in1=s_hi[:, t].rearrange("p c n -> p (c n)"), op0=ALU.max, op1=ALU.subtract).then_inc(slo_done, 1)

            dve.wait_ge(tex_done, G)
            features(0, 0)
            quad(0, 0)
            quad(1, 1)
            with dve.Fori(1, PAIRS - 1) as p:
                for par in range(2):
                    quad(p * 2 + par, par)
            quad(QUADS - 2, 0)
            quad(QUADS - 1, 1, next_features=False)
            for pair in range(2):
                output(QUADS - 1, 1, pair)

            def low_features(first, last, k):
                for i in range(first, last):
                    dve.wait_ge(hi_made, k * NB + i + 1)
                    cols = slice(i * N, (i + 1) * N)
                    TT(xT_lo[:, cols], ps[:, turn_bank(i, k), :], xT_hi[:, cols], ALU.subtract).then_inc(lo_made, 1)

            for g in range(G):
                for b in range(g * B // G, (g + 1) * B // G):
                    dve.wait_ge(gath[b], 16 * JT)
                    for t in range(b * JT, (b + 1) * JT):
                        ins = STT(out=x[:, t, :], in0=yg[:, t, :], scalar=gate[:, t:t + 1], in1=x[:, t, :], op0=ALU.mult, op1=ALU.add)
                    ins.then_inc(yadd, 1)
                    dve.wait_ge(yadd, b + 1)
                    token_statistics(b)
                    if b == B - 2:
                        low_features(0, GB, 0)
                        dve.wait_ge(pw_hi_done, 1)
                        STT(out=pw_lo[:].rearrange("p n d -> p (n d)"), in0=ps[:, 7, :], scalar=WS,
                            in1=pw_hi[:].rearrange("p n d -> p (n d)"), op0=ALU.mult, op1=ALU.subtract).then_inc(pw_lo_done, 1)
                tiles = slice(g * GT, (g + 1) * GT)
                inverse_root(rs, mv[:, tiles, 1], tiles, g + 5)
                shift(tiles)

            def experts():
                def accumulate(s, q):
                    dve.wait_ge(g2_done, s + 1)
                    if not (isinstance(s, int) and s == 0):
                        dve.wait_ge(acc_done, s)
                    for t in range(TB):
                        tile = (s // E1) * TB + t
                        xt = x[:, ds(tile, 1), :].rearrange("p a d -> p (a d)")
                        ins = nc.vector.scalar_tensor_tensor(out=xt, in0=ps[:, 4 + q, t * P:(t + 1) * P],
                                                             scalar=comb[:, ds(s * TB + t, 1)], in1=xt,
                                                             op0=ALU.mult, op1=ALU.add)
                    ins.then_inc(acc_done, 1)

                def steps(f):
                    for q in range(QS):
                        s = f * QS + q
                        dve.wait_ge(act_done, s * NI1 + 2)
                        if not (isinstance(f, int) and s < QS):
                            dve.wait_ge(g2_done, s - QS + 1)
                        nc.vector.tensor_copy(h_hi[:, q, 1, :], h32[:, (q % 2) * 2 + 1, :]).then_inc(hhi_odd, 1)
                        dve.wait_ge(hhi_done, s + 1)
                        nc.vector.tensor_tensor(h_lo[:, q, 0, :], h32[:, (q % 2) * 2, :], h_hi[:, q, 0, :],
                                                ALU.subtract).then_inc(hlo_done, 1)
                        if not (isinstance(f, int) and s < LAG):
                            accumulate(s - LAG, q % 2)

                steps(0)
                with dve.Fori(1, STEPS // QS) as f:
                    steps(f)
                for s in range(STEPS - LAG, STEPS):
                    accumulate(s, s % 2)
                dve.wait_ge(acc_done, STEPS)

            dve.wait_ge(v_const, 3)

            def queries_keys(b):
                for m in range(4):
                    dve.wait_ge(qk_hi, b * 4 + m + 1)
                    cols = slice((m % 2) * N, (m % 2 + 1) * N)
                    hi, lo = (q_hi, q_lo) if m < 2 else (k_hi, k_lo)
                    STT(out=lo[:, cols], in0=ps[:, qk_bank(m), :], scalar=SCORE / WS if m < 2 else 1.0 / WS, in1=hi[:, cols],
                        op0=ALU.mult, op1=ALU.subtract).then_inc(qk_lo, 1)

            def maxima(b, scores=True, values=True):
                if scores:
                    after(dve, st_mm, b * 2 * JT)
                if values:
                    after(dve, o_norm, (b - 1) * JT)
                for qt in range(JT):
                    if scores:
                        dve.wait_ge(sn_mm, b * JT + qt + 1)
                        pair = 2 * (qt % 2)
                        nc.vector.tensor_reduce(nmax[:, qt:qt + 1], ps[:, pair:pair + 2, :].rearrange("p a n -> p (a n)"),
                                                AX_X, ALU.max).then_inc(max_done, 1)
                    if values:
                        dve.wait_ge(pv_mm, (b - 1) * JT + qt + 1)
                        nc.vector.reciprocal(osum[:, qt:qt + 1], ps[:, 6 + qt % 2, D:D + 1]).then_inc(o_rcp, 1)
                    if scores:
                        dve.wait_ge(max_done, b * JT + qt + 1)
                        TS(dg[:, qt, :], ident[:], nmax[:, qt:qt + 1], -1.0, ALU.mult, ALU.mult).then_inc(diag_done, 1)
                if values:
                    dve.wait_ge(o_hi_done, b)
                    TT(o_lo, o32[:], o_hi, ALU.subtract).then_inc(o_lo_done, 1)

            def residual(b):
                dve.wait_ge(wo_mm, b + 1)
                STT(out=x[:, ds(b * JT, JT), :].rearrange("p j d -> p (j d)"), in0=ps[:, 6:8, :].rearrange("p a n -> p (a n)"),
                    scalar=1.0 / WS, in1=stage_a[:, ds(b * S, S)], op0=ALU.mult, op1=ALU.add).then_inc(x3_done, 1)

            def batch_statistics(b, tiles):
                if tiles.start == 0:
                    wait_alone(x3_done, b + 1)
                for t in range(JT)[tiles]:
                    ins = nc.vector.bn_stats(st8[:, t, :], x[:, ds(b * JT + t, 1), :].rearrange("p a d -> p (a d)"))
                if tiles.stop == JT:
                    ins.then_inc(stats, 1)
                    after(dve, mv_copied, b)
                    wait_alone(stats, b + 1)
                    for t in range(JT):
                        ins = nc.vector.bn_aggr(agg8[:, t, :], st8[:, t, :])
                    ins.then_inc(aggr, 1)
                    dve.wait_ge(aggr, b + 1)
                    nc.vector.tensor_copy(mv[:, ds(b * JT, JT), :], agg8[:]).then_inc(mv_copied, 1)

            def probabilities(b, previous=True):
                after(dve, pv_mm, b * JT)
                for v in range(0, 2 * JT, 2):
                    dve.wait_ge(p_exp, b * 2 * JT + v + 2)
                    nc.vector.tensor_copy(pr_hi[:, v // JT, v % JT + 1, :], prob32[(v + 1) % 4]).then_inc(p_hi_odd, 1)
                    dve.wait_ge(p_hi_even, b * JT + v // 2 + 1)
                    TT(pr_lo[:, v // JT, v % JT, :], prob32[v % 4], pr_hi[:, v // JT, v % JT, :],
                       ALU.subtract).then_inc(p_lo_even, 1)
                    if v == 4 and previous:
                        residual(b - 1)
                    if v in (6, 8):
                        hc = (v - 6) // 2
                        dve.wait_ge(vp_hi, b * 2 + hc + 1)
                        tiles = slice(hc * TB, (hc + 1) * TB)
                        STT(out=v_lo[:, tiles, 0:D], in0=ps[:, 4 + hc, :].rearrange("p (t d) -> p t d", t=TB), scalar=1.0 / WS,
                            in1=v_hi[:, tiles, 0:D], op0=ALU.mult, op1=ALU.subtract).then_inc(vp_lo, 1)
                    if 6 <= v <= 12 and previous:
                        batch_statistics(b - 1, slice(v - 6, v - 4))

            queries_keys(0)
            maxima(0, values=False)
            low_features(GB, NB, 0)
            dve.wait_ge(ew_lo, E0 + 3)
            probabilities(0, previous=False)
            dve.wait_ge(x2_in, 16 * B)

            def batch(b):
                queries_keys(b)
                maxima(b)
                probabilities(b)
            batch(1)
            with dve.Fori(2, B) as b:
                batch(b)
            dve.wait_ge(mv_copied, B - 1)
            inverse_root(rs, mv[:, 0:NT - JT, 1], slice(0, NT - JT), G + 5)
            shift(slice(0, NT - JT))
            maxima(B, scores=False)
            residual(B - 1)
            batch_statistics(B - 1, slice(0, JT))

            dve.wait_ge(mv_copied, B)
            inverse_root(rs, mv[:, NT - JT:, 1], slice(NT - JT, NT), G + 6)
            shift(slice(NT - JT, NT))

            def route_top(g):
                dve.wait_ge(routed_mm, GB * (g + 1))
                raw = ps[:, 4 + g, 0:GT * E1].rearrange("p (t e) -> p t e", t=GT)
                link(TT(lg, raw, br[1][:].unsqueeze(1).to_broadcast([P, GT, E1]), ALU.add))
                for t in range(GT):
                    ins = nc.vector.max(top[:, t, :], lg[:, t, :])
                link(ins)
                for t in range(GT):
                    ins = nc.vector.max_index(idx[:, t, :], top[:, t, :], lg[:, t, :])
                link(ins)
                TT(exm, lg, over(top[:, :, 0], GT, E1), ALU.subtract).then_inc(shifted1, 1)
                link(nc.vector.tensor_copy(idf[:], idx[:]))
                iob = iota_e[:].unsqueeze(1).to_broadcast([P, GT, E1])
                for k in range(4):
                    ins = TT(eqk[:, k], iob, over(idf[:, :, k], GT, E1), ALU.is_equal)
                link(ins)
                link(TT(eqk[:, 0:2], eqk[:, 0:2], eqk[:, 2:4], ALU.add))
                link(TT(eqk[:, 0], eqk[:, 0], eqk[:, 1], ALU.add))
                dve.wait_ge(exp_done, g + 1)
                link(TT(num, ex, eqk[:, 0], ALU.mult))
                link(nc.vector.tensor_reduce(den[:], num, AX_X, ALU.add))
                link(nc.vector.reciprocal(rden[:], den[:]))
                link(TT(cw[:, g], num, over(rden[:], GT, E1), ALU.mult))
                link(nc.vector.tensor_copy(cw_parts[:, g, 0], cw[:, g]))
                TT(cw_parts[:, g, 1], cw[:, g], cw_parts[:, g, 0], ALU.subtract).then_inc(c_ready, 1)
                for k in range(GB):
                    i = g * GB + k
                    cv = comb[:, i * E1 * TB:(i + 1) * E1 * TB].rearrange("p (e t) -> p t e", t=TB)
                    ins = TS(cv, cw[:, g, k * TB:(k + 1) * TB, :], 1.0 / WS, None, ALU.mult)
                link(ins)

            for g in range(G):
                low_features(g * GB, (g + 1) * GB, 1)
                route_top(g)
            for i in range(NB):
                dve.wait_ge(b2_mm, i + 1)
                xb = x[:, i * TB:(i + 1) * TB, :].rearrange("p t d -> p (t d)")
                TT(xb, ps[:, b2_bank(i), :], xb, ALU.add).then_inc(b2_added, 1)
            dve.wait_ge(b2_added, NB)
            experts()

        @block.tensor
        def _(pe):
            mm = nc.tensor.matmul

            def product(out, a, b, last=True):
                mm(out, a[0], b[0], start=True, stop=False)
                mm(out, a[0], b[1], start=False, stop=False)
                return mm(out, a[1], b[0], start=False, stop=last)

            pe.wait_ge(pool_const, POOL_CONSTS)
            def turn(src, bank, counted):
                for t in range(TB):
                    ins = nc.tensor.transpose(ps[:, bank, t * P:(t + 1) * P], src[t], ident[:])
                ins.then_inc(counted, 1)

            pe.wait_ge(W_split, 1)
            for i in range(-3, NB):
                if i >= 0:
                    pe.wait_ge(scanned, i + 1)
                    after(pe, x_added, i - 1)
                    turn([hT[:, i % 2, t * P:(t + 1) * P] for t in range(TB)], 2 + i % 2, back_t)
                j = i + 2
                if 0 <= j < NB:
                    pe.wait_ge(a_lo, j + 1)
                    after(pe, gates, j - 1)
                    xi = (xT_hi[:, j * N:(j + 1) * N], xT_lo[:, j * N:(j + 1) * N])
                    bank = 4 + 2 * (j % 2)
                    product(ps[:, bank, :], (W_hi[:, 0:D], W_lo[:, 0:D]), xi)
                    product(ps[:, bank + 1, :], (W_hi[:, D:2 * D], W_lo[:, D:2 * D]), xi).then_inc(hg_done, 1)
                j = i + 3
                if j < NB:
                    pe.wait_ge(n1, j + 1)
                    after(pe, a_lo, j - 1)
                    turn([xh[:, j % 2, t, :] for t in range(TB)], j % 2, a_t)

            def counts(g):
                pe.wait_ge(oh_done, g + 1)
                oh = oh_bf[:].rearrange("p t e -> p (t e)")
                mm(ps[:, 2 + g, 128:128 + GT * E0], tri_bf[:], oh, start=True, stop=True)
                mm(ps[:, 2 + g, 256:256 + GT * E0], ones_bf[:], oh, start=True, stop=True).then_inc(pre_mm, 1)

            pe.wait_ge(in_small, 16 * 8)
            pe.wait_ge(x_added, NB)
            for i in range(NB + 1):
                if i < NB:
                    pe.wait_ge(n2, i + 1)
                    after(pe, p_t32, i - 1)
                    turn([xn_tile(i * TB + t) for t in range(TB)], i % 2, p_t)
                j = i - 1
                if j >= 0:
                    pe.wait_ge(p_t32, j + 1)
                    for t in range(TB):
                        k = (j % GB) * TB + t
                        ins = mm(ps[:, 2 + j // GB, k * E0:(k + 1) * E0], xT32[:, j % 2, t * P:(t + 1) * P], Wr[0][:],
                                 start=True, stop=True)
                    ins.then_inc(rt_mm, 1)
                if i == AHEAD:
                    counts(0)
            counts(1)

            def turned(q, par):
                pe.wait_ge(in_xs[par], 16 * (q // 2 + 1) if isinstance(q, int) else (q - par) * 8 + 16)
                after(pe, xg_done, q - 1)
                turn([xs_t[:, par, t, :] for t in range(TB)], par, xs_tr)

            def experts_of(tile, n):
                return nc.values_load_multi_w_load_instructions(
                    tex[0:1, ds(tile, n)], (mybir.EngineType.PE,), min_val=0, max_val=E0 - 1,
                    skip_runtime_bounds_check_because="the sort's last step takes the minimum with E0 - 1 of a count")[1]

            def hidden(q, t, par, expert):
                if t == 0:
                    pe.wait_ge(xglo_done, q + 1)
                    pe.wait_ge(sel_done, q + 1)
                after(pe, slo_done, q * TB + t - TB + 1)
                tok = slice(t * P, (t + 1) * P)
                for c in range(NI0):
                    w = ds((expert * NI0 + c) * P, P)
                    o = ps[:, 2 + t, c * P:(c + 1) * P]
                    product(o, (w1_hi[:, w], w1_lo[:, w]), (xg_hi[:, par, tok], xg_lo[:, par, tok]), last=False)
                    ins = mm(o, b1_rows[:, c * P:(c + 1) * P], selq[:, par, tok], start=False, stop=True)
                ins.then_inc(s1_mm, 1)

            def output(q, t, par, expert):
                pe.wait_ge(slo_done, q * TB + t + 1)
                if t % 2 == 0:
                    after(pe, y_cp, q * 2 + t // 2 - 1)
                o = ps[:, 6 + t // 2, (t % 2) * 2 * P:(t % 2 + 1) * 2 * P]
                for c in range(NI0):
                    w = ds(expert * NI0 + c + W2_AT, 1)
                    both = w2_parts[:, w].rearrange("p a h n -> p (a h n)")
                    mm(o, s_hi[:, t, c], both, start=c == 0, stop=False)
                    ins = mm(o[:, 0:P], s_lo[:, t, c], both[:, 0:P], start=False, stop=c == NI0 - 1)
                    if c == 0:
                        mm(o[:, 0:P], selq[:, par, t * P:(t + 1) * P], b2_rows[:], start=False, stop=False)
                ins.then_inc(s2_mm, 1)

            def quad(q, par, next_quad=True):
                if isinstance(q, int) and q == 0:
                    experts = (None,) * LAG + experts_of(0, TB)
                else:
                    experts = experts_of(q * TB - LAG, LAG + TB)
                for t in range(TB):
                    if t == 1 and next_quad:
                        turned(q + 1, 1 - par)
                    hidden(q, t, par, experts[LAG + t])
                    if t >= LAG:
                        output(q, t - LAG, par, experts[t])
                    elif not (isinstance(q, int) and q == 0):
                        output(q - 1, t + TB - LAG, 1 - par, experts[t])

            pe.wait_ge(rows_lo, 2)
            pe.wait_ge(tex_done, G)
            pe.wait_ge(ew_lo, E0)
            turned(0, 0)
            quad(0, 0)
            quad(1, 1)
            with pe.Fori(1, PAIRS - 1) as p:
                for par in range(2):
                    quad(p * 2 + par, par)
            quad(QUADS - 2, 0)
            quad(QUADS - 1, 1, next_quad=False)
            for t, expert in enumerate(experts_of(QUADS * TB - LAG, LAG)):
                output(QUADS - 1, TB - LAG + t, 1, expert)

            def turned_block(i, k):
                pe.wait_ge(normed, k * NB + i + 1)
                if i in (4, 5) and k == 0:
                    pe.wait_ge(qk_lo, i - 3)
                elif i >= 4 and k == 1:
                    pe.wait_ge(lo_made, NB + i - 3)
                turn([xh[:, i % 2, t, :] for t in range(TB)], turn_bank(i, k), transposed)

            def experts():
                def first(f, q):
                    s = f * QS + q
                    blk = f // (E1 // QS)
                    e = (f % (E1 // QS)) * QS + q
                    xi = (xT_hi[:, ds(blk * N, N)], xT_lo[:, ds(blk * N, N)])
                    for ic in range(NI1):
                        if not (isinstance(f, int) and s < 2):
                            pe.wait_ge(act_done, s * NI1 + ic - 3)
                        w = ds((e * NI1 + ic) * P, P)
                        product(ps[:, (q % 2) * 2 + ic, :], (w1_hi[:, w], w1_lo[:, w]), xi).then_inc(g1_done, 1)

                def second(f, q):
                    s = f * QS + q - LAG
                    e = (f % (E1 // QS)) * QS + q
                    buf = (q - LAG) % QS
                    pe.wait_ge(hlo_done, s + 1)
                    pe.wait_ge(hlo_odd, s + 1)
                    if isinstance(s, int) and s < 2:
                        pe.wait_ge(b2_added, NB)
                    else:
                        pe.wait_ge(acc_done, s - 1)
                    for t in range(TB):
                        tok = slice(t * P, (t + 1) * P)
                        o = ps[:, 4 + q % 2, tok]
                        for ic in range(NI1):
                            both = w2_parts[:, ds(e * NI1 + ic, 1)].rearrange("p a h n -> p (a h n)")
                            mm(o, h_hi[:, buf, ic, tok], both[:, 0:P], start=ic == 0, stop=False)
                            mm(o, h_hi[:, buf, ic, tok], both[:, P:2 * P], start=False, stop=False)
                            ins = mm(o, h_lo[:, buf, ic, tok], both[:, 0:P], start=False, stop=ic == NI1 - 1)
                    ins.then_inc(g2_done, 1)

                pe.wait_ge(b2_added, GB)
                for q in range(QS):
                    first(0, q)
                    if q >= LAG:
                        second(0, q)
                with pe.Fori(1, STEPS // QS) as f:
                    for q in range(QS):
                        first(f, q)
                        second(f, q)
                for q in range(LAG):
                    second(STEPS // QS, q)

            pe.wait_ge(in_pw, 16 * 4)
            pe.wait_ge(y_cp, QUADS * 2)
            for n in range(4):
                ins = nc.tensor.transpose(ps[:, 7, n * P:(n + 1) * P], pw_raw[:, n, :], ident[:])
            ins.then_inc(pw_t, 1)
            for i in range(GB):
                turned_block(i, 0)
            pe.wait_ge(pw_lo_done, 1)
            pe.wait_ge(lo_made, GB)

            def queries_keys(b):
                for m in range(4):
                    if m < 2:
                        after(pe, vp_lo, b * 2)
                    else:
                        after(pe, p_exp, b * 2 * JT)
                    cols, w = ds(b * S + (m % 2) * N, N), m // 2
                    product(ps[:, qk_bank(m), :], (pw_hi[:, w, :], pw_lo[:, w, :]),
                            (xT_hi[:, cols], xT_lo[:, cols])).then_inc(qk_mm, 1)

            def scores_and_values(b, scores=True, values=True, turned={}, k=0):
                if scores:
                    pe.wait_ge(qk_hi, b * 4 + 4)
                    after(pe, p_exp, b * 2 * JT)
                if values:
                    pe.wait_ge(p_lo_even, b * JT)
                    pe.wait_ge(p_lo_odd, b * JT)
                    pe.wait_ge(vp_lo, b * 2)
                    after(pe, x3_done, b - 1)
                for qt in range(JT):
                    if scores:
                        if qt == 1:
                            pe.wait_ge(qk_lo, b * 4 + 4)
                        if qt >= 2:
                            pe.wait_ge(max_done, b * JT + qt - 1)
                        for h in range(2):
                            ins = mm(ps[:, 2 * (qt % 2) + h, :], q_hi[:, qt * P:(qt + 1) * P], k_hi[:, h * N:(h + 1) * N],
                                     start=True, stop=True)
                        ins.then_inc(sn_mm, 1)
                    if values:
                        qh, t = qt // TB, qt % TB
                        if qt >= 2:
                            pe.wait_ge(o_norm, (b - 1) * JT + qt - 1)
                        o = ps[:, 6 + qt % 2, 0:VC]
                        for kt in range(JT):
                            ph, pl = pr_hi[:, qh, kt, t * P:(t + 1) * P], pr_lo[:, qh, kt, t * P:(t + 1) * P]
                            mm(o, ph, v_hi[:, kt, :], start=kt == 0, stop=False)
                            mm(o, ph, v_lo[:, kt, :], start=False, stop=False)
                            ins = mm(o, pl, v_hi[:, kt, :], start=False, stop=kt == JT - 1)
                        ins.then_inc(pv_mm, 1)
                    if qt in turned:
                        turned_block(turned[qt], k)

            def projected(b):
                pe.wait_ge(o_lo_done, b + 1)
                for j in range(JT):
                    ins = product(ps[:, 6 + j // TB, (j % TB) * P:(j % TB + 1) * P], (o_hi[:, j, :], o_lo[:, j, :]),
                                  (pw_hi[:, 3, :], pw_lo[:, 3, :]))
                ins.then_inc(wo_mm, 1)

            def shifted_scores(b, previous=True):
                pe.wait_ge(diag_done, b * JT + JT)
                pe.wait_ge(qk_lo, b * 4 + 4)
                for u in range(2 * JT):
                    qh, kt = u // JT, u % JT
                    if u >= 4:
                        pe.wait_ge(p_exp, b * 2 * JT + u - 3)
                    o = ps[:, u % 4, :]
                    kk, qq = slice(kt * P, (kt + 1) * P), slice(qh * N, (qh + 1) * N)
                    product(o, (k_hi[:, kk], k_lo[:, kk]), (q_hi[:, qq], q_lo[:, qq]), last=False)
                    mm(o, ones_bf[:], dg[:, qh * TB:(qh + 1) * TB, :].rearrange("p t q -> p (t q)"), start=False,
                       stop=True).then_inc(st_mm, 1)
                    if u == 1 and previous:
                        projected(b - 1)
                    if u in (3, 5):
                        hc = (u - 3) // 2
                        if not previous:
                            pe.wait_ge(lo_made, NB)
                        for t in range(TB):
                            cols = ds(b * S + (hc * TB + t) * P, P)
                            ins = product(ps[:, 4 + hc, t * P:(t + 1) * P], (xT_hi[:, cols], xT_lo[:, cols]),
                                          (pw_hi[:, 2, :], pw_lo[:, 2, :]))
                        ins.then_inc(vp_mm, 1)

            queries_keys(0)
            scores_and_values(0, values=False, turned={1: 4, 3: 5, 5: 6, 7: 7})
            shifted_scores(0, previous=False)
            pe.wait_ge(lo_made, NB)

            def batch(b):
                queries_keys(b)
                scores_and_values(b)
                shifted_scores(b)
            batch(1)
            with pe.Fori(2, B) as b:
                batch(b)
            scores_and_values(B, scores=False, turned={5: 0, 7: 1}, k=1)
            projected(B - 1)

            for i in range(NB):
                if 2 <= i + 1 < NB:
                    turned_block(i + 1, 1)
                pe.wait_ge(t32_made, i + 1)
                for t in range(TB):
                    k = (i % GB) * TB + t
                    ins = mm(ps[:, 4 + i // GB, k * E1:(k + 1) * E1], xT32[:, i % 2, t * P:(t + 1) * P], Wr[1][:],
                             start=True, stop=True)
                ins.then_inc(routed_mm, 1)
            pe.wait_ge(x3_done, B)
            for i in range(NB + 1):
                if i < NB:
                    g = i // GB
                    pe.wait_ge(c_ready, g + 1)
                    after(pe, cT_cp, i - 1)
                    for t in range(TB):
                        for part in range(2):
                            ins = mm(ps[0:E1, 6 + i % 2, t * P:(t + 1) * P], cw_parts[:, g, part, (i % GB) * TB + t, :],
                                     ident16[:], start=part == 0, stop=part == 1)
                    ins.then_inc(cT_mm, 1)
                j = i - 1
                if j >= 0:
                    if j == 0:
                        pe.wait_ge(lo_made, 2 * NB)
                    pe.wait_ge(cT_cp, j + 1)
                    if j >= GB + 2:
                        pe.wait_ge(b2_added, j - 1)
                    for t in range(TB):
                        ins = mm(ps[:, b2_bank(j), t * P:(t + 1) * P], cT[0:E1, j % 2, t * P:(t + 1) * P], b2[:], start=True, stop=True)
                    ins.then_inc(b2_mm, 1)
            pe.wait_ge(ew_lo, E0 + 3)
            experts()


_INS = ["L0_attn_x", "L0_attn_W", "L0_ffn_Wr", "L0_ffn_br", "L0_ffn_ln_g", "L0_ffn_ln_b", "L0_ffn_W1", "L0_ffn_b1",
        "L0_ffn_W2", "L0_ffn_b2", "L1_attn_wq", "L1_attn_wk", "L1_attn_wv", "L1_attn_wo", "L1_ffn_router_w",
        "L1_ffn_router_b", "L1_ffn_w1", "L1_ffn_b1", "L1_ffn_w2", "L1_ffn_b2"]
_OUTS = [((4, 1024, 128), "float32")]


def kernel(**inputs):
    import numpy as _np
    import concourse.bacc as _bacc
    from concourse import mybir as _mybir
    from concourse.bass_utils import run_bass_kernel_spmd as _run

    nc = _bacc.Bacc("TRN2", target_bir_lowering=False, num_devices=1)
    arrays, args = {}, []
    for name in _INS:
        a = _np.ascontiguousarray(inputs[name])
        arrays[f"in_{name}_dram"] = a
        args.append(nc.dram_tensor(f"in_{name}_dram", a.shape, _mybir.dt.from_np(a.dtype), kind="ExternalInput").ap())
    for i, (shape, dtype) in enumerate(_OUTS):
        dt = _mybir.dt.from_np(_np.dtype(dtype))
        args.append(nc.dram_tensor(f"out_{i}_dram", shape, dt, kind="ExternalOutput").ap())
    build(nc, *args)
    r = _run(nc, [arrays], core_ids=[0])
    return r.results[0]["out_0_dram"]
```
